# Optimizing a Trainium2 kernel written in Bass

```python
import numpy as np
import jax
import jax.numpy as jnp

def _softmax(x, axis=-1):
    return jax.nn.softmax(x, axis=axis)

def _gelu(x):
    return jax.nn.gelu(x, approximate=True)

def _silu(x):
    return jax.nn.silu(x)

def _sigmoid(x):
    return jax.nn.sigmoid(x)

def _layernorm(x, axis=-1, eps=1e-05):
    m = jnp.mean(x, axis=axis, keepdims=True)
    v = jnp.var(x, axis=axis, keepdims=True)
    return (x - m) / jnp.sqrt(v + eps)

def _scatter_add(tgt, idx, src, axis=0):
    return tgt.at[idx].add(src)

def _segment_sum(src, seg, n):
    return jax.ops.segment_sum(src, seg, n)
kernel_name = 'mk_gnn_ffn_d2_gnn_r64_b6c7a0'

def setup_inputs(seed: int=0):
    np.random.seed(seed)
    _w = jnp.asarray

    def _rec_inputs():
        import jax
        import jax.numpy as jnp
        _gk = jax.random.key(seed)
        x = -8.776e-05 + 1 * jax.random.normal(jax.random.fold_in(_gk, 1), (20000, 256), jnp.float32)
        src = jax.random.randint(jax.random.fold_in(_gk, 2), (10000,), 0, 20000, jnp.int32)
        dst = jnp.minimum((20000 * jax.random.uniform(jax.random.fold_in(_gk, 3), (10000,)) ** 2.0).astype(jnp.int32), 19999)
        _o = jnp.argsort(dst, stable=True)
        src = src[_o]
        dst = dst[_o]
        edge_attr_16 = -0.000153872 + 1.00011 * jax.random.normal(jax.random.fold_in(_gk, 12), (10000, 16), jnp.float32)
        edge_attr_4 = 0.0007022 + 0.999661 * jax.random.normal(jax.random.fold_in(_gk, 13), (10000, 4), jnp.float32)
        return (x, src, dst, edge_attr_16, edge_attr_4)
    x, src, dst, edge_attr_16, edge_attr_4 = _rec_inputs()

    def _L0_gnn_setup():
        import jax, jax.numpy as jnp
        import numpy as np
        N = 20000
        E = 10000
        F_IN = 256
        H = 4
        F_OUT = 64
        NEG_SLOPE = 0.2
        key = jax.random.key(seed)
        k = jax.random.split(key, 6)
        x = jax.random.normal(k[0], (N, F_IN), jnp.float32)
        edge_src = jax.random.randint(k[1], (E,), 0, N, jnp.int32)
        edge_dst = jax.random.randint(k[2], (E,), 0, N, jnp.int32)
        W = jax.random.normal(k[3], (H, F_IN, F_OUT), jnp.float32) * (1.0 / np.sqrt(F_IN))
        a_src = jax.random.normal(k[4], (H, F_OUT), jnp.float32) * 0.1
        a_dst = jax.random.normal(k[5], (H, F_OUT), jnp.float32) * 0.1
        return {'x': x, 'edge_src': edge_src, 'edge_dst': edge_dst, 'W': W, 'a_src': a_src, 'a_dst': a_dst}
    _L0_gnn_all = _L0_gnn_setup()
    _L0_gnn_in = {k: v for k, v in _L0_gnn_all.items() if k in ('W', 'a_src', 'a_dst')}
    del _L0_gnn_all

    def _L0_ffn_setup():
        import math
        import jax, jax.numpy as jnp
        import numpy as np
        CAPACITY_FACTOR = 1.25
        key = jax.random.key(seed)
        ks = jax.random.split(key, 5)
        B, L, D, F, E = (8, 128, 256, 1024, 8)
        h = jax.random.normal(ks[0], (B, L, D), dtype=jnp.float32)
        gate_w = jax.random.normal(ks[1], (D, E), dtype=jnp.float32) * 0.02
        gate_b = jnp.zeros((E,), dtype=jnp.float32)
        w1 = jax.random.normal(ks[2], (E, D, F), dtype=jnp.float32) * (1.0 / math.sqrt(D))
        b1 = jnp.zeros((E, F), dtype=jnp.float32)
        w2 = jax.random.normal(ks[3], (E, F, D), dtype=jnp.float32) * (1.0 / math.sqrt(F))
        b2 = jnp.zeros((E, D), dtype=jnp.float32)
        return {'h': h, 'gate_w': gate_w, 'gate_b': gate_b, 'w1': w1, 'b1': b1, 'w2': w2, 'b2': b2}
    _L0_ffn_all = _L0_ffn_setup()
    _L0_ffn_in = {k: v for k, v in _L0_ffn_all.items() if k in ('gate_w', 'gate_b', 'w1', 'b1', 'w2', 'b2')}
    del _L0_ffn_all

    def _L1_gnn_setup():
        import jax, jax.numpy as jnp
        import numpy as np
        N, E, C, R, HID = (50000, 500000, 64, 16, 64)
        key = jax.random.key(seed)
        ks = jax.random.split(key, 24)
        g = lambda k, shape, s=1.0: jax.random.normal(k, shape, dtype=jnp.float32) * s
        cs = C ** (-0.5)
        inp = {'h': g(ks[0], (N, 4 * C)), 'edge_index': jax.random.randint(ks[1], (2, E), 0, N), 'edge_sh': g(ks[2], (E, 4)), 'edge_rbf': g(ks[3], (E, R)), 'W_up0': g(ks[4], (C, C), cs), 'W_up1': g(ks[5], (C, C), cs), 'M1': g(ks[6], (R, HID), R ** (-0.5)), 'M2': g(ks[7], (HID, HID), HID ** (-0.5)), 'M3': g(ks[8], (HID, HID), HID ** (-0.5)), 'M4': g(ks[9], (HID, 4 * C), HID ** (-0.5)), 'W_lin0': g(ks[10], (C, C), cs), 'W_lin1': g(ks[11], (C, C), cs), 'Wsc0': g(ks[12], (C, C), cs), 'Wsc1': g(ks[13], (C, C), cs), 'Wc0': g(ks[14], (C, 5)), 'Wc1': g(ks[15], (C, 4)), 'WB0': g(ks[16], (C, C), cs), 'WB1': g(ks[17], (C, C), cs), 'gamma0': jnp.ones((C,), jnp.float32), 'beta0': jnp.zeros((C,), jnp.float32), 'gamma1': jnp.ones((C,), jnp.float32)}
        return inp
    _L1_gnn_all = _L1_gnn_setup()
    _L1_gnn_in = {k: v for k, v in _L1_gnn_all.items() if k in ('W_up0', 'W_up1', 'M1', 'M2', 'M3', 'M4', 'W_lin0', 'W_lin1', 'Wsc0', 'Wsc1', 'Wc0', 'Wc1', 'WB0', 'WB1', 'gamma0', 'beta0', 'gamma1')}
    del _L1_gnn_all

    def _L1_ffn_setup():
        import jax, jax.numpy as jnp
        import numpy as np
        B, S, D = (8, 64, 256)
        H = 4 * D
        CAPACITY = 0.5
        key = jax.random.key(seed)
        ks = jax.random.split(key, 6)
        x = jax.random.normal(ks[0], (B, S, D), dtype=jnp.float32)
        attention_mask = jnp.zeros((B, 1, 1, S), dtype=jnp.float32)
        wr = jax.random.normal(ks[1], (D, 1), dtype=jnp.float32) * 0.02
        br = jnp.zeros((1,), dtype=jnp.float32)
        w1 = jax.random.normal(ks[2], (D, H), dtype=jnp.float32) * 0.02
        b1 = jnp.zeros((H,), dtype=jnp.float32)
        w2 = jax.random.normal(ks[3], (H, D), dtype=jnp.float32) * 0.02
        b2 = jnp.zeros((D,), dtype=jnp.float32)
        return {'x': x, 'attention_mask': attention_mask, 'wr': wr, 'br': br, 'w1': w1, 'b1': b1, 'w2': w2, 'b2': b2}
    _L1_ffn_all = _L1_ffn_setup()
    _L1_ffn_in = {k: v for k, v in _L1_ffn_all.items() if k in ('attention_mask', 'wr', 'br', 'w1', 'b1', 'w2', 'b2')}
    del _L1_ffn_all
    return {'x': x, 'src': src, 'dst': dst, 'edge_attr_16': edge_attr_16, 'edge_attr_4': edge_attr_4, 'L0_gnn_W': _L0_gnn_in['W'], 'L0_gnn_a_src': _L0_gnn_in['a_src'], 'L0_gnn_a_dst': _L0_gnn_in['a_dst'], 'L0_ffn_gate_w': _L0_ffn_in['gate_w'], 'L0_ffn_gate_b': _L0_ffn_in['gate_b'], 'L0_ffn_w1': _L0_ffn_in['w1'], 'L0_ffn_b1': _L0_ffn_in['b1'], 'L0_ffn_w2': _L0_ffn_in['w2'], 'L0_ffn_b2': _L0_ffn_in['b2'], 'L1_gnn_W_up0': _L1_gnn_in['W_up0'], 'L1_gnn_W_up1': _L1_gnn_in['W_up1'], 'L1_gnn_M1': _L1_gnn_in['M1'], 'L1_gnn_M2': _L1_gnn_in['M2'], 'L1_gnn_M3': _L1_gnn_in['M3'], 'L1_gnn_M4': _L1_gnn_in['M4'], 'L1_gnn_W_lin0': _L1_gnn_in['W_lin0'], 'L1_gnn_W_lin1': _L1_gnn_in['W_lin1'], 'L1_gnn_Wsc0': _L1_gnn_in['Wsc0'], 'L1_gnn_Wsc1': _L1_gnn_in['Wsc1'], 'L1_gnn_Wc0': _L1_gnn_in['Wc0'], 'L1_gnn_Wc1': _L1_gnn_in['Wc1'], 'L1_gnn_WB0': _L1_gnn_in['WB0'], 'L1_gnn_WB1': _L1_gnn_in['WB1'], 'L1_gnn_gamma0': _L1_gnn_in['gamma0'], 'L1_gnn_beta0': _L1_gnn_in['beta0'], 'L1_gnn_gamma1': _L1_gnn_in['gamma1'], 'L1_ffn_attention_mask': _L1_ffn_in['attention_mask'], 'L1_ffn_wr': _L1_ffn_in['wr'], 'L1_ffn_br': _L1_ffn_in['br'], 'L1_ffn_w1': _L1_ffn_in['w1'], 'L1_ffn_b1': _L1_ffn_in['b1'], 'L1_ffn_w2': _L1_ffn_in['w2'], 'L1_ffn_b2': _L1_ffn_in['b2']}

def reference(x, src, dst, edge_attr_16, edge_attr_4, L0_gnn_W, L0_gnn_a_src, L0_gnn_a_dst, L0_ffn_gate_w, L0_ffn_gate_b, L0_ffn_w1, L0_ffn_b1, L0_ffn_w2, L0_ffn_b2, L1_gnn_W_up0, L1_gnn_W_up1, L1_gnn_M1, L1_gnn_M2, L1_gnn_M3, L1_gnn_M4, L1_gnn_W_lin0, L1_gnn_W_lin1, L1_gnn_Wsc0, L1_gnn_Wsc1, L1_gnn_Wc0, L1_gnn_Wc1, L1_gnn_WB0, L1_gnn_WB1, L1_gnn_gamma0, L1_gnn_beta0, L1_gnn_gamma1, L1_ffn_attention_mask, L1_ffn_wr, L1_ffn_br, L1_ffn_w1, L1_ffn_b1, L1_ffn_w2, L1_ffn_b2):
    import jax
    import jax.numpy as jnp

    def _L0_gnn_ref(x, edge_src, edge_dst, W, a_src, a_dst):
        import jax, jax.numpy as jnp
        import numpy as np
        N = 20000
        E = 10000
        F_IN = 256
        H = 4
        F_OUT = 64
        NEG_SLOPE = 0.2
        h = jnp.einsum('nf,hfo->nho', x, W)
        e_s = jnp.einsum('nho,ho->nh', h, a_src)
        e_d = jnp.einsum('nho,ho->nh', h, a_dst)
        scores = jax.nn.leaky_relu(e_s[edge_src] + e_d[edge_dst], NEG_SLOPE)
        m = jax.ops.segment_max(scores, edge_dst, num_segments=N)
        m = jnp.where(jnp.isfinite(m), m, 0.0)
        ex = jnp.exp(scores - m[edge_dst])
        denom = jax.ops.segment_sum(ex, edge_dst, num_segments=N)
        alpha = ex / jnp.maximum(denom[edge_dst], 1e-09)
        msg = alpha[:, :, None] * h[edge_src]
        agg = jax.ops.segment_sum(msg, edge_dst, num_segments=N)
        return jax.nn.relu(agg).reshape(N, H * F_OUT)

    def _L0_ffn_ref(h, gate_w, gate_b, w1, b1, w2, b2):
        import math
        import jax, jax.numpy as jnp
        import numpy as np
        CAPACITY_FACTOR = 1.25
        B, L, D = h.shape
        E = gate_w.shape[1]
        T = B * L
        C = max(1, math.ceil(CAPACITY_FACTOR * T / E))
        x = h.reshape(T, D)
        logits = x @ gate_w + gate_b
        probs = jax.nn.softmax(logits, axis=-1)
        idx = jnp.argmax(probs, axis=-1)
        prb = jnp.take_along_axis(probs, idx[:, None], axis=1)[:, 0]
        one_hot = jax.nn.one_hot(idx, E, dtype=jnp.float32)
        pos = (jnp.cumsum(one_hot, axis=0) * one_hot).sum(-1).astype(jnp.int32) - 1
        kept = pos < C
        pos_safe = jnp.where(kept, pos, C)
        buf = jnp.zeros((E, C, D), dtype=h.dtype).at[idx, pos_safe].set(x, mode='drop')
        hmid = jax.nn.relu(jnp.einsum('ecd,edf->ecf', buf, w1) + b1[:, None, :])
        ybuf = jnp.einsum('ecf,efd->ecd', hmid, w2) + b2[:, None, :]
        pos_g = jnp.minimum(pos, C - 1)
        y_tok = ybuf[idx, pos_g] * (prb * kept)[:, None]
        y = y_tok.reshape(B, L, D)
        y = jnp.nan_to_num(y, nan=0.0, posinf=10000.0, neginf=-10000.0)
        return y

    def _L1_gnn_ref(h, edge_index, edge_sh, edge_rbf, W_up0, W_up1, M1, M2, M3, M4, W_lin0, W_lin1, Wsc0, Wsc1, Wc0, Wc1, WB0, WB1, gamma0, beta0, gamma1):
        import jax, jax.numpy as jnp
        import numpy as np
        N, E, C, R, HID = (50000, 500000, 64, 16, 64)
        n = h.shape[0]
        h0 = h[:, :C]
        h1 = h[:, C:].reshape(n, C, 3)
        up0 = h0 @ W_up0
        up1 = jnp.einsum('ncx,cd->ndx', h1, W_up1)
        r = jax.nn.silu(edge_rbf @ M1)
        r = jax.nn.silu(r @ M2)
        r = jax.nn.silu(r @ M3)
        tpw = (r @ M4).reshape(-1, 4, C)
        snd, rcv = (edge_index[0], edge_index[1])
        x0 = up0[snd]
        x1 = up1[snd]
        sh0 = edge_sh[:, 0]
        sh1 = edge_sh[:, 1:]
        inv3 = 1.0 / jnp.sqrt(jnp.float32(3.0))
        m0e = tpw[:, 0] * x0 * sh0[:, None] + tpw[:, 3] * jnp.einsum('ecx,ex->ec', x1, sh1) * inv3
        m1e = tpw[:, 1][:, :, None] * x0[:, :, None] * sh1[:, None, :] + tpw[:, 2][:, :, None] * x1 * sh0[:, None, None]
        msg0 = jax.ops.segment_sum(m0e, rcv, num_segments=n)
        msg1 = jax.ops.segment_sum(m1e, rcv, num_segments=n)
        A0 = msg0 @ W_lin0
        A1 = jnp.einsum('ncx,cd->ndx', msg1, W_lin1)
        sc0 = h0 @ Wsc0
        sc1 = jnp.einsum('ncx,cd->ndx', h1, Wsc1)
        vv = jnp.sum(A1 * A1, -1)
        B0 = Wc0[:, 0] * A0 + Wc0[:, 1] * A0 * A0 + Wc0[:, 2] * vv + Wc0[:, 3] * A0 ** 3 + Wc0[:, 4] * A0 * vv
        B1 = (Wc1[:, 0] + Wc1[:, 1] * A0 + Wc1[:, 2] * A0 * A0 + Wc1[:, 3] * vv)[..., None] * A1
        o0 = B0 @ WB0 + sc0
        o1 = jnp.einsum('ncx,cd->ndx', B1, WB1) + sc1
        eps = jnp.float32(1e-05)
        mu = jnp.mean(o0, 0)
        xc = o0 - mu
        var = jnp.mean(xc * xc, 0)
        n0 = xc * jax.lax.rsqrt(var + eps) * gamma0 + beta0
        nrm1 = jnp.mean(jnp.sum(o1 * o1, -1) / 3.0, 0)
        n1 = o1 * (jax.lax.rsqrt(nrm1 + eps) * gamma1)[None, :, None]
        return jnp.concatenate([n0, n1.reshape(n, 3 * C)], -1)

    def _L1_ffn_ref(x, attention_mask, wr, br, w1, b1, w2, b2):
        import jax, jax.numpy as jnp
        import numpy as np
        B, S, D = (8, 64, 256)
        H = 4 * D
        CAPACITY = 0.5
        b, s, d = x.shape
        weights = (jnp.einsum('bsd,do->bso', x, wr) + br)[..., 0]
        k = max(1, int(CAPACITY * s))
        kk = k - 1 if k > 1 else 1
        _, idx = jax.lax.top_k(weights, k)
        sel_idx = idx[:, :kk]
        sel = jnp.take_along_axis(x, sel_idx[:, :, None], axis=1)
        h = jax.nn.gelu(jnp.einsum('bkd,dh->bkh', sel, w1) + b1)
        y = jnp.einsum('bkh,hd->bkd', h, w2) + b2
        w_sel = jnp.take_along_axis(weights, sel_idx, axis=1)
        y = y * w_sel[..., None]
        batch_idx = jnp.arange(b)[:, None]
        processed = jnp.zeros_like(x).at[batch_idx, sel_idx].set(y)
        return processed + x
    edge_index = jnp.stack([src, dst])
    x = x + _L0_gnn_ref(_layernorm(x, axis=-1), src, dst, L0_gnn_W, L0_gnn_a_src, L0_gnn_a_dst)
    x = x + _L0_ffn_ref(_layernorm(x, axis=-1)[None], L0_ffn_gate_w, L0_ffn_gate_b, L0_ffn_w1, L0_ffn_b1, L0_ffn_w2, L0_ffn_b2)[0]
    x = x + _L1_gnn_ref(_layernorm(x, axis=-1), edge_index, edge_attr_4, edge_attr_16, L1_gnn_W_up0, L1_gnn_W_up1, L1_gnn_M1, L1_gnn_M2, L1_gnn_M3, L1_gnn_M4, L1_gnn_W_lin0, L1_gnn_W_lin1, L1_gnn_Wsc0, L1_gnn_Wsc1, L1_gnn_Wc0, L1_gnn_Wc1, L1_gnn_WB0, L1_gnn_WB1, L1_gnn_gamma0, L1_gnn_beta0, L1_gnn_gamma1)
    x = x + _L1_ffn_ref(_layernorm(x, axis=-1)[None], L1_ffn_attention_mask, L1_ffn_wr, L1_ffn_br, L1_ffn_w1, L1_ffn_b1, L1_ffn_w2, L1_ffn_b2)[0]
    return x

_drawn_inputs = setup_inputs


def setup_inputs(seed=0):
    import zlib

    import numpy as np

    out = dict(_drawn_inputs(seed))
    spreads = {'L0_ffn_gate_b': (0.0, 0.1),
     'L0_ffn_b1': (0.0, 0.621),
     'L0_ffn_b2': (0.0, 0.438),
     'L1_gnn_gamma0': (1.0, 0.2),
     'L1_gnn_beta0': (0.0, 0.1),
     'L1_gnn_gamma1': (1.0, 0.2),
     'L1_ffn_b1': (0.0, 0.8),
     'L1_ffn_b2': (0.0, 0.787)}
    factors = {'L0_gnn_a_dst': 3.163, 'L1_ffn_wr': 4.558, 'L1_ffn_w1': 5.452, 'L1_ffn_w2': 5.063}
    for name, (base, spread) in spreads.items():
        noise = np.random.default_rng([zlib.crc32(name.encode()), seed]).standard_normal(out[name].shape)
        drawn = base * np.exp(spread * noise) if base else spread * noise
        out[name] = jnp.asarray(drawn.astype(out[name].dtype))
    for name, factor in factors.items():
        out[name] = (out[name] * factor).astype(out[name].dtype)
    return out
```

```python
from contextlib import ExitStack

import concourse.bass as bass
from concourse import mybir

F32 = mybir.dt.float32
BF16 = mybir.dt.bfloat16
I32 = mybir.dt.int32
U32 = mybir.dt.uint32
ALU = mybir.AluOpType
ACT = mybir.ActivationFunctionType
AX = mybir.AxisListType

P = 128
N = 20000
C = 256
E = 10000
EPS = 1e-5
G = 4
NG = 40
NT = NG * G
NP = NT * P
EG = 20
ET = EG * G
EP = ET * P
GR = G * P
HEADS = 4
EXPERTS = 8
HID = 1024
CAP = 3125
FT = 5
FB = FT * P
XB = 5
SLOTS = XB * FB
KEEP = 9999
SB = 16
SKIP = 1 << 20
FAR = 3.0e38
FMAX = 3.4028234663852886e38
GAT_IN = HEADS + C


class Tally:

    def __init__(self, sem, step=1):
        self.sem, self.step = sem, step
        self.base, self.i, self.per, self.n = 0, 0, 0, 0

    def add(self, k=1):
        self.n += k * self.step
        return self

    def skip(self, k=1):
        self.n += k * self.step
        self.base -= k * self.step

    def now(self, less=0):
        v = self.n + self.base - less * self.step
        return v if isinstance(self.i, int) else self.i * self.per + v


def wait(eng, tally, less=0):
    v = tally.now(less)
    if not isinstance(v, int) or v > 0:
        eng.wait_ge(tally.sem, v)


def rounds(eng, n, body, *tallies):
    for t in tallies:
        t.base, t.n = t.base + t.n, 0
    body(0)
    for t in tallies:
        t.per, t.n = t.n, 0
    with eng.Fori(1, n) as i:
        for t in tallies:
            t.i = i
        body(i)
        for t in tallies:
            assert t.n == t.per, (t.n, t.per)
    for t in tallies:
        t.base, t.i, t.per, t.n = t.base + n * t.per, 0, 0, 0


class Banks:

    def __init__(self, banks, full, empty):
        self.banks, self.full, self.empty = banks, full, empty

    def writer(self):
        return Tally(self.full)

    def reader(self):
        return Tally(self.full)

    def take(self, pe, t, all_empty=False):
        k = len(self.banks)
        v = t.now() - k + 1
        if not all_empty and (not isinstance(v, int) or v > 0):
            pe.wait_ge(self.empty, v)
        return self.banks[t.n // t.step % k]

    def filled(self, ins, t):
        ins.then_inc(self.full, 1)
        t.add()

    def get(self, eng, t):
        bank = self.banks[t.n // t.step % len(self.banks)]
        t.add()
        eng.wait_ge(self.full, t.now())
        return bank


class Stage:

    def __init__(self, nc, tag):
        self.nc, self.tag, self.ctx, self.used = nc, tag, ExitStack(), []

    def __enter__(self):
        self.ctx.__enter__()
        return self

    def __exit__(self, *e):
        if e[0] is None:
            self.nc.clear_and_free_semaphores(self.used)
            self.nc.all_engine_barrier()
        return self.ctx.__exit__(*e)

    def sb(self, name, shape, dt=F32):
        return self.ctx.enter_context(self.nc.sbuf_tensor(f"{self.tag}_{name}", shape, dt))

    def sem(self, name):
        self.used.append(self.nc.alloc_semaphore(name=f"{self.tag}_{name}"))
        return self.used[-1]

    def sems(self, name, n=2):
        return [self.sem(f"{name}{k}") for k in range(n)]

    def banks(self, name, first, n, psum):
        return Banks([psum[k] for k in range(first, first + n)], self.sem(f"{name}_full"), self.sem(f"{name}_empty"))


def hold(eng, passed):
    eng.sem_inc(passed, 1)


def ln_stats(dve, own, passed, rows, st, mv, tiles, ready):
    for j in range(tiles):
        last = dve.bn_stats(st[:, j, :], rows[:, j, :])
    last.then_inc(own.sem, 1)
    wait(dve, own.add())
    hold(dve, passed)
    for j in range(tiles):
        last = dve.bn_aggr(mv[:, j, :], st[:, j, :])
    last.then_inc(ready, 1)


def ln_deviation(act, stats, mv, sd, eps, done):
    wait(act, stats.add())
    act.activation(sd[:, :], mv[:, :, 1], ACT.Sqrt, bias=eps[:, 0:1]).then_inc(done, 1)


def ln_apply(dve, own, deviation, rows, mv, sd, out, tiles, ready):
    wait(dve, deviation.add())
    dve.reciprocal(sd[:, :], sd[:, :]).then_inc(own.sem, 1)
    wait(dve, own.add())
    for j in range(tiles):
        last = dve.tensor_scalar(out[:, j, :], rows[:, j, :], mv[:, j, 0:1], sd[:, j:j + 1],
                                 ALU.subtract, ALU.mult)
    last.then_inc(ready, 1)


def rows_of(dram, start, tiles):
    return dram[bass.ds(start, tiles * P), :].rearrange("(j p) c -> p j c", p=P)


def stage_edge_scores(nc, d, s, psum):
    with Stage(nc, "es") as m:
        idx = m.sb("idx", [P, EG, 2 * G], I32)
        cur = m.sb("cur", [P, 2, 2 * G], I32)
        rows = [m.sb(f"rows{b}", [P, 2 * G, C]) for b in range(2)]
        xn = [m.sb(f"xn{b}", [P, 2 * G, C]) for b in range(2)]
        xt = [m.sb(f"xt{b}", [P, 2, 2, GR]) for b in range(2)]
        h = [m.sb(f"h{b}", [P, G, GAT_IN]) for b in range(2)]
        w = m.sb("w", [P, 2, GAT_IN])
        wd = m.sb("wd", [P, 2, HEADS])
        av = m.sb("av", [P, 2, C])
        prod = m.sb("prod", [P, 2, C])
        st = m.sb("st", [P, 2, 2 * G, 6])
        mv = m.sb("mv", [P, 2, 2 * G, 2])
        sd = m.sb("sd", [P, 2, 2 * G])
        zeros = m.sb("zeros", [P, 2048])
        table = m.sb("table", [P, EXPERTS * SLOTS // P, 2], I32)
        idx_in, w_in, filled, zeroed = m.sem("idx_in"), m.sem("w_in"), m.sem("filled"), m.sem("zeroed")
        cur_ready, gathered, xn_ready = m.sem("cur_ready"), m.sems("gathered"), m.sem("xn_ready")
        stats_ready, sd_ready, own = m.sem("stats_ready"), m.sem("sd_ready"), m.sem("own")
        w_ready = m.sem("w_ready")
        h_stored, passed = m.sems("h_stored"), m.sems("passed", 2)
        on_act = m.banks("on_act", 0, 4, psum)
        on_dve = m.banks("on_dve", 4, 3, psum)
        with nc.Block() as block:
            @block.sync
            def _(sp):
                sp.dma_start(idx[:, :, :], d["edge_idx"]).then_inc(idx_in, 16)
                sp.dma_start(w[:, :, 0:C], d["gat_w"]).then_inc(w_in, 16)
                sp.dma_start(av[:, :, :], d["gat_a"]).then_inc(w_in, 16)
                sp.dma_start(s.ident[:, :], d["ident"]).then_inc(w_in, 16)
                for k in range(4):
                    r = NP // 4
                    sp.dma_start(d["X"][k * r:(k + 1) * r, :].rearrange("(p t) c -> p (t c)", p=P),
                                 d["x"][k * r:(k + 1) * r, :].rearrange("(p t) c -> p (t c)", p=P)).then_inc(filled, 16)
                sp.wait_ge(zeroed, 3)
                for k in range(20):
                    r = NP // 20
                    sp.dma_start(d["D"][k * r:(k + 1) * r, :].rearrange("(p t) c -> p (t c)", p=P),
                                 zeros[:, :]).then_inc(filled, 16)
                sp.dma_start(d["moe_table"].rearrange("(p t) w -> p t w", p=P), table[:, :, :]).then_inc(filled, 16)
                sp.dma_start(d["mod_table"].rearrange("(p t) w -> p t w", p=P),
                             table[:, 0:SB * FB // P, :]).then_inc(filled, 16)
                ready = Tally(on_act.empty, 2 + G)

                def body(i):
                    for b in range(2):
                        wait(sp, ready.add())
                        sp.dma_start(rows_of(d["H"], (i * 2 + b) * GR, G), h[b][:, :, 0:C]).then_inc(h_stored[b], 16)

                rounds(sp, EG // 2, body, ready)
                sp.wait_ge(filled, 16 * 26)
                for b in range(2):
                    sp.wait_ge(h_stored[b], 16 * EG // 2)

            @block.gpsimd
            def _(pool):
                pool.memset(zeros[:, :], 0.0).then_inc(zeroed, 1)
                pool.memset(table[:, :, 0:1], SKIP).then_inc(zeroed, 1)
                pool.memset(table[:, :, 1:2], 0).then_inc(zeroed, 1)
                pool.wait_ge(idx_in, 16)
                loaded = [Tally(gathered[b], 16) for b in range(2)]
                taken, used = Tally(cur_ready), Tally(xn_ready)

                def body(i):
                    for b in range(2):
                        wait(pool, loaded[b])
                        hold(pool, passed[0])
                        pool.tensor_copy(cur[:, b, :], idx[:, bass.ds(i * 2 + b, 1), :].rearrange("p a j -> p (a j)")).then_inc(cur_ready, 1)
                        wait(pool, taken.add())
                        wait(pool, used, 1)
                        used.add()
                        hold(pool, passed[0])
                        for j in range(2 * G):
                            pool.indirect_dma_start(
                                out=rows[b][:, j, :], out_offset=None, in_=d["x"],
                                in_offset=bass.IndirectOffsetOnAxis(ap=cur[:, b, j:j + 1], axis=0),
                                bounds_check=NP - 1, oob_is_err=False).then_inc(gathered[b], 16)
                            loaded[b].add()

                rounds(pool, EG // 2, body, *loaded, taken, used)

            @block.vector
            def _(dve):
                chain = Tally(own)
                dve.wait_ge(w_in, 48)
                for k in range(2):
                    for end, out in ((0, w[:, k, C:GAT_IN]), (1, wd[:, k, :])):
                        dve.tensor_tensor(prod[:, end, :], w[:, k, 0:C], av[:, end, :], ALU.mult).then_inc(own, 1)
                        wait(dve, chain.add())
                        dve.tensor_reduce(out, prod[:, end, :].rearrange("p (h o) -> p h o", h=HEADS), AX.X, ALU.add).then_inc(w_ready, 1)
                loaded = [Tally(gathered[b], 16) for b in range(2)]
                deviation, read = Tally(sd_ready), on_dve.reader()

                def body(i):
                    for b in range(2):
                        wait(dve, loaded[b].add(2 * G))
                        ln_stats(dve, chain, passed[1], rows[b], st[:, b], mv[:, b], 2 * G, stats_ready)
                    for b in range(2):
                        ln_apply(dve, chain, deviation, rows[b], mv[:, b], sd[:, b], xn[b], 2 * G, xn_ready)
                    for b in range(2):
                        for k in range(2):
                            bank = on_dve.get(dve, read)
                            dve.tensor_copy(xt[b][:, 1, k, :], bank[:, :]).then_inc(on_dve.empty, 1)
                        bank = on_dve.get(dve, read)
                        hold(dve, passed[1])
                        dve.tensor_copy(s.scores[:, bass.ds((i * 2 + b) * GR, GR)], bank[0:HEADS, :]).then_inc(on_dve.empty, 1)

                rounds(dve, EG // 2, body, *loaded, chain, deviation, read)

            @block.scalar
            def _(act):
                stats, read, stored = Tally(stats_ready), on_act.reader(), [Tally(h_stored[b], 16) for b in range(2)]

                def body(i):
                    for b in range(2):
                        ln_deviation(act, stats, mv[:, b], sd[:, b], s.eps, sd_ready)
                    for b in range(2):
                        for k in range(2):
                            bank = on_act.get(act, read)
                            act.activation(xt[b][:, 0, k, :], bank[:, :], ACT.Copy).then_inc(on_act.empty, 1)
                        wait(act, stored[b])
                        stored[b].add()
                        for j in range(G):
                            bank = on_act.get(act, read)
                            act.activation(h[b][:, j, :], bank[:, 0:GAT_IN], ACT.Copy).then_inc(on_act.empty, 1)

                rounds(act, EG // 2, body, stats, read, *stored)

            @block.tensor
            def _(pe):
                pe.wait_ge(w_in, 48)
                pe.wait_ge(w_ready, 4)
                xn_in, ta, td = Tally(xn_ready), on_act.writer(), on_dve.writer()

                def transposes(b):
                    wait(pe, xn_in.add())
                    for end, ring, t in ((0, on_act, ta), (1, on_dve, td)):
                        for k in range(2):
                            bank = ring.take(pe, t)
                            for j in range(G):
                                last = pe.transpose(bank[:, j * P:(j + 1) * P], xn[b][:, end * G + j, k * P:(k + 1) * P], s.ident[:, :])
                            ring.filled(last, t)
                    pe.wait_ge(on_act.empty, ta.now())
                    pe.wait_ge(on_dve.empty, td.now())

                def products(b):
                    for j in range(G):
                        e = slice(j * P, (j + 1) * P)
                        bank = on_act.take(pe, ta, True)
                        pe.matmul(bank[:, 0:GAT_IN], xt[b][:, 0, 0, e], w[:, 0, :], start=True, stop=False)
                        pe.matmul(bank[:, 0:GAT_IN], xt[b][:, 0, 1, e], w[:, 1, :], start=False, stop=False)
                        pe.matmul(bank[:, C:GAT_IN], xt[b][:, 1, 0, e], wd[:, 0, :], start=False, stop=False)
                        last = pe.matmul(bank[:, C:GAT_IN], xt[b][:, 1, 1, e], wd[:, 1, :], start=False, stop=True)
                        on_act.filled(last, ta)

                def scores(b):
                    pe.wait_ge(on_act.empty, ta.now())
                    bank = on_dve.take(pe, td)
                    for j in range(G):
                        last = pe.transpose(bank[0:HEADS, j * P:(j + 1) * P], h[b][:, j, C:GAT_IN], s.ident[:, :])
                    on_dve.filled(last, td)

                def body(i):
                    for b in range(2):
                        transposes(b)
                        products(b)
                        scores(b)

                rounds(pe, EG // 2, body, xn_in, ta, td)


def stage_edge_softmax(nc, d, s, psum):
    with Stage(nc, "sm") as m:
        ids = m.sb("ids", [HEADS, EP], I32)
        cut = m.sb("cut", [HEADS, EP + 1])
        top = m.sb("top", [HEADS, EP])
        nxt = m.sb("nxt", [P, ET], I32)
        col = m.sb("col", [P, 1 + ET], I32)
        more = m.sb("more", [P, ET])
        ids_in, own, ready, exps = m.sem("ids_in"), m.sem("own"), m.sem("ready"), m.sem("exps")
        with nc.Block() as block:
            @block.sync
            def _(sp):
                sp.dma_start(ids[:, :], d["dst_rows"][0:HEADS, :]).then_inc(ids_in, 16)
                sp.dma_start(col[:, :], d["dst_col"]).then_inc(ids_in, 16)
                sp.dma_start(nxt[:, :], d["dst_next"]).then_inc(ids_in, 16)
                sp.dma_start(s.dst_row_id[:, :], d["dst_col"][:, 1:1 + ET]).then_inc(ids_in, 16)

            @block.vector
            def _(dve):
                chain = Tally(own)

                def then(ins):
                    ins.then_inc(own, 1)
                    wait(dve, chain.add())

                dve.wait_ge(ids_in, 64)
                then(dve.tensor_copy(s.dst_col[:, :], col[:, :]))
                then(dve.tensor_copy(more[:, :], nxt[:, :]))
                then(dve.tensor_tensor(more[:, :], s.dst_col[:, 1:1 + ET], more[:, :], ALU.is_equal))
                then(dve.scalar_tensor_tensor(s.end_row[:, :], more[:, :], float(SKIP), s.dst_col[:, 1:1 + ET], ALU.mult, ALU.add))
                then(dve.memset(cut[:, 0:1], -FAR))
                then(dve.memset(cut[:, EP:EP + 1], -FAR))
                then(dve.tensor_tensor(cut[:, 1:EP], ids[:, 1:EP], ids[:, 0:EP - 1], ALU.not_equal))
                then(dve.tensor_scalar(cut[:, 1:EP], cut[:, 1:EP], -FAR, None, ALU.mult))
                then(dve.scalar_tensor_tensor(s.scores[:, :], s.scores[:, :], 0.2, s.scores[:, :], ALU.mult, ALU.max))
                then(dve.tensor_tensor_scan(top[:, :], cut[:, 0:EP], s.scores[:, :], 0.0, ALU.add, ALU.max))
                then(dve.tensor_tensor_scan(top[:, ::-1], cut[:, EP:0:-1], top[:, ::-1], 0.0, ALU.add, ALU.max))
                dve.tensor_tensor(s.scores[:, :], s.scores[:, :], top[:, :], ALU.subtract).then_inc(ready, 1)

            @block.scalar
            def _(act):
                act.wait_ge(ready, 1)
                act.activation(s.scores[:, :], s.scores[:, :], ACT.Exp).then_inc(exps, 1)


def run_masks(dve, own, passed, s, here, t, same, carry, row, last_row, tiles):
    for j in range(tiles):
        dve.tensor_scalar(same[:, j, :], row[:, j * P:(j + 1) * P], s.dst_col[:, bass.ds(t + 1 + j, 1)], None, ALU.is_equal)
        last = dve.tensor_scalar(carry[:, j, :], row[:, j * P:(j + 1) * P], s.dst_col[:, bass.ds(t + j, 1)],
                                 last_row[:, 0:1], ALU.is_equal, ALU.mult)
    return last


def stage_edge_sum(nc, d, s, psum):
    WD = GAT_IN
    with Stage(nc, "gs") as m:
        hin = [m.sb(f"hin{b}", [P, G, C]) for b in range(2)]
        row = [m.sb(f"row{b}", [P, GR], I32) for b in range(2)]
        xd = [m.sb(f"xd{b}", [P, G, C]) for b in range(2)]
        msg = [m.sb(f"msg{b}", [P, G, WD]) for b in range(2)]
        exs = [m.sb(f"exs{b}", [HEADS, GR]) for b in range(2)]
        same = [m.sb(f"same{b}", [P, G, P]) for b in range(2)]
        carry = [m.sb(f"carry{b}", [P, G, P]) for b in range(2)]
        run = [m.sb(f"run{b}", [P, G, WD]) for b in range(2)]
        rec = m.sb("rec", [P, 2, G, HEADS])
        agg = [m.sb(f"agg{b}", [P, G, C]) for b in range(2)]
        cur = m.sb("cur", [P, 2, 2 * G], I32)
        h_in, xd_in, stored = m.sems("h_in"), m.sems("xd_in"), m.sems("stored")
        cur_ready, exs_ready, own, msg_ready = m.sem("cur_ready"), m.sem("exs_ready"), m.sem("own"), m.sem("msg_ready")
        agg_ready, start, passed = m.sem("agg_ready"), m.sem("start"), m.sems("passed", 4)
        on_act = m.banks("on_act", 0, 4, psum)
        on_dve = m.banks("on_dve", 4, 2, psum)
        with nc.Block() as block:
            @block.sync
            def _(sp):
                made = Tally(msg_ready)

                def body(i):
                    for b in range(2):
                        wait(sp, made, 1)
                        made.add()
                        g = i * 2 + b
                        sp.dma_start(hin[b][:, :, :], rows_of(d["H"], g * GR, G)).then_inc(h_in[b], 16)
                        sp.dma_start(row[b][:, :], d["dst_rows"][:, bass.ds(g * GR, GR)]).then_inc(h_in[b], 16)

                rounds(sp, EG // 2, body, made)

            @block.gpsimd
            def _(pool):
                pool.memset(run[1][:, G - 1, :], 0.0).then_inc(start, 1)
                ready, summed = Tally(cur_ready), Tally(agg_ready)
                old = [Tally(stored[b], 16) for b in range(2)]

                def body(i):
                    for b in range(2):
                        g = i * 2 + b
                        wait(pool, old[b])
                        hold(pool, passed[0])
                        pool.tensor_copy(cur[:, b, 0:G], s.dst_row_id[:, bass.ds(g * G, G)])
                        pool.tensor_copy(cur[:, b, G:2 * G], s.end_row[:, bass.ds(g * G, G)]).then_inc(cur_ready, 1)
                        wait(pool, ready.add())
                        hold(pool, passed[0])
                        for j in range(G):
                            pool.indirect_dma_start(
                                out=xd[b][:, j, :], out_offset=None, in_=d["x"],
                                in_offset=bass.IndirectOffsetOnAxis(ap=cur[:, b, j:j + 1], axis=0),
                                bounds_check=NP - 1, oob_is_err=False).then_inc(xd_in[b], 16)
                    for b in range(2):
                        wait(pool, summed.add())
                        hold(pool, passed[0])
                        for j in range(G):
                            pool.indirect_dma_start(
                                out=d["X"], out_offset=bass.IndirectOffsetOnAxis(ap=cur[:, b, G + j:G + j + 1], axis=0),
                                in_=agg[b][:, j, :], in_offset=None,
                                bounds_check=NP - 1, oob_is_err=False).then_inc(stored[b], 16)
                            old[b].add()

                rounds(pool, EG // 2, body, ready, summed, *old)
                for b in range(2):
                    pool.wait_ge(stored[b], 16 * G * EG // 2)

            @block.scalar
            def _(act):
                read, exin, used = on_act.reader(), Tally(on_dve.full), Tally(agg_ready)

                def body(i):
                    for b in range(2):
                        wait(act, exin, 1)
                        exin.add()
                        hold(act, passed[3])
                        act.activation(exs[b][:, :], s.scores[:, bass.ds((i * 2 + b) * GR, GR)], ACT.Copy).then_inc(exs_ready, 1)
                    for b in range(2):
                        wait(act, used, 1)
                        used.add()
                        for j in range(G):
                            bank = on_act.get(act, read)
                            act.activation(run[b][:, j, :], bank[:, 0:WD], ACT.Copy).then_inc(on_act.empty, 1)

                rounds(act, EG // 2, body, read, exin, used)

            @block.vector
            def _(dve):
                chain, read = Tally(own), on_dve.reader()
                h_here = [Tally(h_in[b], 16) for b in range(2)]
                x_here = [Tally(xd_in[b], 16) for b in range(2)]
                old = [Tally(stored[b], 16) for b in range(2)]
                sums = Tally(on_act.empty, G)

                def body(i):
                    for b in range(2):
                        t = (i * 2 + b) * G
                        wait(dve, h_here[b].add(2))
                        bank = on_dve.get(dve, read)
                        dve.tensor_copy(msg[b][:, :, C:WD], bank[:, 0:G * HEADS].rearrange("p (j h) -> p j h", h=HEADS)).then_inc(on_dve.empty, 1)
                        dve.wait_ge(on_dve.empty, read.now())
                        for j in range(G):
                            ex = msg[b][:, j, C:WD].rearrange("p (h o) -> p h o", o=1).to_broadcast([P, HEADS, C // HEADS])
                            dve.tensor_tensor(msg[b][:, j, 0:C].rearrange("p (h o) -> p h o", h=HEADS),
                                              hin[b][:, j, :].rearrange("p (h o) -> p h o", h=HEADS), ex, ALU.mult)
                        run_masks(dve, chain, passed[2], s, None, t, same[b], carry[b], row[b], s.last_row, G).then_inc(msg_ready, 1)
                    for b in range(2):
                        wait(dve, sums.add())
                        hold(dve, passed[2])
                        dve.tensor_scalar(rec[:, b], run[b][:, :, C:WD], 1e-9, None, ALU.max).then_inc(own, 1)
                        wait(dve, chain.add())
                        dve.reciprocal(rec[:, b], rec[:, b]).then_inc(own, 1)
                        wait(dve, chain.add())
                        wait(dve, old[b])
                        old[b].add(G)
                        hold(dve, passed[2])
                        for j in range(G):
                            r = rec[:, b, j, :].rearrange("p (h o) -> p h o", o=1).to_broadcast([P, HEADS, C // HEADS])
                            last = dve.tensor_tensor(agg[b][:, j, :].rearrange("p (h o) -> p h o", h=HEADS),
                                                     run[b][:, j, 0:C].rearrange("p (h o) -> p h o", h=HEADS), r, ALU.mult)
                        last.then_inc(own, 1)
                        wait(dve, chain.add())
                        wait(dve, x_here[b].add(G))
                        dve.scalar_tensor_tensor(agg[b][:, :, :], agg[b][:, :, :], 0.0, xd[b][:, :, :], ALU.max, ALU.add).then_inc(agg_ready, 1)

                rounds(dve, EG // 2, body, chain, read, *h_here, *x_here, *old, sums)

            @block.tensor
            def _(pe):
                pe.wait_ge(start, 1)
                ta, td, ex_in, made = on_act.writer(), on_dve.writer(), Tally(exs_ready), Tally(msg_ready)

                def body(i):
                    for b in range(2):
                        wait(pe, ex_in.add())
                        bank = on_dve.take(pe, td)
                        hold(pe, passed[1])
                        for j in range(G):
                            last = pe.transpose(bank[:, j * HEADS:(j + 1) * HEADS], exs[b][:, j * P:(j + 1) * P], s.ident[0:HEADS, 0:HEADS])
                        on_dve.filled(last, td)
                    for b in range(2):
                        wait(pe, made.add())
                        for j in range(G):
                            before = run[1 - b][:, G - 1, :] if j == 0 else run[b][:, j - 1, :]
                            bank = on_act.take(pe, ta)
                            pe.matmul(bank[:, 0:WD], same[b][:, j, :], msg[b][:, j, :], start=True, stop=False)
                            v = ta.now()
                            if not isinstance(v, int) or v > 0:
                                pe.wait_ge(on_act.empty, v)
                            last = pe.matmul(bank[:, 0:WD], carry[b][:, j, :], before, start=False, stop=True)
                            on_act.filled(last, ta)

                rounds(pe, EG // 2, body, ta, td, ex_in, made)


def over(ap, n):
    return ap.unsqueeze(1).to_broadcast([ap.shape[0], n, ap.shape[1]])


def each(ap, n):
    return ap.unsqueeze(2).to_broadcast([ap.shape[0], ap.shape[1], n])


def stage_router_logits(nc, d, s, psum):
    with Stage(nc, "rl") as m:
        rows = [m.sb(f"rows{b}", [P, G, C]) for b in range(2)]
        xn = [m.sb(f"xn{b}", [P, G, C]) for b in range(2)]
        xt = [m.sb(f"xt{b}", [P, 2, GR]) for b in range(2)]
        gate = m.sb("gate", [P, 2, EXPERTS])
        gate_b = m.sb("gate_b", [P, G * EXPERTS])
        st, mv, sd = m.sb("st", [P, 2, G, 6]), m.sb("mv", [P, 2, G, 2]), m.sb("sd", [P, 2, G])
        rows_in, w_in, own = m.sems("rows_in"), m.sem("w_in"), m.sem("own")
        stats_ready, sd_ready, xn_ready, passed = m.sem("stats_ready"), m.sem("sd_ready"), m.sem("xn_ready"), m.sem("passed")
        on_act = m.banks("on_act", 0, 4, psum)
        on_dve = m.banks("on_dve", 4, 2, psum)
        with nc.Block() as block:
            @block.sync
            def _(sp):
                sp.dma_start(gate[:, :, :], d["gate_w"]).then_inc(w_in, 16)
                sp.dma_start(gate_b[:, :], d["gate_b"]).then_inc(w_in, 16)
                used = Tally(xn_ready)

                def body(i):
                    for b in range(2):
                        wait(sp, used, 1)
                        used.add()
                        sp.dma_start(rows[b][:, :, :], rows_of(d["X"], (i * 2 + b) * GR, G)).then_inc(rows_in[b], 16)

                rounds(sp, NG // 2, body, used)

            @block.vector
            def _(dve):
                dve.wait_ge(w_in, 32)
                chain, deviation, read = Tally(own), Tally(sd_ready), on_dve.reader()
                loaded = [Tally(rows_in[b], 16) for b in range(2)]

                def body(i):
                    for b in range(2):
                        wait(dve, loaded[b].add())
                        ln_stats(dve, chain, passed, rows[b], st[:, b], mv[:, b], G, stats_ready)
                    for b in range(2):
                        ln_apply(dve, chain, deviation, rows[b], mv[:, b], sd[:, b], xn[b], G, xn_ready)
                    for b in range(2):
                        bank = on_dve.get(dve, read)
                        hold(dve, passed)
                        dve.tensor_tensor(s.logits[:, bass.ds((i * 2 + b) * G, G), :].rearrange("p t e -> p (t e)"),
                                          bank[:, 0:G * EXPERTS], gate_b[:, :], ALU.add).then_inc(on_dve.empty, 1)

                rounds(dve, NG // 2, body, *loaded, chain, deviation, read)

            @block.scalar
            def _(act):
                stats, read = Tally(stats_ready), on_act.reader()

                def body(i):
                    for b in range(2):
                        ln_deviation(act, stats, mv[:, b], sd[:, b], s.eps, sd_ready)
                    for b in range(2):
                        for k in range(2):
                            bank = on_act.get(act, read)
                            act.activation(xt[b][:, k, :], bank[:, :], ACT.Copy).then_inc(on_act.empty, 1)

                rounds(act, NG // 2, body, stats, read)

            @block.tensor
            def _(pe):
                pe.wait_ge(w_in, 32)
                xn_in, ta, td = Tally(xn_ready), on_act.writer(), on_dve.writer()

                def body(i):
                    for b in range(2):
                        wait(pe, xn_in.add())
                        for k in range(2):
                            bank = on_act.take(pe, ta)
                            for j in range(G):
                                last = pe.transpose(bank[:, j * P:(j + 1) * P], xn[b][:, j, k * P:(k + 1) * P], s.ident[:, :])
                            on_act.filled(last, ta)
                    for b in range(2):
                        pe.wait_ge(on_act.empty, ta.now(2 * (1 - b)))
                        bank = on_dve.take(pe, td)
                        for j in range(G):
                            o = bank[:, j * EXPERTS:(j + 1) * EXPERTS]
                            pe.matmul(o, xt[b][:, 0, j * P:(j + 1) * P], gate[:, 0, :], start=True, stop=False)
                            last = pe.matmul(o, xt[b][:, 1, j * P:(j + 1) * P], gate[:, 1, :], start=False, stop=True)
                        on_dve.filled(last, td)

                rounds(pe, NG // 2, body, xn_in, ta, td)


def stage_router(nc, d, s, psum):
    W = NT * EXPERTS
    with Stage(nc, "ro") as m:
        ex, hot, a, b_, tot, incl = (m.sb(n, [P, NT, EXPERTS]) for n in ("ex", "hot", "a", "b", "tot", "incl"))
        hot16 = m.sb("hot16", [P, NT, EXPERTS], BF16)
        tri, ones = m.sb("tri", [P, P], BF16), m.sb("ones", [P, P], BF16)
        tri32, real = m.sb("tri32", [P, P]), m.sb("real", [P, NT])
        ones_row = m.sb("ones_row", [P, NT])
        top, total, prob = m.sb("top", [P, NT]), m.sb("total", [P, NT]), m.sb("prob", [P, NT])
        rank, base = m.sb("rank", [P, EXPERTS]), m.sb("base", [P, EXPERTS])
        c_in, own, shifted, exps, hot_ready, counted = (m.sem(n) for n in ("c_in", "own", "shifted", "exps", "hot_ready", "counted"))
        cuts = [(0, 512), (512, 1024), (1024, W)]
        flat = lambda t: t[:, :, :].rearrange("p t e -> p (t e)")
        with nc.Block() as block:
            @block.sync
            def _(sp):
                sp.dma_start(rank[:, :], d["expert_rank"]).then_inc(c_in, 16)
                sp.dma_start(tri32[:, :], d["tri"]).then_inc(c_in, 16)
                sp.dma_start(real[:, :], d["real"]).then_inc(c_in, 16)
                sp.dma_start(base[:, :], d["slot_base"]).then_inc(c_in, 16)
                sp.dma_start(s.entry[:, :, 0], d["node_id"], allow_slow_non_contiguous=True).then_inc(c_in, 16)

            @block.vector
            def _(dve):
                chain = Tally(own)

                def then(ins):
                    ins.then_inc(own, 1)
                    wait(dve, chain.add())

                dve.memset(ones[:, :], 1.0)
                dve.memset(ones_row[:, :], 1.0)
                dve.wait_ge(c_in, 80)
                dve.tensor_copy(tri[:, :], tri32[:, :])
                lg = s.logits
                then(dve.tensor_reduce(top[:, :], lg[:, :, :], AX.X, ALU.max))
                dve.tensor_tensor(a[:, :, :], lg[:, :, :], each(top[:, :], EXPERTS), ALU.subtract).then_inc(shifted, 1)
                dve.wait_ge(exps, 1)
                then(dve.tensor_reduce(total[:, :], ex[:, :, :], AX.X, ALU.add))
                then(dve.tensor_reduce(top[:, :], ex[:, :, :], AX.X, ALU.max))
                then(dve.tensor_tensor(hot[:, :, :], ex[:, :, :], each(top[:, :], EXPERTS), ALU.is_ge))
                then(dve.reciprocal(total[:, :], total[:, :]))
                then(dve.tensor_tensor(s.entry[:, :, 1].bitcast(F32), top[:, :], total[:, :], ALU.mult))
                then(dve.tensor_tensor(a[:, :, :], hot[:, :, :], over(rank[:, :], NT), ALU.mult))
                then(dve.tensor_reduce(top[:, :], a[:, :, :], AX.X, ALU.max))
                then(dve.tensor_tensor(hot[:, :, :], a[:, :, :], each(top[:, :], EXPERTS), ALU.is_equal))
                then(dve.tensor_tensor(hot[:, :, :], hot[:, :, :], each(real[:, :], EXPERTS), ALU.mult))
                dve.tensor_copy(hot16[:, :, :], hot[:, :, :]).then_inc(hot_ready, 1)
                dve.wait_ge(counted, 1)
                for k, (lo, hi) in enumerate(cuts):
                    dve.tensor_copy(flat(incl)[:, lo:hi], psum[k][:, 0:hi - lo])
                    last = dve.tensor_copy(flat(tot)[:, lo:hi], psum[3 + k][:, 0:hi - lo])
                then(last)
                for e in range(EXPERTS):
                    last = dve.tensor_tensor_scan(a[:, :, e], ones_row[:, :], tot[:, :, e], 0.0, ALU.mult, ALU.add)
                then(last)
                then(dve.tensor_tensor(a[:, :, :], a[:, :, :], tot[:, :, :], ALU.subtract))
                then(dve.tensor_tensor(a[:, :, :], a[:, :, :], incl[:, :, :], ALU.add))
                then(dve.tensor_scalar(b_[:, :, :], a[:, :, :], float(CAP), float(SKIP), ALU.is_gt, ALU.mult))
                then(dve.tensor_tensor(a[:, :, :], a[:, :, :], over(base[:, :], NT), ALU.add))
                then(dve.tensor_tensor(a[:, :, :], a[:, :, :], b_[:, :, :], ALU.add))
                then(dve.tensor_scalar(a[:, :, :], a[:, :, :], -float(SKIP), None, ALU.add))
                then(dve.tensor_tensor(a[:, :, :], a[:, :, :], hot[:, :, :], ALU.mult))
                then(dve.tensor_reduce(top[:, :], a[:, :, :], AX.X, ALU.add))
                then(dve.tensor_scalar(s.slot[:, :], top[:, :], float(SKIP), None, ALU.add))

            @block.scalar
            def _(act):
                act.wait_ge(shifted, 1)
                act.activation(ex[:, :, :], a[:, :, :], ACT.Exp).then_inc(exps, 1)

            @block.tensor
            def _(pe):
                pe.wait_ge(hot_ready, 1)
                for k, (lo, hi) in enumerate(cuts):
                    pe.matmul(psum[k][:, 0:hi - lo], tri[:, :], flat(hot16)[:, lo:hi], start=True, stop=True)
                    last = pe.matmul(psum[3 + k][:, 0:hi - lo], ones[:, :], flat(hot16)[:, lo:hi], start=True, stop=True)
                last.then_inc(counted, 1)


def stage_table(nc, d, s, table, slots, tag):
    K = 8
    with Stage(nc, tag) as m:
        cur = [m.sb(f"cur{b}", [P, K], I32) for b in range(2)]
        ent = [m.sb(f"ent{b}", [P, K, 2], I32) for b in range(2)]
        sent, cur_ready, passed = m.sems("sent"), m.sem("cur_ready"), m.sem("passed")
        with nc.Block() as block:
            @block.gpsimd
            def _(pool):
                ready, old = Tally(cur_ready), [Tally(sent[b], 16) for b in range(2)]

                def body(i):
                    for b in range(2):
                        t = (i * 2 + b) * K
                        wait(pool, old[b])
                        hold(pool, passed)
                        pool.tensor_copy(cur[b][:, :], s.slot[:, bass.ds(t, K)])
                        pool.tensor_copy(ent[b][:, :, :], s.entry[:, bass.ds(t, K), :]).then_inc(cur_ready, 1)
                        wait(pool, ready.add())
                        hold(pool, passed)
                        for j in range(K):
                            pool.indirect_dma_start(
                                out=d[table], out_offset=bass.IndirectOffsetOnAxis(ap=cur[b][:, j:j + 1], axis=0),
                                in_=ent[b][:, j, :], in_offset=None,
                                bounds_check=slots - 1, oob_is_err=False).then_inc(sent[b], 16)
                            old[b].add()

                rounds(pool, NT // K // 2, body, ready, *old)
                for b in range(2):
                    pool.wait_ge(sent[b], 16 * NT // 2)


def stage_ffn(nc, d, s, psum, moe):
    tag = "moe" if moe else "mod"
    M = 2 * XB if moe else 4
    RN = (EXPERTS * XB if moe else SB) // M
    R = XB if moe else 4
    table = d["moe_table"] if moe else d["mod_table"]
    DST = d["X"] if moe else d["out"]
    HF = FB // 2
    HC = HID // P
    LAG = R - 1
    FR = mybir.dt.float32r
    with Stage(nc, tag) as m:
        tab = [m.sb(f"tab{r}", [P, FT, 2], I32) for r in range(R)]
        rows = [m.sb(f"rows{r}", [P, FT, C]) for r in range(R)]
        xn = [m.sb(f"xn{r}", [P, FT, C]) for r in range(2 if moe else R)]
        NX = len(xn)
        RING = 4
        x_raw, x = m.sb("x_raw", [P, 2, FB]), [m.sb(f"x_{n}", [P, 2, FB], FR) for n in ("high", "low")]
        h_raw, h = m.sb("h_raw", [P, RING, FB]), [m.sb(f"h_{n}", [P, HC, FB], FR) for n in ("high", "low")]
        y = [m.sb(f"y{b}", [P, FT, C]) for b in range(2)]
        nb = 2 if moe else 1
        w1_raw, w1 = m.sb("w1_raw", [P, 2, HID]), [m.sb(f"w1_{n}", [P, 2, HID], FR) for n in ("high", "low")]
        w2_raw, w2 = m.sb("w2_raw", [P, HC, C]), [m.sb(f"w2_{n}", [P, HC, C], FR) for n in ("high", "low")]
        b1 = [m.sb(f"b1{q}", [P, HC]) for q in range(nb)]
        b2 = [m.sb(f"b2{q}", [P, C]) for q in range(nb)]
        st, mv, sd = m.sb("st", [P, FT, 6]), m.sb("mv", [P, 2, FT, 2]), m.sb("sd", [P, 2, FT])
        safe = m.sb("safe", [P, FT, C]) if moe else None
        low = m.sb("low", [P, FT, C]) if moe else None
        tab_in, rows_in, scattered = m.sems("tab_in", R), m.sems("rows_in", R), m.sems("scattered", R)
        (w_in, zeroed, stats_ready, sd_ready, xn_ready, own, y_ready, w1_high, w2_high, w1_split, w2_split, x_split, h_split) = (
            m.sem(n) for n in ("w_in", "zeroed", "stats_ready", "sd_ready", "xn_ready", "own", "y_ready",
                               "w1_high", "w2_high", "w1_split", "w2_split", "x_split", "h_split"))
        passed = m.sems("passed", 3)
        turned = m.banks("turned", 0, 2, psum)
        hidden = m.banks("hidden", 2, 4, psum)
        result = m.banks("result", 6, 2, psum)

        def last(i):
            return isinstance(i, int) and i == RN - 1

        def all_rounds(eng, body, *tallies):
            rounds(eng, RN - 1, body, *tallies)
            body(RN - 1)

        def at_start(i, k):
            return isinstance(i, int) and i == 0 and k == 0

        with nc.Block() as block:
            @block.sync
            def _(sp):
                done = Tally(w2_split)
                freed = [Tally(scattered[r], 16 * FT) for r in range(R)]

                def weights(e, q):
                    pick = (lambda a: a[bass.ds(e, 1)].rearrange("o p n -> (o p) n")) if moe else (lambda a: a)
                    for t, name in ((w1_raw[:, :, :].rearrange("p k n -> p (k n)"), "w1"),
                                    (w2_raw[:, :, :].rearrange("p k n -> p (k n)"), "w2"),
                                    (b1[q][:, :], "b1"), (b2[q][:, :], "b2")):
                        sp.dma_start(t, pick(d[f"{tag}_{name}"])).then_inc(w_in, 16)

                def body(i):
                    for k in range(M):
                        r = k % R
                        wait(sp, freed[r])
                        freed[r].add()
                        sp.dma_start(tab[r][:, :, :], rows_of(table, (i * M + k) * FB, FT)).then_inc(tab_in[r], 16)
                        if moe and k % XB == 3 and not (k > XB and last(i)):
                            wait(sp, done.add())
                            weights(i * 2 + k // XB + 1, 1 - k // XB)

                weights(0, 0)
                all_rounds(sp, body, *freed, *([done] if moe else []))

            @block.gpsimd
            def _(pool):
                for t in rows + ([] if moe else xn):
                    pool.memset(t[:, :, :], 0.0).then_inc(zeroed, 1)
                pool.wait_ge(zeroed, R if moe else 2 * R)
                here, made = [Tally(tab_in[r], 16) for r in range(R)], Tally(y_ready)

                def gather(k):
                    r = k % R
                    wait(pool, here[r].add())
                    hold(pool, passed[0])
                    for j in range(FT):
                        for t, src in ((rows[r], d["X"] if moe else d["base"]),) + (() if moe else ((xn[r], d["XN"]),)):
                            pool.indirect_dma_start(
                                out=t[:, j, :], out_offset=None, in_=src,
                                in_offset=bass.IndirectOffsetOnAxis(ap=tab[r][:, j, 0:1], axis=0),
                                bounds_check=NP - 1, oob_is_err=False).then_inc(rows_in[r], 16)

                def scatter(k):
                    r = k % R
                    wait(pool, made.add())
                    hold(pool, passed[0])
                    for j in range(FT):
                        pool.indirect_dma_start(
                            out=DST, out_offset=bass.IndirectOffsetOnAxis(ap=tab[r][:, j, 0:1], axis=0),
                            in_=rows[r][:, j, :], in_offset=None,
                            bounds_check=NP - 1, oob_is_err=False).then_inc(scattered[r], 16)

                def body(i):
                    for k in range(M):
                        gather(k)
                        if isinstance(i, int) and i == 0 and k < LAG:
                            made.skip()
                        else:
                            scatter(k - LAG)

                all_rounds(pool, body, *here, made)
                for k in range(LAG):
                    scatter(M - LAG + k)
                for r in range(R):
                    pool.wait_ge(scattered[r], 16 * FT * RN * M // R)

            @block.scalar
            def _(act):
                stats, turn, read, res = Tally(stats_ready), turned.reader(), hidden.reader(), result.reader()
                w_here, finished, used = Tally(w_in, 64), Tally(y_ready), Tally(h_split)
                fn = ACT.Relu if moe else ACT.Gelu_apprx_tanh

                def weights_high(whole, high, ready):
                    for n in range(2):
                        half = slice(n * (whole.shape[1] // 2), (n + 1) * (whole.shape[1] // 2))
                        ins = act.activation(high[:, half, :], whole[:, half, :], ACT.Copy)
                    ins.then_inc(ready, 1)

                def body(i):
                    for k in range(M):
                        q = k // XB if moe else 0
                        if at_start(i, k):
                            res.skip(FT)
                            finished.skip()
                        else:
                            wait(act, finished, 1)
                            finished.add()
                            hold(act, passed[2])
                        for j in range(FT):
                            for t in range(2 * j, min(2 * j + 2, FT)):
                                bank = turned.get(act, turn)[:, 0:C].rearrange("p (k n) -> p k n", k=2)
                                n = slice(t * P, (t + 1) * P)
                                act.activation(x_raw[:, :, n], bank, ACT.Copy)
                                act.activation(x[0][:, :, n], bank, ACT.Copy).then_inc(turned.empty, 1)
                            if not at_start(i, k):
                                result_out(k - 1, j)
                            if j == 0 and moe and not (last(i) and k == M - 1):
                                ln_deviation(act, stats, mv[:, (k + 1) % 2], sd[:, (k + 1) % 2], s.eps, sd_ready)
                            if j == 1 and moe and k % XB == 0:
                                wait(act, w_here.add())
                                hold(act, passed[2])
                                weights_high(w1_raw, w1[0], w1_high)
                        if moe and k % XB == 0:
                            weights_high(w2_raw, w2[0], w2_high)
                        for f in range(HC):
                            wait(act, used, RING - 1)
                            used.add()
                            hold(act, passed[2])
                            for half in range(2):
                                bank = hidden.get(act, read)
                                act.activation(h_raw[:, f % RING, half * HF:(half + 1) * HF], bank[:, 0:HF], fn, bias=b1[q][:, f:f + 1]).then_inc(hidden.empty, 1)

                def result_out(k, j):
                    bank = result.get(act, res)
                    act.activation(y[k % 2][:, j, :], bank[:, 0:C], ACT.Copy, scale=tab[k % R][:, j, 1:2].bitcast(F32)).then_inc(result.empty, 1)

                if moe:
                    ln_deviation(act, stats, mv[:, 0], sd[:, 0], s.eps, sd_ready)
                else:
                    wait(act, w_here.add())
                    weights_high(w1_raw, w1[0], w1_high)
                    weights_high(w2_raw, w2[0], w2_high)
                all_rounds(act, body, stats, turn, read, res, finished, used, *([w_here] if moe else []))
                wait(act, finished, 1)
                hold(act, passed[2])
                for j in range(FT):
                    result_out(M - 1, j)

            @block.vector
            def _(dve):
                chain, deviation = Tally(own), Tally(sd_ready)
                loaded = [Tally(rows_in[r], 16 * FT * (1 if moe else 2)) for r in range(R)]
                turn, read, res = turned.reader(), hidden.reader(), Tally(result.empty)
                highs = {w1_high: Tally(w1_high), w2_high: Tally(w2_high)}

                def then(ins):
                    ins.then_inc(own, 1)
                    wait(dve, chain.add())

                def split_weights(whole, w, high, ready):
                    wait(dve, highs[high].add())
                    dve.tensor_tensor(w[1][:, :, :], whole[:, :, :], w[0][:, :, :].bitcast(F32), ALU.subtract).then_inc(ready, 1)

                def statistics(k):
                    r = k % R
                    wait(dve, loaded[r].add())
                    ln_stats(dve, chain, passed[1], rows[r], st, mv[:, k % 2], FT, stats_ready)

                def normalise(k):
                    ln_apply(dve, chain, deviation, rows[k % R], mv[:, k % 2], sd[:, k % 2], xn[k % 2], FT, xn_ready)

                def bias(k, j):
                    r, q = k % R, (k % M) // XB if moe else 0
                    wait(dve, res.add())
                    yj = y[k % 2][:, j, :]
                    ins = dve.scalar_tensor_tensor(yj, b2[q][:, :], tab[r][:, j, 1:2].bitcast(F32), yj, ALU.mult, ALU.add)
                    if j == FT - 1:
                        then(ins)

                def finish(k):
                    r, z = k % R, y[k % 2]
                    if moe:
                        then(dve.tensor_scalar(low[:, :, :], z[:, :, :], 0.0, None, ALU.min))
                        yield
                        then(dve.scalar_tensor_tensor(safe[:, :, :], z[:, :, :], 0.0, low[:, :, :], ALU.max, ALU.add))
                        yield
                        dve.tensor_scalar(safe[:, :, :], safe[:, :, :], 1e4, -1e4, ALU.min, ALU.max)
                        dve.tensor_scalar(low[:, :, :].bitcast(U32), z[:, :, :], 0.0, 0.0, ALU.mult, ALU.is_equal).then_inc(own, 1)
                        wait(dve, chain.add())
                        yield
                        hold(dve, passed[1])
                        then(dve.copy_predicated(safe[:, :, :], low[:, :, :].bitcast(U32), z[:, :, :]))
                    else:
                        wait(dve, loaded[r].add())
                    yield
                    dve.tensor_tensor(rows[r][:, :, :], rows[r][:, :, :], (safe if moe else z)[:, :, :], ALU.add).then_inc(y_ready, 1)

                FINISH = 4 if moe else 0

                def body(i):
                    for k in range(M):
                        steps, last_block = iter(()), last(i) and k == M - 1
                        if at_start(i, k):
                            res.skip(FT)
                            chain.skip()
                        if at_start(i, k) or at_start(i, k - 1):
                            chain.skip(FINISH)
                            if not moe:
                                loaded[(k - 2) % R].skip()
                        else:
                            steps = finish(k - 2)
                        if moe and not last_block:
                            statistics(k + 1)
                        for j in range(FT):
                            if not at_start(i, k):
                                bias(k - 1, j)
                            if j == 1:
                                turn.add(FT)
                                dve.wait_ge(turned.empty, turn.now())
                                dve.tensor_tensor(x[1][:, :, :], x_raw[:, :, :], x[0][:, :, :].bitcast(F32), ALU.subtract).then_inc(x_split, 1)
                                if moe and k % XB == 0:
                                    split_weights(w1_raw, w1, w1_high, w1_split)
                            if j == 2 and moe and not last_block:
                                normalise(k + 1)
                            if j < 4:
                                next(steps, None)
                        for f in range(HC):
                            read.add(2)
                            dve.wait_ge(hidden.empty, read.now())
                            then(dve.tensor_copy(h[0][:, f, :], h_raw[:, f % RING, :]))
                            dve.tensor_tensor(h[1][:, f, :], h_raw[:, f % RING, :], h[0][:, f, :].bitcast(F32), ALU.subtract).then_inc(h_split, 1)
                            if f == 0:
                                next(steps, None)
                            if moe and f == 3 and k % XB == 0:
                                split_weights(w2_raw, w2, w2_high, w2_split)

                if not moe:
                    split_weights(w1_raw, w1, w1_high, w1_split)
                    split_weights(w2_raw, w2, w2_high, w2_split)
                if moe:
                    statistics(0)
                    normalise(0)
                all_rounds(dve, body, chain, deviation, *loaded, turn, read, res, *(highs.values() if moe else []))
                for _ in finish(M - 2):
                    pass
                for j in range(FT):
                    bias(M - 1, j)
                for _ in finish(M - 1):
                    pass

            @block.tensor
            def _(pe):
                tt, th, tr = turned.writer(), hidden.writer(), result.writer()
                xn_in, w1_in, w2_in, x_in, h_in = Tally(xn_ready), Tally(w1_split), Tally(w2_split), Tally(x_split), Tally(h_split)
                loaded = [Tally(rows_in[r], 16 * FT * 2) for r in range(R)]

                def product(out, a, sa, b, sb, start, stop):
                    pe.matmul(out, a[0][sa], b[0][sb], start=start, stop=False)
                    pe.matmul(out, a[0][sa], b[1][sb], start=False, stop=False)
                    return pe.matmul(out, a[1][sa], b[0][sb], start=False, stop=stop)

                every = slice(None)

                def turn(k, j):
                    bank = turned.take(pe, tt)
                    for c in range(2):
                        last = pe.transpose(bank[:, c * P:(c + 1) * P], xn[k % NX][:, j, c * P:(c + 1) * P], s.ident[:, :])
                    turned.filled(last, tt)

                def first(k):
                    wait(pe, x_in.add())
                    for f in range(HC):
                        fs = slice(f * P, (f + 1) * P)
                        for half in range(2):
                            bank = hidden.take(pe, th)
                            n = slice(half * HF, (half + 1) * HF)
                            for c in range(2):
                                last = product(bank[:, 0:HF], w1, (every, c, fs), x, (every, c, n), c == 0, c == 1)
                            hidden.filled(last, th)

                def second(k, j):
                    bank = result.take(pe, tr)
                    js = slice(j * P, (j + 1) * P)
                    for f in range(HC):
                        if j == 0:
                            wait(pe, h_in.add())
                        last = product(bank[:, 0:C], h, (every, f, js), w2, (every, f, every), f == 0, f == HC - 1)
                    result.filled(last, tr)

                def body(i):
                    for k in range(M):
                        wait(pe, xn_in.add() if moe else loaded[k % R].add())
                        if at_start(i, k):
                            tr.skip(FT)
                            h_in.skip(HC)
                        for j in range(FT):
                            for t in range(2 * j, min(2 * j + 2, FT)):
                                turn(k, t)
                            if moe and k % XB == 1 and j == 0:
                                wait(pe, w2_in.add())
                            if not at_start(i, k):
                                second(k - 1, j)
                        if moe and k % XB == 0:
                            wait(pe, w1_in.add())
                        first(k)

                if not moe:
                    wait(pe, w1_in.add())
                    wait(pe, w2_in.add())
                all_rounds(pe, body, tt, th, tr, x_in, h_in, *((xn_in, w1_in, w2_in) if moe else loaded))
                for j in range(FT):
                    second(M - 1, j)


H1 = 64


def planar(row):
    return row[:, H1:C].rearrange("p (c x) -> p x c", x=3)


def ln_apply_planar(dve, own, deviation, rows, mv, sd, out, tiles, ready):
    wait(dve, deviation.add())
    dve.reciprocal(sd[:, :], sd[:, :]).then_inc(own.sem, 1)
    wait(dve, own.add())
    for j in range(tiles):
        dve.tensor_scalar(out[:, j, 0:H1], rows[:, j, 0:H1], mv[:, j, 0:1], sd[:, j:j + 1], ALU.subtract, ALU.mult)
        last = dve.tensor_scalar(out[:, j, H1:C].rearrange("p (x c) -> p x c", x=3), planar(rows[:, j, :]),
                                 mv[:, j, 0:1], sd[:, j:j + 1], ALU.subtract, ALU.mult)
    last.then_inc(ready, 1)


def stage_edge_mlp(nc, d, s, psum):
    R_IN = 16
    with Stage(nc, "em") as m:
        rbf = [m.sb(f"rbf{b}", [R_IN, GR]) for b in range(2)]
        r1 = [m.sb(f"r1{b}", [H1, GR]) for b in range(2)]
        r2 = [m.sb(f"r2{b}", [H1, GR]) for b in range(2)]
        m1, m2, m3 = m.sb("m1", [R_IN, H1]), m.sb("m2", [H1, H1]), m.sb("m3", [H1, H1])
        w_in, rbf_in, passed = m.sem("w_in"), m.sems("rbf_in"), m.sems("passed")
        on_act = m.banks("on_act", 0, 6, psum)
        with nc.Block() as block:
            @block.sync
            def _(sp):
                for t, name in ((m1, "M1"), (m2, "M2"), (m3, "M3")):
                    sp.dma_start(t[:, :], d[name]).then_inc(w_in, 16)
                read = Tally(on_act.empty, 6)

                def body(i):
                    for b in range(2):
                        wait(sp, read)
                        sp.dma_start(rbf[b][:, :], d["rbf"][:, bass.ds((i * 2 + b) * GR, GR)]).then_inc(rbf_in[b], 16)
                    read.add()

                rounds(sp, EG // 2, body, read)

            @block.scalar
            def _(act):
                t = on_act.reader()

                def body(i):
                    for out in (r1, r2, None):
                        for b in range(2):
                            bank = on_act.get(act, t)
                            if out is None:
                                hold(act, passed[0])
                                o = s.radial[:, bass.ds((i * 2 + b) * GR, GR)]
                            else:
                                o = out[b][:, :]
                            act.activation(o, bank[0:H1, :], ACT.Silu).then_inc(on_act.empty, 1)

                rounds(act, EG // 2, body, t)

            @block.tensor
            def _(pe):
                pe.wait_ge(w_in, 48)
                t, here = on_act.writer(), [Tally(rbf_in[b], 16) for b in range(2)]

                def body(i):
                    for w, src in ((m1, rbf), (m2, r1), (m3, r2)):
                        for b in range(2):
                            if src is rbf:
                                wait(pe, here[b].add())
                            else:
                                pe.wait_ge(on_act.empty, t.now(1))
                            bank = on_act.take(pe, t, src is not rbf)
                            hold(pe, passed[1])
                            on_act.filled(pe.matmul(bank[0:H1, :], w[:, :], src[b][:, :], start=True, stop=True), t)

                rounds(pe, EG // 2, body, t, *here)


def stage_messages(nc, d, s, psum):
    with Stage(nc, "ms") as m:
        rows, xn, up, msg, run, a, bb, dl = ([m.sb(f"{n}{b}", [P, G, C]) for b in range(2)]
                                             for n in ("rows", "xn", "up", "msg", "run", "a", "bb", "dl"))
        xt = [m.sb(f"xt{b}", [P, 2, GR]) for b in range(2)]
        rad = [m.sb(f"rad{b}", [H1, GR]) for b in range(2)]
        row = [m.sb(f"row{b}", [P, GR], I32) for b in range(2)]
        sh = [m.sb(f"sh{b}", [P, G, 4]) for b in range(2)]
        same = [m.sb(f"same{b}", [P, G, P]) for b in range(2)]
        carry = [m.sb(f"carry{b}", [P, G, P]) for b in range(2)]
        src_col = m.sb("src_col", [P, ET], I32)
        curg, cure = m.sb("curg", [P, 2, G], I32), m.sb("cure", [P, 2, G], I32)
        w_up, w_lin, w_b = (m.sb(n, [P, 2, P]) for n in ("w_up", "w_lin", "w_b"))
        m4 = m.sb("m4", [H1, C])
        wc = m.sb("wc", [P, 9, H1])
        t1, t2, t3 = (m.sb(n, [P, G, H1]) for n in ("t1", "t2", "t3"))
        v1, v2 = (m.sb(n, [P, G, 3, H1]) for n in ("v1", "v2"))
        st, mv, sd = m.sb("st", [P, 2, G, 6]), m.sb("mv", [P, 2, G, 2]), m.sb("sd", [P, 2, G])
        w_in, row_in, rows_in, scattered = m.sem("w_in"), m.sems("row_in"), m.sems("rows_in"), m.sems("scattered")
        (own, stats_ready, sd_ready, xn_ready, msg_ready, bb_ready, rad_ready, start, g_ready, e_ready) = (
            m.sem(n) for n in ("own", "stats_ready", "sd_ready", "xn_ready", "msg_ready", "bb_ready", "rad_ready", "start", "g_ready", "e_ready"))
        passed = m.sems("passed", 4)
        on_act = m.banks("on_act", 0, 4, psum)
        on_dve = m.banks("on_dve", 4, 4, psum)
        PER_GROUP = 2 + 2 + G + 2 + 2 + 2 + 2
        with nc.Block() as block:
            @block.sync
            def _(sp):
                for t, name in ((w_up[:, :, :], "w_up"), (w_lin[:, :, :], "w_lin"), (w_b[:, :, :], "w_b"), (m4[:, :], "M4"), (wc[:, :, :], "wc"), (src_col[:, :], "src_col")):
                    sp.dma_start(t, d[name]).then_inc(w_in, 16)
                made = Tally(msg_ready)

                def body(i):
                    for b in range(2):
                        g = i * 2 + b
                        wait(sp, made, 1)
                        made.add()
                        sp.dma_start(row[b][:, :], d["dst_rows"][:, bass.ds(g * GR, GR)]).then_inc(row_in[b], 16)
                        sp.dma_start(sh[b][:, :, :], rows_of(d["sh"], g * GR, G)).then_inc(row_in[b], 16)

                rounds(sp, EG // 2, body, made)

            @block.gpsimd
            def _(pool):
                pool.memset(run[1][:, G - 1, :], 0.0).then_inc(start, 1)
                pool.wait_ge(w_in, 96)
                gi, ei, used = Tally(g_ready), Tally(e_ready), Tally(xn_ready)
                here, old, made = [Tally(rows_in[b], 16) for b in range(2)], [Tally(scattered[b], 16) for b in range(2)], Tally(on_act.empty, 2 * PER_GROUP)

                def gather(i, b):
                    wait(pool, here[b])
                    wait(pool, used, 1)
                    used.add()
                    hold(pool, passed[0])
                    pool.tensor_copy(curg[:, b, :], src_col[:, bass.ds((i * 2 + b) * G, G)]).then_inc(g_ready, 1)
                    wait(pool, gi.add())
                    hold(pool, passed[0])
                    for j in range(G):
                        pool.indirect_dma_start(out=rows[b][:, j, :], out_offset=None, in_=d["X"],
                                                in_offset=bass.IndirectOffsetOnAxis(ap=curg[:, b, j:j + 1], axis=0),
                                                bounds_check=NP - 1, oob_is_err=False).then_inc(rows_in[b], 16)
                        here[b].add()

                def scatter(i, b):
                    wait(pool, old[b])
                    hold(pool, passed[0])
                    pool.tensor_copy(cure[:, b, :], s.end_row[:, bass.ds((i * 2 + b) * G, G)]).then_inc(e_ready, 1)
                    wait(pool, ei.add())
                    if b == 0:
                        made.add()
                    wait(pool, made)
                    hold(pool, passed[0])
                    for j in range(G):
                        pool.indirect_dma_start(out=d["D"], out_offset=bass.IndirectOffsetOnAxis(ap=cure[:, b, j:j + 1], axis=0),
                                                in_=dl[b][:, j, :], in_offset=None,
                                                bounds_check=NP - 1, oob_is_err=False).then_inc(scattered[b], 16)
                        old[b].add()

                def body(i):
                    for b in range(2):
                        gather(i, b)
                    for b in range(2):
                        if isinstance(i, int):
                            ei.skip()
                            made.skip(1 - b)
                            old[b].skip(G)
                        else:
                            scatter(i - 1, b)

                rounds(pool, EG // 2, body, gi, ei, used, made, *here, *old)
                for b in range(2):
                    scatter(EG // 2 - 1, b)
                for b in range(2):
                    pool.wait_ge(scattered[b], 16 * G * EG // 2)

            @block.scalar
            def _(act):
                stats, read, old = Tally(stats_ready), on_act.reader(), [Tally(scattered[b], 16) for b in range(2)]
                made = Tally(msg_ready)

                def two(out, n=2):
                    for k in range(n):
                        bank = on_act.get(act, read)
                        act.activation(out[:, k * (G // n):(k + 1) * (G // n), :], bank[:, 0:G * C // n].rearrange("p (j c) -> p j c", c=C), ACT.Copy).then_inc(on_act.empty, 1)

                def turned(out):
                    for k in range(2):
                        bank = on_act.get(act, read)
                        act.activation(out[:, k, :], bank[:, :], ACT.Copy).then_inc(on_act.empty, 1)

                def body(i):
                    for b in range(2):
                        ln_deviation(act, stats, mv[:, b], sd[:, b], s.eps, sd_ready)
                    for b in range(2):
                        wait(act, made, 1)
                        made.add()
                        hold(act, passed[3])
                        act.activation(rad[b][:, :], s.radial[:, bass.ds((i * 2 + b) * GR, GR)], ACT.Copy).then_inc(rad_ready, 1)
                    for b in range(2):
                        turned(xt[b])
                    for b in range(2):
                        two(up[b])
                    for b in range(2):
                        two(run[b], G)
                    for b in range(2):
                        turned(xt[b])
                        two(a[b])
                    for b in range(2):
                        turned(xt[b])
                        wait(act, old[b])
                        old[b].add(G)
                        two(dl[b])

                rounds(act, EG // 2, body, stats, read, made, *old)

            @block.vector
            def _(dve):
                dve.wait_ge(w_in, 96)
                chain, deviation, read = Tally(own), Tally(sd_ready), on_dve.reader()
                loaded = [Tally(rows_in[b], 16 * G) for b in range(2)]
                row_here = [Tally(row_in[b], 32) for b in range(2)]
                on_a = Tally(on_act.empty)

                def then(ins):
                    ins.then_inc(own, 1)
                    wait(dve, chain.add())

                def tt(o, x, y, op=ALU.mult):
                    then(dve.tensor_tensor(o, x, y, op))

                x3 = lambda t: t[:, :, H1:C].rearrange("p j (x c) -> p j x c", x=3)

                def messages(i, b):
                    wait(dve, row_here[b].add())
                    wait(dve, on_a)
                    x0 = up[b][:, :, 0:H1]
                    s0 = sh[b][:, :, 0]
                    for k in range(2):
                        bank = on_dve.get(dve, read)
                        j2 = slice(2 * k, 2 * k + 2)
                        w = bank[:, :].rearrange("p (j f c) -> p j f c", j=2, f=4)
                        dve.tensor_tensor(t1[:, j2, :], w[:, :, 0, :], x0[:, j2, :], ALU.mult)
                        dve.tensor_tensor(t2[:, j2, :], w[:, :, 1, :], x0[:, j2, :], ALU.mult)
                        for x in range(3):
                            dve.tensor_tensor(v1[:, j2, x, :], w[:, :, 2, :], x3(up[b])[:, j2, x, :], ALU.mult)
                        dve.tensor_copy(t3[:, j2, :], w[:, :, 3, :]).then_inc(on_dve.empty, 1)
                    dve.wait_ge(on_dve.empty, read.now())
                    for j in range(G):
                        c = lambda k: sh[b][:, j, k:k + 1]
                        u = lambda x: x3(up[b])[:, j, x, :]
                        then(dve.tensor_scalar(v2[:, j, 0, :], u(0), c(1), None, ALU.mult))
                        then(dve.scalar_tensor_tensor(v2[:, j, 0, :], u(1), c(2), v2[:, j, 0, :], ALU.mult, ALU.add))
                        then(dve.scalar_tensor_tensor(v2[:, j, 0, :], u(2), c(3), v2[:, j, 0, :], ALU.mult, ALU.add))
                    then(dve.scalar_tensor_tensor(t3[:, :, :], v2[:, :, 0, :], 3.0 ** -0.5, t3[:, :, :], ALU.mult, ALU.mult))
                    for j in range(G):
                        dve.scalar_tensor_tensor(msg[b][:, j, 0:H1], t1[:, j, :], sh[b][:, j, 0:1], t3[:, j, :], ALU.mult, ALU.add)
                        last = dve.tensor_scalar(v1[:, j].rearrange("p x c -> p (x c)"), v1[:, j].rearrange("p x c -> p (x c)"), sh[b][:, j, 0:1], None, ALU.mult)
                    then(last)
                    for j in range(G):
                        for x in range(3):
                            dve.scalar_tensor_tensor(x3(msg[b])[:, j, x, :], t2[:, j, :], sh[b][:, j, 1 + x:2 + x], v1[:, j, x, :], ALU.mult, ALU.add)
                    run_masks(dve, chain, passed[1], s, None, (i * 2 + b) * G, same[b], carry[b], row[b], s.last_row, G).then_inc(msg_ready, 1)

                def products(b):
                    wait(dve, on_a)
                    a0, a1, k = a[b][:, :, 0:H1], x3(a[b]), lambda n: over(wc[:, n, :], G)
                    vv, p_, q_ = t1[:, :, :], t2[:, :, :], t3[:, :, :]
                    tt(v1[:, :, :, :].rearrange("p j x c -> p j (x c)"), a[b][:, :, H1:C], a[b][:, :, H1:C])
                    tt(vv, v1[:, :, 0, :], v1[:, :, 1, :], ALU.add)
                    tt(vv, vv, v1[:, :, 2, :], ALU.add)
                    tt(p_, a0, k(3))
                    tt(p_, p_, k(1), ALU.add)
                    tt(p_, p_, a0)
                    tt(q_, vv, k(4))
                    tt(p_, p_, q_, ALU.add)
                    tt(p_, p_, k(0), ALU.add)
                    tt(p_, p_, a0)
                    tt(q_, vv, k(2))
                    tt(bb[b][:, :, 0:H1], p_, q_, ALU.add)
                    tt(p_, a0, k(7))
                    tt(p_, p_, k(6), ALU.add)
                    tt(p_, p_, a0)
                    tt(q_, vv, k(8))
                    tt(p_, p_, q_, ALU.add)
                    tt(p_, p_, k(5), ALU.add)
                    for x in range(3):
                        last = dve.tensor_tensor(x3(bb[b])[:, :, x, :], a1[:, :, x, :], p_, ALU.mult)
                    last.then_inc(bb_ready, 1)

                bd, md = Tally(bb_ready), Tally(msg_ready)

                def body(i):
                    for b in range(2):
                        wait(dve, loaded[b].add())
                        ln_stats(dve, chain, passed[1], rows[b], st[:, b], mv[:, b], G, stats_ready)
                    for b in range(2):
                        ln_apply_planar(dve, chain, deviation, rows[b], mv[:, b], sd[:, b], xn[b], G, xn_ready)
                    on_a.add(4)
                    for b in range(2):
                        on_a.add(2)
                        messages(i, b)
                        wait(dve, md.add())
                    on_a.add(2 * G)
                    for b in range(2):
                        on_a.add(4)
                        products(b)
                        wait(dve, bd.add())
                    on_a.add(8)

                rounds(dve, EG // 2, body, *loaded, *row_here, chain, deviation, read, on_a, bd, md)

            @block.tensor
            def _(pe):
                pe.wait_ge(w_in, 96)
                pe.wait_ge(start, 1)
                ta, td = on_act.writer(), on_dve.writer()
                xn_in, rad_in, msg_in, bb_in = Tally(xn_ready), Tally(rad_ready), Tally(msg_ready), Tally(bb_ready)

                def turn(t, all_empty=False):
                    for k in range(2):
                        bank = on_act.take(pe, ta, all_empty)
                        for j in range(G):
                            last = pe.transpose(bank[:, j * P:(j + 1) * P], t[:, j, k * P:(k + 1) * P], s.ident[:, :])
                        on_act.filled(last, ta)

                def mix(t, w, all_empty=True):
                    for j in range(G):
                        if j % 2 == 0:
                            bank = on_act.take(pe, ta, all_empty)
                        for k in range(2):
                            o = j % 2 * C + k * P
                            last = pe.matmul(bank[:, o:o + P], t[:, k, j * P:(j + 1) * P], w[:, k, :], start=True, stop=True)
                        if j % 2:
                            on_act.filled(last, ta)

                def emptied(less=0):
                    v = ta.now(less)
                    if not isinstance(v, int) or v > 0:
                        pe.wait_ge(on_act.empty, v)

                def body(i):
                    for b in range(2):
                        wait(pe, xn_in.add())
                        turn(xn[b])
                    for b in range(2):
                        emptied(2)
                        mix(xt[b], w_up)
                        wait(pe, rad_in.add())
                        for j in range(G):
                            if j % 2 == 0:
                                bank = on_dve.take(pe, td)
                                hold(pe, passed[2])
                            last = pe.matmul(bank[:, j % 2 * C:j % 2 * C + C], rad[b][:, j * P:(j + 1) * P], m4[:, :], start=True, stop=True)
                            if j % 2:
                                on_dve.filled(last, td)
                    for b in range(2):
                        wait(pe, msg_in.add())
                        for j in range(G):
                            before = run[1 - b][:, G - 1, :] if j == 0 else run[b][:, j - 1, :]
                            bank = on_act.take(pe, ta)
                            pe.matmul(bank[:, 0:C], same[b][:, j, :], msg[b][:, j, :], start=True, stop=False)
                            emptied()
                            on_act.filled(pe.matmul(bank[:, 0:C], carry[b][:, j, :], before, start=False, stop=True), ta)
                    for b in range(2):
                        emptied()
                        turn(run[b], True)
                        emptied()
                        mix(xt[b], w_lin)
                    for b in range(2):
                        wait(pe, bb_in.add())
                        turn(bb[b])
                        emptied()
                        mix(xt[b], w_b)

                rounds(pe, EG // 2, body, ta, td, xn_in, rad_in, msg_in, bb_in)


def stage_node_sums(nc, d, s, psum):
    with Stage(nc, "ns") as m:
        rows, dd, xn = ([m.sb(f"{n}{b}", [P, G, C]) for b in range(2)] for n in ("rows", "dd", "xn"))
        xt = [m.sb("xt0", [P, 2, GR])] * 2
        w_sc = m.sb("w_sc", [P, 2, P])
        st, mv, sd = m.sb("st", [P, 2, G, 6]), m.sb("mv", [P, 2, G, 2]), m.sb("sd", [P, 2, G])
        w_in, rows_in, dd_in = m.sem("w_in"), m.sems("rows_in"), m.sems("dd_in")
        own, stats_ready, sd_ready, xn_ready = (m.sem(n) for n in ("own", "stats_ready", "sd_ready", "xn_ready"))
        passed = m.sems("passed", 3)
        on_act = m.banks("on_act", 0, 8, psum)
        with nc.Block() as block:
            @block.sync
            def _(sp):
                sp.dma_start(w_sc[:, :, :], d["w_sc"]).then_inc(w_in, 16)
                used, summed = Tally(xn_ready), Tally(on_act.full, 4)

                def body(i):
                    for b in range(2):
                        g = i * 2 + b
                        wait(sp, used, 1)
                        used.add()
                        sp.dma_start(rows[b][:, :, :], rows_of(d["X"], g * GR, G)).then_inc(rows_in[b], 16)
                        wait(sp, summed, 1)
                        summed.add()
                        sp.dma_start(dd[b][:, :, :], rows_of(d["D"], g * GR, G)).then_inc(dd_in[b], 16)

                rounds(sp, NG // 2, body, used, summed)

            @block.vector
            def _(dve):
                chain, deviation, loaded = Tally(own), Tally(sd_ready), [Tally(rows_in[b], 16) for b in range(2)]
                kept = Tally(on_act.empty)

                def body(i):
                    for b in range(2):
                        wait(dve, loaded[b].add())
                        ln_stats(dve, chain, passed[0], rows[b], st[:, b], mv[:, b], G, stats_ready)
                    for b in range(2):
                        ln_apply_planar(dve, chain, deviation, rows[b], mv[:, b], sd[:, b], xn[b], G, xn_ready)
                    for b in range(2):
                        g = i * 2 + b
                        wait(dve, kept.add(4))
                        hold(dve, passed[0])
                        for k in range(2):
                            dve.bn_stats(s.ost[:, k, bass.ds(g, 1), :].rearrange("p a n -> p (a n)"), s.o[:, k, bass.ds(g * GR, GR)])

                rounds(dve, NG // 2, body, chain, deviation, kept, *loaded)

            @block.scalar
            def _(act):
                stats, read = Tally(stats_ready), on_act.reader()

                def body(i):
                    for b in range(2):
                        ln_deviation(act, stats, mv[:, b], sd[:, b], s.eps, sd_ready)
                    for b in range(2):
                        for k in range(2):
                            bank = on_act.get(act, read)
                            act.activation(xt[b][:, k, :], bank[:, :], ACT.Copy).then_inc(on_act.empty, 1)
                        for k in range(2):
                            bank = on_act.get(act, read)
                            hold(act, passed[1])
                            act.activation(s.o[:, k, bass.ds((i * 2 + b) * GR, GR)], bank[:, :], ACT.Copy).then_inc(on_act.empty, 1)

                rounds(act, NG // 2, body, stats, read)

            @block.tensor
            def _(pe):
                pe.wait_ge(w_in, 16)
                ta, xn_in, dd_here = on_act.writer(), Tally(xn_ready), [Tally(dd_in[b], 16) for b in range(2)]

                def body(i):
                    for b in range(2):
                        wait(pe, xn_in.add())
                        for k in range(2):
                            bank = on_act.take(pe, ta)
                            for j in range(G):
                                last = pe.transpose(bank[:, j * P:(j + 1) * P], xn[b][:, j, k * P:(k + 1) * P], s.ident[:, :])
                            on_act.filled(last, ta)
                        wait(pe, dd_here[b].add())
                        pe.wait_ge(on_act.empty, ta.now())
                        for k in range(2):
                            bank = on_act.take(pe, ta, True)
                            pe.matmul(bank[:, :], w_sc[:, k, :], xt[b][:, k, :], start=True, stop=False)
                            for j in range(G):
                                last = pe.matmul(bank[:, j * P:(j + 1) * P], dd[b][:, j, k * P:(k + 1) * P], s.ident[:, :], start=False, stop=(j == G - 1))
                            on_act.filled(last, ta)

                rounds(pe, NG // 2, body, ta, xn_in, *dd_here)


def stage_norm_factors(nc, d, s, psum):
    with Stage(nc, "nf") as m:
        mv, sq, gam, beta, sel = m.sb("mv", [P, 2, 2]), m.sb("sq", [P, 2]), m.sb("gam", [P, 2]), m.sb("beta", [P, 1]), m.sb("sel", [P, 2, P])
        val = m.sb("val", [P, 2])
        c_in, own, sq_ready, nrm, val_ready, sd = (m.sem(n) for n in ("c_in", "own", "sq_ready", "nrm", "val_ready", "sd"))
        with nc.Block() as block:
            @block.sync
            def _(sp):
                for t, name in ((gam[:, :], "gamma"), (beta[:, :], "beta"), (sel[:, :, :], "same_channel")):
                    sp.dma_start(t, d[name]).then_inc(c_in, 16)

            @block.vector
            def _(dve):
                chain = Tally(own)

                def then(ins):
                    ins.then_inc(own, 1)
                    wait(dve, chain.add())

                dve.wait_ge(c_in, 48)
                g, n = N // GR, N % GR
                for k in range(2):
                    last = dve.bn_stats(s.ost[:, k, g, :], s.o[:, k, g * GR:g * GR + n])
                then(last)
                for k in range(2):
                    last = dve.bn_aggr(mv[:, k, :], s.ost[:, k, :, :].rearrange("p g n -> p (g n)"))
                then(last)
                then(dve.tensor_tensor(sq[:, :], mv[:, :, 0], mv[:, :, 0], ALU.mult))
                dve.tensor_tensor(sq[:, :], sq[:, :], mv[:, :, 1], ALU.add).then_inc(sq_ready, 1)
                dve.wait_ge(nrm, 1)
                then(dve.tensor_scalar(val[:, 0:1], psum[0][:, 0:1], 1.0 / 3.0, None, ALU.mult))
                then(dve.tensor_scalar(val[:, 1:2], psum[0][:, 0:1], 1.0 / 3.0, None, ALU.mult))
                dve.tensor_copy(val[0:H1, 0:1], mv[0:H1, 0, 1:2]).then_inc(val_ready, 1)
                dve.wait_ge(sd, 1)
                then(dve.reciprocal(val[:, :], val[:, :]))
                then(dve.tensor_tensor(s.factor[:, :], val[:, :], gam[:, :], ALU.mult))
                then(dve.memset(s.shift[:, :], 0.0))
                then(dve.tensor_tensor(sq[0:H1, 0:1], mv[0:H1, 0, 0:1], s.factor[0:H1, 0:1], ALU.mult))
                then(dve.tensor_tensor(s.shift[0:H1, 0:1], beta[0:H1, :], sq[0:H1, 0:1], ALU.subtract))

            @block.scalar
            def _(act):
                act.wait_ge(val_ready, 1)
                act.activation(val[:, :], val[:, :], ACT.Sqrt, bias=s.eps[:, 0:1]).then_inc(sd, 1)

            @block.tensor
            def _(pe):
                pe.wait_ge(c_in, 48)
                pe.wait_ge(sq_ready, 1)
                pe.matmul(psum[0][:, 0:1], sel[:, 0, :], sq[:, 0:1], start=True, stop=False)
                pe.matmul(psum[0][:, 0:1], sel[:, 1, :], sq[:, 1:2], start=False, stop=True).then_inc(nrm, 1)


def stage_node_update(nc, d, s, psum):
    with Stage(nc, "nu") as m:
        rows = [m.sb(f"rows{b}", [P, G, C]) for b in range(2)]
        xn = [m.sb(f"xn{b}", [P, G, C]) for b in range(2)]
        base = [m.sb("base0", [P, G, C])] * 2
        nt = [m.sb(f"nt{b}", [P, 2, GR]) for b in range(2)]
        wr = m.sb("wr", [P, C])
        junk = m.sb("junk", [P, C])
        wt = m.sb("wt", [P, 2, G])
        st, mv, sd = m.sb("st", [P, 2, G, 6]), m.sb("mv", [P, 2, G, 2]), m.sb("sd", [P, 2, G])
        w_in, rows_in, stored = m.sem("w_in"), m.sems("rows_in"), m.sems("stored")
        base_out = m.sem("base_out")
        own, stats_ready, sd_ready, xn_ready, base_ready, nt_ready = (m.sem(n) for n in ("own", "stats_ready", "sd_ready", "xn_ready", "base_ready", "nt_ready"))
        passed = m.sems("passed", 3)
        on_dve = m.banks("on_dve", 0, 4, psum)
        with nc.Block() as block:
            @block.sync
            def _(sp):
                sp.dma_start(wr[:, :], d["wr"]).then_inc(w_in, 16)
                xr, br = Tally(xn_ready), Tally(base_ready)

                def load(g, b):
                    sp.dma_start(rows[b][:, :, :], rows_of(d["X"], g * GR, G)).then_inc(rows_in[b], 16)

                for b in range(2):
                    load(b, b)

                def body(i):
                    for b in range(2):
                        wait(sp, xr.add())
                        sp.dma_start(rows_of(d["XN"], (i * 2 + b) * GR, G), xn[b][:, :, :]).then_inc(stored[b], 16)
                        wait(sp, br.add())
                        sp.dma_start(rows_of(d["out"], (i * 2 + b) * GR, G), base[b][:, :, :]).then_inc(base_out, 16)
                        load((i * 2 + b + 2), b)

                rounds(sp, NG // 2 - 1, body, xr, br)
                for b in range(2):
                    g = NG - 2 + b
                    wait(sp, xr.add())
                    sp.dma_start(rows_of(d["XN"], g * GR, G), xn[b][:, :, :]).then_inc(stored[b], 16)
                    wait(sp, br.add())
                    sp.dma_start(rows_of(d["out"], g * GR, G), base[b][:, :, :]).then_inc(base_out, 16)
                for b in range(2):
                    sp.wait_ge(stored[b], 16 * NG // 2)
                sp.wait_ge(base_out, 16 * NG)

            @block.scalar
            def _(act):
                stats, used = Tally(stats_ready), Tally(on_dve.full, 2)

                def body(i):
                    for b in range(2):
                        wait(act, used, 1)
                        used.add()
                        hold(act, passed[0])
                        for k in range(2):
                            last = act.activation(nt[b][:, k, :], s.o[:, k, bass.ds((i * 2 + b) * GR, GR)], ACT.Identity,
                                                  bias=s.shift[:, k:k + 1], scale=s.factor[:, k:k + 1])
                        last.then_inc(nt_ready, 1)
                    for b in range(2):
                        ln_deviation(act, stats, mv[:, b], sd[:, b], s.eps, sd_ready)

                rounds(act, NG // 2, body, stats, used)

            @block.tensor
            def _(pe):
                td, made = on_dve.writer(), Tally(nt_ready)

                def body(i):
                    for b in range(2):
                        wait(pe, made.add())
                        for j in range(G):
                            if j % 2 == 0:
                                bank = on_dve.take(pe, td)
                            for k in range(2):
                                o = j % 2 * C + k * P
                                last = pe.transpose(bank[:, o:o + P], nt[b][:, k, j * P:(j + 1) * P], s.ident[:, :])
                            if j % 2:
                                on_dve.filled(last, td)

                rounds(pe, NG // 2, body, td, made)

            @block.vector
            def _(dve):
                dve.wait_ge(w_in, 16)
                chain, deviation, read = Tally(own), Tally(sd_ready), on_dve.reader()
                loaded, old = [Tally(rows_in[b], 16) for b in range(2)], [Tally(stored[b], 16) for b in range(2)]
                base_gone, base_made = Tally(base_out, 16), Tally(base_ready)

                def body(i):
                    for b in range(2):
                        wait(dve, loaded[b].add())
                        for k in range(2):
                            bank = on_dve.get(dve, read)
                            n = bank[:, :].rearrange("p (j c) -> p j c", j=2)
                            for j in range(2):
                                r = rows[b][:, 2 * k + j, :]
                                dve.tensor_tensor(r[:, 0:H1], r[:, 0:H1], n[:, j, 0:H1], ALU.add)
                                last = dve.tensor_tensor(planar(r), planar(r), n[:, j, H1:C].rearrange("p (x c) -> p x c", x=3), ALU.add)
                            last.then_inc(on_dve.empty, 1)
                        dve.wait_ge(on_dve.empty, read.now())
                        ln_stats(dve, chain, passed[1], rows[b], st[:, b], mv[:, b], G, stats_ready)
                    for b in range(2):
                        wait(dve, old[b])
                        old[b].add()
                        hold(dve, passed[1])
                        ln_apply(dve, chain, deviation, rows[b], mv[:, b], sd[:, b], xn[b], G, xn_ready)
                        wait(dve, xr.add())
                        for j in range(G):
                            last = dve.scalar_tensor_tensor(junk[:, :], xn[b][:, j, :], 1.0, wr[:, :], ALU.mult, ALU.mult, accum_out=wt[:, b, j:j + 1])
                            then(last)
                        dve.tensor_copy(s.weight[:, bass.ds((i * 2 + b) * G, G)], wt[:, b, :]).then_inc(own, 1)
                        wait(dve, chain.add())
                        wait(dve, base_gone)
                        base_gone.add()
                        dve.tensor_tensor(base[b][:, :, :], rows[b][:, :, :], xn[b][:, :, :], ALU.add).then_inc(base_ready, 1)

                def then(ins):
                    ins.then_inc(own, 1)
                    wait(dve, chain.add())

                xr = Tally(xn_ready)
                rounds(dve, NG // 2, body, chain, deviation, read, xr, base_gone, *loaded, *old)


def stage_select(nc, d, s, psum):
    with Stage(nc, "se") as m:
        w, v, junk, gt, eq, tot, incl, pos = (m.sb(n, [P, NT]) for n in ("w", "v", "junk", "gt", "eq", "tot", "incl", "pos"))
        h16 = m.sb("h16", [P, NT], BF16)
        real, ones_row, tri32 = m.sb("real", [P, NT]), m.sb("ones_row", [P, NT]), m.sb("tri32", [P, P])
        tri, ones = m.sb("tri", [P, P], BF16), m.sb("ones", [P, P], BF16)
        ones32 = m.sb("ones32", [P, P])
        bits = m.sb("bits", [P, 31], I32)
        best, cand, ok = m.sb("best", [P, 1], I32), m.sb("cand", [P, 1], I32), m.sb("ok", [P, 1], I32)
        br, cnt, neg, sign, want, thr, room = (m.sb(n, [P, 1]) for n in ("br", "cnt", "neg", "sign", "want", "thr", "room"))
        absent = m.sb("absent", [P, NT])
        c_in, own, cnt_ready, total_ready, h_ready, counted, passed = (m.sem(n) for n in ("c_in", "own", "cnt_ready", "total_ready", "h_ready", "counted", "passed"))
        BITS = 31
        with nc.Block() as block:
            @block.sync
            def _(sp):
                for t, name in ((real[:, :], "real"), (tri32[:, :], "tri"), (bits[:, :], "bits"), (br[:, :], "br")):
                    sp.dma_start(t, d[name]).then_inc(c_in, 16)
                sp.dma_start(s.entry[:, :, 0], d["node_id"], allow_slow_non_contiguous=True).then_inc(c_in, 16)

            @block.vector
            def _(dve):
                chain, totals, counts = Tally(own), Tally(total_ready), Tally(cnt_ready)

                def then(ins):
                    ins.then_inc(own, 1)
                    wait(dve, chain.add())

                dve.memset(ones[:, :], 1.0)
                dve.memset(ones32[:, :], 1.0)
                dve.memset(ones_row[:, :], 1.0)
                then(dve.memset(best[:, :], 0))
                dve.wait_ge(c_in, 80)
                dve.tensor_copy(tri[:, :], tri32[:, :])
                then(dve.tensor_scalar(w[:, :], s.weight[:, :], br[:, 0:1], None, ALU.add))
                then(dve.tensor_copy(s.entry[:, :, 1].bitcast(F32), w[:, :]))
                then(dve.tensor_scalar(junk[:, :], w[:, :], 0.0, None, ALU.is_ge))
                then(dve.tensor_tensor(junk[:, :], junk[:, :], real[:, :], ALU.mult))
                dve.tensor_reduce(cnt[:, :], junk[:, :], AX.X, ALU.add).then_inc(cnt_ready, 1)
                wait(dve, totals.add())
                then(dve.tensor_scalar(neg[:, :], psum[0][:, 0:1], float(KEEP), None, ALU.is_lt))
                then(dve.tensor_scalar(sign[:, :], neg[:, :], -2.0, 1.0, ALU.mult, ALU.add))
                then(dve.tensor_scalar(want[:, :], neg[:, :], float(N - KEEP + 1 - KEEP), float(KEEP), ALU.mult, ALU.add))
                then(dve.tensor_scalar(absent[:, :], real[:, :], -1.0, FAR, ALU.add, ALU.mult))
                then(dve.tensor_scalar(v[:, :], w[:, :], sign[:, 0:1], None, ALU.mult))
                then(dve.tensor_tensor(v[:, :], v[:, :], real[:, :], ALU.mult))
                then(dve.tensor_tensor(v[:, :], v[:, :], absent[:, :], ALU.add))

                def body(i):
                    then(dve.tensor_tensor(cand[:, :], best[:, :], bits[:, bass.ds(i, 1)], ALU.bitwise_or))
                    dve.tensor_scalar(junk[:, :], v[:, :], cand[:, 0:1].bitcast(F32), None, ALU.is_ge, ALU.add, accum_out=cnt[:, :]).then_inc(cnt_ready, 1)
                    wait(dve, totals.add())
                    dve.tensor_scalar(ok[:, :], psum[0][:, 0:1], want[:, 0:1], None, ALU.is_ge).then_inc(own, 1)
                    wait(dve, chain.add())
                    hold(dve, passed)
                    then(dve.copy_predicated(best[:, :], ok[:, :], cand[:, :]))

                rounds(dve, BITS, body, chain, totals)
                then(dve.tensor_scalar(thr[:, :], best[:, :].bitcast(F32), sign[:, 0:1], None, ALU.mult))
                then(dve.tensor_scalar(gt[:, :], w[:, :], thr[:, 0:1], None, ALU.is_gt))
                then(dve.tensor_tensor(gt[:, :], gt[:, :], real[:, :], ALU.mult))
                dve.tensor_reduce(cnt[:, :], gt[:, :], AX.X, ALU.add).then_inc(cnt_ready, 1)
                then(dve.tensor_scalar(eq[:, :], w[:, :], thr[:, 0:1], None, ALU.is_equal))
                then(dve.tensor_tensor(eq[:, :], eq[:, :], real[:, :], ALU.mult))
                wait(dve, totals.add())
                then(dve.tensor_scalar(room[:, :], psum[0][:, 0:1], -1.0, float(KEEP), ALU.mult, ALU.add))

                def order(hot, n):
                    dve.tensor_copy(h16[:, :], hot[:, :]).then_inc(h_ready, 1)
                    dve.wait_ge(counted, n)
                    dve.tensor_copy(incl[:, :], psum[1][:, 0:NT])
                    then(dve.tensor_copy(tot[:, :], psum[2][:, 0:NT]))
                    then(dve.tensor_tensor_scan(pos[:, :], ones_row[:, :], tot[:, :], 0.0, ALU.mult, ALU.add))
                    then(dve.tensor_tensor(pos[:, :], pos[:, :], tot[:, :], ALU.subtract))
                    then(dve.tensor_tensor(pos[:, :], pos[:, :], incl[:, :], ALU.add))

                order(eq, 1)
                then(dve.tensor_scalar(pos[:, :], pos[:, :], room[:, 0:1], None, ALU.is_le))
                then(dve.tensor_tensor(eq[:, :], eq[:, :], pos[:, :], ALU.mult))
                then(dve.tensor_tensor(gt[:, :], gt[:, :], eq[:, :], ALU.add))
                order(gt, 2)
                then(dve.tensor_scalar(pos[:, :], pos[:, :], -1.0 - SKIP, None, ALU.add))
                then(dve.tensor_tensor(pos[:, :], pos[:, :], gt[:, :], ALU.mult))
                then(dve.tensor_scalar(s.slot[:, :], pos[:, :], float(SKIP), None, ALU.add))

            @block.tensor
            def _(pe):
                counts = Tally(cnt_ready)

                def total(i):
                    wait(pe, counts.add())
                    pe.matmul(psum[0][:, 0:1], ones32[:, :], cnt[:, :], start=True, stop=True).then_inc(total_ready, 1)

                total(0)
                rounds(pe, BITS, total, counts)
                total(0)
                for n in range(2):
                    pe.wait_ge(h_ready, n + 1)
                    pe.matmul(psum[1][:, 0:NT], tri[:, :], h16[:, :], start=True, stop=True)
                    pe.matmul(psum[2][:, 0:NT], ones[:, :], h16[:, :], start=True, stop=True).then_inc(counted, 1)


def stages(nc, d, s, psum):
    with nc.sbuf_tensor("scores", [HEADS, EP], F32) as s.scores:
        stage_edge_scores(nc, d, s, psum)
        stage_edge_softmax(nc, d, s, psum)
        stage_edge_sum(nc, d, s, psum)
    with nc.sbuf_tensor("slot", [P, NT], I32) as s.slot, nc.sbuf_tensor("entry", [P, NT, 2], I32) as s.entry:
        with nc.sbuf_tensor("logits", [P, NT, EXPERTS], F32) as s.logits:
            stage_router_logits(nc, d, s, psum)
            stage_router(nc, d, s, psum)
        stage_table(nc, d, s, "moe_table", EXPERTS * SLOTS, "mt")
    stage_ffn(nc, d, s, psum, True)
    with nc.sbuf_tensor("radial", [H1, EP], F32) as s.radial:
        stage_edge_mlp(nc, d, s, psum)
        stage_messages(nc, d, s, psum)
    with ExitStack() as kept:
        sb = lambda name, shape, dt=F32: kept.enter_context(nc.sbuf_tensor(name, shape, dt))
        s.weight, s.slot, s.entry = sb("weight", [P, NT]), sb("slot2", [P, NT], I32), sb("entry2", [P, NT, 2], I32)
        with nc.sbuf_tensor("o", [P, 2, NP], F32) as s.o, nc.sbuf_tensor("ost", [P, 2, NG, 6], F32) as s.ost, \
                nc.sbuf_tensor("factor", [P, 2], F32) as s.factor, nc.sbuf_tensor("shift", [P, 2], F32) as s.shift:
            stage_node_sums(nc, d, s, psum)
            stage_norm_factors(nc, d, s, psum)
            stage_node_update(nc, d, s, psum)
        stage_select(nc, d, s, psum)
        stage_table(nc, d, s, "mod_table", SB * FB, "dt")
    d["base"] = d["out"]
    stage_ffn(nc, d, s, psum, False)


def _layout_rest(np, v, a, f, pad, col, halves):
    spread = lambda z: np.broadcast_to(f(z).reshape(1, -1), (P, z.size))
    a["gate_w"] = halves(v["L0_ffn_gate_w"])
    a["gate_b"] = np.tile(spread(v["L0_ffn_gate_b"]), (1, G))
    a["expert_rank"] = np.broadcast_to(np.arange(EXPERTS, 0, -1, dtype=np.float32), (P, EXPERTS))
    a["slot_base"] = np.broadcast_to(np.arange(EXPERTS, dtype=np.float32) * SLOTS - 1, (P, EXPERTS))
    a["node_id"] = np.arange(NP, dtype=np.int32).reshape(NT, P).T
    a["real"] = (a["node_id"] < N).astype(np.float32)
    a["tri"] = np.triu(np.ones((P, P), np.float32))
    k = HID // P
    a["moe_w1"] = f(v["L0_ffn_w1"]).reshape(EXPERTS, 2, P, HID).transpose(0, 2, 1, 3).reshape(EXPERTS, P, -1)
    a["moe_w2"] = f(v["L0_ffn_w2"]).reshape(EXPERTS, k, P, C).transpose(0, 2, 1, 3).reshape(EXPERTS, P, -1)
    a["moe_b1"] = f(v["L0_ffn_b1"]).reshape(EXPERTS, k, P).transpose(0, 2, 1)
    a["moe_b2"] = np.broadcast_to(f(v["L0_ffn_b2"])[:, None], (EXPERTS, P, C))
    def blocks(w0, w1):
        z = np.zeros((P, 2, P), np.float32)
        w0, w1 = f(w0), f(w1)
        z[:H1, 0, :H1], z[H1:, 0, H1:], z[:H1, 1, :H1], z[H1:, 1, H1:] = w0, w1, w1, w1
        return z
    for name, w in (("w_up", "W_up"), ("w_lin", "W_lin"), ("w_sc", "Wsc"), ("w_b", "WB")):
        a[name] = blocks(v[f"L1_gnn_{w}0"], v[f"L1_gnn_{w}1"])
    for n in ("M1", "M2", "M3", "M4"):
        a[n] = f(v[f"L1_gnn_{n}"])
    a["wc"] = np.broadcast_to(np.concatenate([f(v["L1_gnn_Wc0"]).T, f(v["L1_gnn_Wc1"]).T])[None], (P, 9, H1))
    a["rbf"] = pad(f(v["edge_attr_16"]), EP).T
    a["sh"] = pad(f(v["edge_attr_4"]), EP)
    g0, g1 = f(v["L1_gnn_gamma0"]), f(v["L1_gnn_gamma1"])
    a["gamma"] = np.stack([np.concatenate([g0, g1]), np.concatenate([g1, g1])], 1)
    a["beta"] = np.concatenate([f(v["L1_gnn_beta0"]), np.zeros(H1, np.float32)])[:, None]
    p, q = np.arange(P)[:, None], np.arange(P)[None]
    same = (p % H1 == q % H1)
    a["same_channel"] = np.stack([same & (p >= H1), same], 1).astype(np.float32)
    a["wr"] = spread(v["L1_ffn_wr"])
    a["bits"] = np.broadcast_to((1 << np.arange(30, -1, -1)).astype(np.int32), (P, 31))
    a["br"] = np.broadcast_to(f(v["L1_ffn_br"]).reshape(1, 1), (P, 1))
    a["mod_w1"] = halves(v["L1_ffn_w1"]).reshape(P, -1)
    a["mod_w2"] = f(v["L1_ffn_w2"]).reshape(k, P, C).transpose(1, 0, 2).reshape(P, -1)
    a["mod_b1"] = f(v["L1_ffn_b1"]).reshape(k, P).T
    a["mod_b2"] = spread(v["L1_ffn_b2"])


class Kept:
    pass


def build(nc, d):
    s = Kept()
    with ExitStack() as ctx:
        def sb(name, shape, dt=F32):
            return ctx.enter_context(nc.sbuf_tensor(name, shape, dt))

        psum = [ctx.enter_context(nc.psum_tensor(f"bank{k}", [P, 512], F32)) for k in range(8)]
        s.ident = sb("ident", [P, P])
        s.eps = sb("eps", [P, 1])
        s.last_row = sb("last_row", [P, 1])
        s.dst_col = sb("dst_col", [P, 1 + ET])
        s.dst_row_id = sb("dst_row_id", [P, ET], I32)
        s.end_row = sb("end_row", [P, ET], I32)
        set_up = ctx.enter_context(nc.semaphore("set_up"))
        with nc.Block() as block:
            @block.sync
            def _(sp):
                sp.dma_start(s.last_row[:, :], d["last_row"]).then_inc(set_up, 16)
                sp.wait_ge(set_up, 16)

            @block.vector
            def _(dve):
                dve.memset(s.eps[:, :], EPS)
        stages(nc, d, s, psum)


def _layout(np, v):
    f = lambda a: np.ascontiguousarray(np.asarray(a))
    pad = lambda a, n, c=0: np.concatenate([f(a), np.full((n - len(a),) + a.shape[1:], c, a.dtype)])
    a = {}
    a["x"] = pad(f(v["x"]), NP)
    src = pad(f(v["src"]).astype(np.int32), EP, NP - 1)
    dst = pad(f(v["dst"]).astype(np.int32), EP, NP - 1)
    col = lambda z: z.reshape(-1, P).T
    both = np.stack([src.reshape(EG, G, P), dst.reshape(EG, G, P)], 1)
    a["edge_idx"] = both.reshape(EG, 2 * G, P).transpose(2, 0, 1)
    a["src_col"] = col(src)
    a["dst_col"] = np.concatenate([np.full((P, 1), -1, np.int32), col(dst)], 1)
    a["dst_next"] = col(np.concatenate([dst[1:], np.full(1, -1, np.int32)]))
    a["dst_row"] = dst[None]
    a["ident"] = np.eye(P, dtype=np.float32)
    a["last_row"] = (np.arange(P) == P - 1).astype(np.float32)[:, None]
    halves = lambda w: f(w).reshape(2, P, -1).transpose(1, 0, 2)
    a["gat_w"] = halves(f(v["L0_gnn_W"]).transpose(1, 0, 2).reshape(C, C))
    a["gat_a"] = np.broadcast_to(np.stack([f(v["L0_gnn_a_src"]).reshape(C), f(v["L0_gnn_a_dst"]).reshape(C)])[None], (P, 2, C))
    _layout_rest(np, v, a, f, pad, col, halves)
    return {k: np.ascontiguousarray(z) for k, z in a.items()}


SCRATCH = {"X": (NP, C), "XN": (NP, C), "H": (EP, C), "D": (NP, C)}
TABLES = {"moe_table": (EXPERTS * SLOTS, 2), "mod_table": (SB * FB, 2)}


def kernel(**inputs):
    import numpy as np
    import concourse.bacc as bacc
    from concourse import mybir as mb
    from concourse.bass_utils import run_bass_kernel_spmd

    nc = bacc.Bacc("TRN2", target_bir_lowering=False, num_devices=1)
    arrays = _layout(np, inputs)
    d = {k: nc.dram_tensor(f"in_{k}", z.shape, mb.dt.from_np(z.dtype), kind="ExternalInput").ap()
         for k, z in arrays.items()}
    for k, shape in SCRATCH.items():
        d[k] = nc.dram_tensor(f"scratch_{k}", shape, F32, kind="Internal").ap()
    for k, shape in TABLES.items():
        d[k] = nc.dram_tensor(f"scratch_{k}", shape, I32, kind="Internal").ap()
    d["out"] = nc.dram_tensor("out", (NP, C), F32, kind="ExternalOutput").ap()
    d["dst_rows"] = d["dst_row"].to_broadcast([P, EP])
    build(nc, d)
    r = run_bass_kernel_spmd(nc, [{f"in_{k}": z for k, z in arrays.items()}], core_ids=[0])
    return r.results[0]["out"][:N]
```

```python
from contextlib import ExitStack

import concourse.bass as bass
from concourse import mybir

F32 = mybir.dt.float32
BF16 = mybir.dt.bfloat16
I32 = mybir.dt.int32
U32 = mybir.dt.uint32
ALU = mybir.AluOpType
ACT = mybir.ActivationFunctionType
AX = mybir.AxisListType

P = 128
N = 20000
C = 256
E = 10000
EPS = 1e-5
G = 4
NG = 40
NT = NG * G
NP = NT * P
EG = 20
ET = EG * G
EP = ET * P
GR = G * P
HEADS = 4
EXPERTS = 8
HID = 1024
CAP = 3125
FT = 5
FB = FT * P
XB = 5
SLOTS = XB * FB
KEEP = 9999
SB = 16
SKIP = 1 << 20
FAR = 3.0e38
GAT_IN = HEADS + C


class Tally:

    def __init__(self, sem, step=1):
        self.sem, self.step = sem, step
        self.base, self.i, self.per, self.n = 0, 0, 0, 0

    def add(self, k=1):
        self.n += k * self.step
        return self

    def skip(self, k=1):
        self.n += k * self.step
        self.base -= k * self.step

    def now(self, less=0):
        v = self.n + self.base - less * self.step
        return v if isinstance(self.i, int) else self.i * self.per + v


def wait(eng, tally, less=0):
    v = tally.now(less)
    if not isinstance(v, int) or v > 0:
        eng.wait_ge(tally.sem, v)


def rounds(eng, n, body, *tallies, lead=1):
    for t in tallies:
        t.base, t.n, t.per = t.base + t.n, 0, 0
    for r in range(lead):
        for t in tallies:
            t.base += t.per
        body(r)
        for t in tallies:
            assert r == 0 or t.n == t.per, (t.n, t.per)
            t.per, t.n = t.n, 0
    with eng.Fori(lead, n) as i:
        for t in tallies:
            t.base -= (lead - 1) * t.per
            t.i = i
        body(i)
        for t in tallies:
            assert t.n == t.per, (t.n, t.per)
    for t in tallies:
        t.base, t.i, t.per, t.n = t.base + n * t.per, 0, 0, 0


class Banks:

    def __init__(self, banks, full, empty):
        self.banks, self.full, self.empty = banks, full, empty

    def writer(self):
        return Tally(self.full)

    def reader(self):
        return Tally(self.full)

    def take(self, pe, t, all_empty=False):
        k = len(self.banks)
        v = t.now() - k + 1
        if not all_empty and (not isinstance(v, int) or v > 0):
            pe.wait_ge(self.empty, v)
        return self.banks[t.n // t.step % k]

    def filled(self, ins, t):
        ins.then_inc(self.full, 1)
        t.add()

    def get(self, eng, t):
        bank = self.banks[t.n // t.step % len(self.banks)]
        t.add()
        eng.wait_ge(self.full, t.now())
        return bank


class Stage:

    def __init__(self, nc, tag):
        self.nc, self.tag, self.ctx, self.used = nc, tag, ExitStack(), []

    def __enter__(self):
        self.ctx.__enter__()
        return self

    def __exit__(self, *e):
        if e[0] is None:
            self.nc.clear_and_free_semaphores(self.used)
            self.nc.all_engine_barrier()
        return self.ctx.__exit__(*e)

    def sb(self, name, shape, dt=F32):
        return self.ctx.enter_context(self.nc.sbuf_tensor(f"{self.tag}_{name}", shape, dt))

    def sem(self, name):
        self.used.append(self.nc.alloc_semaphore(name=f"{self.tag}_{name}"))
        return self.used[-1]

    def sems(self, name, n=2):
        return [self.sem(f"{name}{k}") for k in range(n)]

    def banks(self, name, first, n, psum):
        return Banks([psum[k] for k in range(first, first + n)], self.sem(f"{name}_full"), self.sem(f"{name}_empty"))


def hold(eng, passed):
    eng.sem_inc(passed, 1)


def ln_stats(dve, own, passed, rows, st, mv, tiles, ready):
    for j in range(tiles):
        last = dve.bn_stats(st[:, j, :], rows[:, j, :])
    last.then_inc(own.sem, 1)
    wait(dve, own.add())
    hold(dve, passed)
    for j in range(tiles):
        last = dve.bn_aggr(mv[:, j, :], st[:, j, :])
    last.then_inc(ready, 1)


def ln_deviation(act, stats, mv, sd, eps, done):
    wait(act, stats.add())
    act.activation(sd[:, :], mv[:, :, 1], ACT.Sqrt, bias=eps[:, 0:1]).then_inc(done, 1)


def ln_apply(dve, own, deviation, rows, mv, sd, out, tiles, ready):
    wait(dve, deviation.add())
    dve.reciprocal(sd[:, :], sd[:, :]).then_inc(own.sem, 1)
    wait(dve, own.add())
    for j in range(tiles):
        last = dve.tensor_scalar(out[:, j, :], rows[:, j, :], mv[:, j, 0:1], sd[:, j:j + 1],
                                 ALU.subtract, ALU.mult)
    last.then_inc(ready, 1)


def rows_of(dram, start, tiles):
    return dram[bass.ds(start, tiles * P), :].rearrange("(j p) c -> p j c", p=P)


def stage_edge_scores(nc, d, s, psum):
    with Stage(nc, "es") as m:
        idx = m.sb("idx", [P, EG, 2 * G], I32)
        cur = m.sb("cur", [P, 2, 2 * G], I32)
        rows = [m.sb(f"rows{b}", [P, 2 * G, C]) for b in range(2)]
        xn = [m.sb(f"xn{b}", [P, 2 * G, C]) for b in range(2)]
        xt = [m.sb(f"xt{b}", [P, 2, 2, GR]) for b in range(2)]
        h = [m.sb(f"h{b}", [P, G, GAT_IN]) for b in range(2)]
        w = m.sb("w", [P, 2, GAT_IN])
        wd = m.sb("wd", [P, 2, HEADS])
        av = m.sb("av", [P, 2, C])
        prod = m.sb("prod", [P, 2, C])
        st = m.sb("st", [P, 2, 2 * G, 6])
        mv = m.sb("mv", [P, 2, 2 * G, 2])
        sd = m.sb("sd", [P, 2, 2 * G])
        table = m.sb("table", [P, EXPERTS * SLOTS // P, 2], I32)
        idx_in, w_in, filled, zeroed = m.sem("idx_in"), m.sem("w_in"), m.sem("filled"), m.sem("zeroed")
        cur_ready, gathered, xn_ready = m.sem("cur_ready"), m.sems("gathered"), m.sem("xn_ready")
        stats_ready, sd_ready, own = m.sem("stats_ready"), m.sem("sd_ready"), m.sem("own")
        w_ready = m.sem("w_ready")
        h_stored, passed = m.sems("h_stored"), m.sems("passed", 3)
        GB = 4 + 1
        on_act = m.banks("on_act", 0, GB, psum)
        for_h = m.banks("for_h", GB, 2, psum)
        with nc.Block() as block:
            @block.sync
            def _(sp):
                sp.dma_start(idx[:, :, :], d["edge_idx"]).then_inc(idx_in, 16)
                sp.dma_start(w[:, :, 0:C], d["gat_w"]).then_inc(w_in, 16)
                sp.dma_start(av[:, :, :], d["gat_a"]).then_inc(w_in, 16)
                sp.dma_start(s.ident[:, :], d["ident"]).then_inc(w_in, 16)
                sp.wait_ge(zeroed, 2)
                sp.dma_start(d["moe_table"].rearrange("(p t) w -> p t w", p=P), table[:, :, :]).then_inc(filled, 16)
                sp.dma_start(d["mod_table"].rearrange("(p t) w -> p t w", p=P),
                             table[:, 0:SB * FB // P, :]).then_inc(filled, 16)
                ready = Tally(for_h.empty, G)

                def body(i):
                    part = bass.ds(i * (NP // (EG // 2)), NP // (EG // 2))
                    sp.dma_start(d["X"][part, :].rearrange("(p t) c -> p t c", p=P),
                                 d["x"][part, :].rearrange("(p t) c -> p t c", p=P)).then_inc(filled, 16)
                    for b in range(2):
                        wait(sp, ready.add())
                        sp.dma_start(rows_of(d["H"], (i * 2 + b) * GR, G), h[b][:, :, 0:C]).then_inc(h_stored[b], 16)

                rounds(sp, EG // 2, body, ready)
                sp.wait_ge(filled, 16 * (EG // 2 + 2))
                for b in range(2):
                    sp.wait_ge(h_stored[b], 16 * EG // 2)

            @block.gpsimd
            def _(pool):
                pool.memset(table[:, :, 0:1], SKIP).then_inc(zeroed, 1)
                pool.memset(table[:, :, 1:2], 0).then_inc(zeroed, 1)
                pool.wait_ge(idx_in, 16)
                loaded = [Tally(gathered[b], 16) for b in range(2)]
                taken, used = Tally(cur_ready), Tally(xn_ready)

                def body(i):
                    for b in range(2):
                        wait(pool, loaded[b])
                        hold(pool, passed[0])
                        pool.tensor_copy(cur[:, b, :], idx[:, bass.ds(i * 2 + b, 1), :].rearrange("p a j -> p (a j)")).then_inc(cur_ready, 1)
                        wait(pool, taken.add())
                        wait(pool, used, 1)
                        used.add()
                        hold(pool, passed[0])
                        for j in range(2 * G):
                            pool.indirect_dma_start(
                                out=rows[b][:, j, :], out_offset=None, in_=d["x"],
                                in_offset=bass.IndirectOffsetOnAxis(ap=cur[:, b, j:j + 1], axis=0),
                                bounds_check=NP - 1, oob_is_err=False).then_inc(gathered[b], 16)
                            loaded[b].add()

                rounds(pool, EG // 2, body, *loaded, taken, used)

            @block.vector
            def _(dve):
                chain = Tally(own)
                dve.wait_ge(w_in, 48)
                for k in range(2):
                    for end, out in ((0, w[:, k, C:GAT_IN]), (1, wd[:, k, :])):
                        dve.tensor_tensor(prod[:, end, :], w[:, k, 0:C], av[:, end, :], ALU.mult).then_inc(own, 1)
                        wait(dve, chain.add())
                        dve.tensor_reduce(out, prod[:, end, :].rearrange("p (h o) -> p h o", h=HEADS), AX.X, ALU.add).then_inc(w_ready, 1)
                loaded = [Tally(gathered[b], 16) for b in range(2)]
                deviation, turned = Tally(sd_ready), Tally(on_act.full)

                def body(i):
                    for b in range(2):
                        wait(dve, loaded[b].add(2 * G))
                        ln_stats(dve, chain, passed[1], rows[b], st[:, b], mv[:, b], 2 * G, stats_ready)
                        wait(dve, turned, (2 - b) * GB - 4)
                        hold(dve, passed[1])
                        ln_apply(dve, chain, deviation, rows[b], mv[:, b], sd[:, b], xn[b], 2 * G, xn_ready)
                    turned.add(2 * GB)

                rounds(dve, EG // 2, body, *loaded, chain, deviation, turned)

            @block.scalar
            def _(act):
                stats, read, read_h, stored = Tally(stats_ready), on_act.reader(), for_h.reader(), [Tally(h_stored[b], 16) for b in range(2)]

                def body(i):
                    ln_deviation(act, stats, mv[:, 0], sd[:, 0], s.eps, sd_ready)
                    if isinstance(i, int):
                        read.skip(GB)
                        read_h.skip(G)
                        stored[1].skip()
                    else:
                        empty(i - 1, 1)
                    ln_deviation(act, stats, mv[:, 1], sd[:, 1], s.eps, sd_ready)
                    empty(i, 0)

                def empty(i, b):
                    for end in range(2):
                        for k in range(2):
                            bank = on_act.get(act, read)
                            act.activation(xt[b][:, end, k, :], bank[:, :], ACT.Copy).then_inc(on_act.empty, 1)
                    wait(act, stored[b])
                    hold(act, passed[2])
                    stored[b].add()
                    for j in range(G):
                        bank = for_h.get(act, read_h)
                        act.activation(h[b][:, j, :], bank[:, 0:GAT_IN], ACT.Copy).then_inc(for_h.empty, 1)
                    bank = on_act.get(act, read)
                    hold(act, passed[2])
                    act.activation(s.scores[:, bass.ds((i * 2 + b) * GR, GR)], bank[0:HEADS, :], ACT.Copy).then_inc(on_act.empty, 1)

                rounds(act, EG // 2, body, stats, read, read_h, *stored)
                empty(EG // 2 - 1, 1)

            @block.tensor
            def _(pe):
                pe.wait_ge(w_in, 48)
                pe.wait_ge(w_ready, 4)
                xn_in, ta, th = Tally(xn_ready), on_act.writer(), for_h.writer()

                def transposes(b):
                    wait(pe, xn_in.add())
                    for end in range(2):
                        for k in range(2):
                            bank = on_act.take(pe, ta)
                            for j in range(G):
                                last = pe.transpose(bank[:, j * P:(j + 1) * P], xn[b][:, end * G + j, k * P:(k + 1) * P], s.ident[:, :])
                            on_act.filled(last, ta)
                    pe.wait_ge(on_act.empty, ta.now())

                def products(b):
                    for j in range(G):
                        e = slice(j * P, (j + 1) * P)
                        bank = for_h.take(pe, th)
                        pe.matmul(bank[:, 0:GAT_IN], xt[b][:, 0, 0, e], w[:, 0, :], start=True, stop=False)
                        pe.matmul(bank[:, 0:GAT_IN], xt[b][:, 0, 1, e], w[:, 1, :], start=False, stop=False)
                        pe.matmul(bank[:, C:GAT_IN], xt[b][:, 1, 0, e], wd[:, 0, :], start=False, stop=False)
                        last = pe.matmul(bank[:, C:GAT_IN], xt[b][:, 1, 1, e], wd[:, 1, :], start=False, stop=True)
                        for_h.filled(last, th)

                def scores(b):
                    pe.wait_ge(for_h.empty, th.now())
                    bank = on_act.take(pe, ta)
                    for j in range(G):
                        last = pe.transpose(bank[0:HEADS, j * P:(j + 1) * P], h[b][:, j, C:GAT_IN], s.ident[:, :])
                    on_act.filled(last, ta)

                def body(i):
                    for b in range(2):
                        transposes(b)
                        products(b)
                        scores(b)

                rounds(pe, EG // 2, body, xn_in, ta, th)


def stage_edge_softmax(nc, d, s, psum):
    with Stage(nc, "sm") as m:
        ids = m.sb("ids", [HEADS, EP], I32)
        cut = m.sb("cut", [HEADS, EP + 1])
        top = m.sb("top", [HEADS, EP])
        nxt = m.sb("nxt", [P, ET], I32)
        col = m.sb("col", [P, 1 + ET], I32)
        more = m.sb("more", [P, ET])
        ids_in, own, ready, exps = m.sem("ids_in"), m.sem("own"), m.sem("ready"), m.sem("exps")
        with nc.Block() as block:
            @block.sync
            def _(sp):
                sp.dma_start(ids[:, :], d["dst_rows"][0:HEADS, :]).then_inc(ids_in, 16)
                sp.dma_start(col[:, :], d["dst_col"]).then_inc(ids_in, 16)
                sp.dma_start(nxt[:, :], d["dst_next"]).then_inc(ids_in, 16)
                sp.dma_start(s.dst_row_id[:, :], d["dst_col"][:, 1:1 + ET]).then_inc(ids_in, 16)

            @block.vector
            def _(dve):
                chain = Tally(own)

                def then(ins):
                    ins.then_inc(own, 1)
                    wait(dve, chain.add())

                dve.wait_ge(ids_in, 64)
                then(dve.tensor_copy(s.dst_col[:, :], col[:, :]))
                then(dve.tensor_copy(more[:, :], nxt[:, :]))
                then(dve.tensor_tensor(more[:, :], s.dst_col[:, 1:1 + ET], more[:, :], ALU.is_equal))
                then(dve.scalar_tensor_tensor(s.end_row[:, :], more[:, :], float(SKIP), s.dst_col[:, 1:1 + ET], ALU.mult, ALU.add))
                then(dve.memset(cut[:, 0:1], -FAR))
                then(dve.memset(cut[:, EP:EP + 1], -FAR))
                then(dve.tensor_tensor(cut[:, 1:EP], ids[:, 1:EP], ids[:, 0:EP - 1], ALU.not_equal))
                then(dve.tensor_scalar(cut[:, 1:EP], cut[:, 1:EP], -FAR, None, ALU.mult))
                then(dve.scalar_tensor_tensor(s.scores[:, :], s.scores[:, :], 0.2, s.scores[:, :], ALU.mult, ALU.max))
                then(dve.tensor_tensor_scan(top[:, :], cut[:, 0:EP], s.scores[:, :], 0.0, ALU.add, ALU.max))
                then(dve.tensor_tensor_scan(top[:, ::-1], cut[:, EP:0:-1], top[:, ::-1], 0.0, ALU.add, ALU.max))
                dve.tensor_tensor(s.scores[:, :], s.scores[:, :], top[:, :], ALU.subtract).then_inc(ready, 1)

            @block.scalar
            def _(act):
                act.wait_ge(ready, 1)
                act.activation(s.scores[:, :], s.scores[:, :], ACT.Exp).then_inc(exps, 1)


def run_masks(dve, s, t, same, carry, row):
    for j in range(G):
        dve.tensor_scalar(same[:, j, :], row[:, j * P:(j + 1) * P], s.dst_col[:, bass.ds(t + 1 + j, 1)], None, ALU.is_equal)
        last = dve.tensor_scalar(carry[:, j, :], row[:, j * P:(j + 1) * P], s.dst_col[:, bass.ds(t + j, 1)],
                                 s.last_row[:, 0:1], ALU.is_equal, ALU.mult)
    return last


def stage_edge_sum(nc, d, s, psum):
    WD = GAT_IN
    with Stage(nc, "gs") as m:
        hin = [m.sb(f"hin{b}", [P, G, C]) for b in range(2)]
        row = [m.sb(f"row{b}", [P, GR], I32) for b in range(2)]
        xd = [m.sb(f"xd{b}", [P, G, C]) for b in range(2)]
        msg = [m.sb(f"msg{b}", [P, G, WD]) for b in range(2)]
        exs = [m.sb(f"exs{b}", [HEADS, GR]) for b in range(2)]
        same = [m.sb(f"same{b}", [P, G, P]) for b in range(2)]
        carry = [m.sb(f"carry{b}", [P, G, P]) for b in range(2)]
        run = [m.sb(f"run{b}", [P, G, WD]) for b in range(2)]
        rec = m.sb("rec", [P, 2, G, HEADS])
        agg = [m.sb(f"agg{b}", [P, G, C]) for b in range(2)]
        cur = m.sb("cur", [P, 2, 2 * G], I32)
        h_in, xd_in, stored = m.sems("h_in"), m.sems("xd_in"), m.sems("stored")
        cur_ready, exs_ready, own, msg_ready = m.sem("cur_ready"), m.sem("exs_ready"), m.sem("own"), m.sem("msg_ready")
        agg_ready, start, passed = m.sem("agg_ready"), m.sem("start"), m.sems("passed", 4)
        on_act = m.banks("on_act", 0, 4, psum)
        on_dve = m.banks("on_dve", 4, 2, psum)
        with nc.Block() as block:
            @block.sync
            def _(sp):
                made = Tally(msg_ready)

                def body(i):
                    for b in range(2):
                        wait(sp, made, 1)
                        made.add()
                        g = i * 2 + b
                        sp.dma_start(hin[b][:, :, :], rows_of(d["H"], g * GR, G)).then_inc(h_in[b], 16)
                        sp.dma_start(row[b][:, :], d["dst_rows"][:, bass.ds(g * GR, GR)]).then_inc(h_in[b], 16)

                rounds(sp, EG // 2, body, made)

            @block.gpsimd
            def _(pool):
                pool.memset(run[1][:, G - 1, :], 0.0).then_inc(start, 1)
                ready, summed = Tally(cur_ready), Tally(agg_ready)
                old = [Tally(stored[b], 16) for b in range(2)]

                def body(i):
                    for b in range(2):
                        g = i * 2 + b
                        wait(pool, old[b])
                        hold(pool, passed[0])
                        pool.tensor_copy(cur[:, b, 0:G], s.dst_row_id[:, bass.ds(g * G, G)])
                        pool.tensor_copy(cur[:, b, G:2 * G], s.end_row[:, bass.ds(g * G, G)]).then_inc(cur_ready, 1)
                        wait(pool, ready.add())
                        hold(pool, passed[0])
                        for j in range(G):
                            pool.indirect_dma_start(
                                out=xd[b][:, j, :], out_offset=None, in_=d["x"],
                                in_offset=bass.IndirectOffsetOnAxis(ap=cur[:, b, j:j + 1], axis=0),
                                bounds_check=NP - 1, oob_is_err=False).then_inc(xd_in[b], 16)
                    for b in range(2):
                        wait(pool, summed.add())
                        hold(pool, passed[0])
                        for j in range(G):
                            pool.indirect_dma_start(
                                out=d["X"], out_offset=bass.IndirectOffsetOnAxis(ap=cur[:, b, G + j:G + j + 1], axis=0),
                                in_=agg[b][:, j, :], in_offset=None,
                                bounds_check=NP - 1, oob_is_err=False).then_inc(stored[b], 16)
                            old[b].add()

                rounds(pool, EG // 2, body, ready, summed, *old)
                for b in range(2):
                    pool.wait_ge(stored[b], 16 * G * EG // 2)

            @block.scalar
            def _(act):
                read, exin, used = on_act.reader(), Tally(on_dve.full), Tally(agg_ready)

                def body(i):
                    for b in range(2):
                        wait(act, exin, 1)
                        exin.add()
                        hold(act, passed[3])
                        act.activation(exs[b][:, :], s.scores[:, bass.ds((i * 2 + b) * GR, GR)], ACT.Copy).then_inc(exs_ready, 1)
                    for b in range(2):
                        wait(act, used, 1)
                        used.add()
                        for j in range(G):
                            bank = on_act.get(act, read)
                            act.activation(run[b][:, j, :], bank[:, 0:WD], ACT.Copy).then_inc(on_act.empty, 1)

                rounds(act, EG // 2, body, read, exin, used)

            @block.vector
            def _(dve):
                chain, read = Tally(own), on_dve.reader()
                h_here = [Tally(h_in[b], 16) for b in range(2)]
                x_here = [Tally(xd_in[b], 16) for b in range(2)]
                old = [Tally(stored[b], 16) for b in range(2)]
                sums = Tally(on_act.empty, G)

                def body(i):
                    for b in range(2):
                        t = (i * 2 + b) * G
                        wait(dve, h_here[b].add(2))
                        bank = on_dve.get(dve, read)
                        dve.tensor_copy(msg[b][:, :, C:WD], bank[:, 0:G * HEADS].rearrange("p (j h) -> p j h", h=HEADS)).then_inc(on_dve.empty, 1)
                        dve.wait_ge(on_dve.empty, read.now())
                        for j in range(G):
                            ex = msg[b][:, j, C:WD].rearrange("p (h o) -> p h o", o=1).to_broadcast([P, HEADS, C // HEADS])
                            dve.tensor_tensor(msg[b][:, j, 0:C].rearrange("p (h o) -> p h o", h=HEADS),
                                              hin[b][:, j, :].rearrange("p (h o) -> p h o", h=HEADS), ex, ALU.mult)
                        run_masks(dve, s, t, same[b], carry[b], row[b]).then_inc(msg_ready, 1)
                    for b in range(2):
                        wait(dve, sums.add())
                        hold(dve, passed[2])
                        dve.tensor_scalar(rec[:, b], run[b][:, :, C:WD], 1e-9, None, ALU.max).then_inc(own, 1)
                        wait(dve, chain.add())
                        dve.reciprocal(rec[:, b], rec[:, b]).then_inc(own, 1)
                        wait(dve, chain.add())
                        wait(dve, old[b])
                        old[b].add(G)
                        hold(dve, passed[2])
                        for j in range(G):
                            r = rec[:, b, j, :].rearrange("p (h o) -> p h o", o=1).to_broadcast([P, HEADS, C // HEADS])
                            last = dve.tensor_tensor(agg[b][:, j, :].rearrange("p (h o) -> p h o", h=HEADS),
                                                     run[b][:, j, 0:C].rearrange("p (h o) -> p h o", h=HEADS), r, ALU.mult)
                        last.then_inc(own, 1)
                        wait(dve, chain.add())
                        wait(dve, x_here[b].add(G))
                        dve.scalar_tensor_tensor(agg[b][:, :, :], agg[b][:, :, :], 0.0, xd[b][:, :, :], ALU.max, ALU.add).then_inc(agg_ready, 1)

                rounds(dve, EG // 2, body, chain, read, *h_here, *x_here, *old, sums)

            @block.tensor
            def _(pe):
                pe.wait_ge(start, 1)
                ta, td, ex_in, made = on_act.writer(), on_dve.writer(), Tally(exs_ready), Tally(msg_ready)

                def body(i):
                    for b in range(2):
                        wait(pe, ex_in.add())
                        bank = on_dve.take(pe, td)
                        hold(pe, passed[1])
                        for j in range(G):
                            last = pe.transpose(bank[:, j * HEADS:(j + 1) * HEADS], exs[b][:, j * P:(j + 1) * P], s.ident[0:HEADS, 0:HEADS])
                        on_dve.filled(last, td)
                    for b in range(2):
                        wait(pe, made.add())
                        for j in range(G):
                            before = run[1 - b][:, G - 1, :] if j == 0 else run[b][:, j - 1, :]
                            bank = on_act.take(pe, ta)
                            pe.matmul(bank[:, 0:WD], same[b][:, j, :], msg[b][:, j, :], start=True, stop=False)
                            v = ta.now()
                            if not isinstance(v, int) or v > 0:
                                pe.wait_ge(on_act.empty, v)
                            last = pe.matmul(bank[:, 0:WD], carry[b][:, j, :], before, start=False, stop=True)
                            on_act.filled(last, ta)

                rounds(pe, EG // 2, body, ta, td, ex_in, made)


def over(ap, n):
    return ap.unsqueeze(1).to_broadcast([ap.shape[0], n, ap.shape[1]])


def each(ap, n):
    return ap.unsqueeze(2).to_broadcast([ap.shape[0], ap.shape[1], n])


def stage_router_logits(nc, d, s, psum):
    B = 4
    with Stage(nc, "rl") as m:
        rows = [m.sb(f"rows{b}", [P, G, C]) for b in range(B)]
        xn = [m.sb(f"xn{b}", [P, G, C]) for b in range(B)]
        xt = [m.sb(f"xt{b}", [P, 2, GR]) for b in range(B)]
        gate = m.sb("gate", [P, 2, EXPERTS])
        st, mv, sd = m.sb("st", [P, B, G, 6]), m.sb("mv", [P, B, G, 2]), m.sb("sd", [P, B, G])
        rows_in, w_in, own = m.sems("rows_in", B), m.sem("w_in"), m.sem("own")
        stats_ready, sd_ready, xn_ready, passed = m.sem("stats_ready"), m.sem("sd_ready"), m.sem("xn_ready"), m.sem("passed")
        on_act = m.banks("on_act", 0, 6, psum)
        with nc.Block() as block:
            @block.sync
            def _(sp):
                sp.dma_start(gate[:, :, :], d["gate_w"]).then_inc(w_in, 16)
                used = Tally(xn_ready)

                def body(i):
                    for b in range(B):
                        wait(sp, used, B - 1)
                        used.add()
                        sp.dma_start(rows[b][:, :, :], rows_of(d["X"], (i * B + b) * GR, G)).then_inc(rows_in[b], 16)

                rounds(sp, NG // B, body, used)

            @block.vector
            def _(dve):
                chain, deviation = Tally(own), Tally(sd_ready)
                loaded, turned = [Tally(rows_in[b], 16) for b in range(B)], Tally(on_act.full)

                def body(i):
                    for b in range(B):
                        wait(dve, loaded[b].add())
                        ln_stats(dve, chain, passed, rows[b], st[:, b], mv[:, b], G, stats_ready)
                    for b in range(B):
                        wait(dve, turned, 3 * B - 2 * (b + 1))
                        hold(dve, passed)
                        ln_apply(dve, chain, deviation, rows[b], mv[:, b], sd[:, b], xn[b], G, xn_ready)
                    turned.add(3 * B)

                rounds(dve, NG // B, body, *loaded, chain, deviation, turned)

            @block.scalar
            def _(act):
                stats, read = Tally(stats_ready), on_act.reader()

                def body(i):
                    for b in range(B):
                        ln_deviation(act, stats, mv[:, b], sd[:, b], s.eps, sd_ready)
                    if isinstance(i, int):
                        read.skip(3 * B)
                    else:
                        empty(i - 1)

                def empty(i):
                    for b in range(B):
                        for k in range(2):
                            bank = on_act.get(act, read)
                            act.activation(xt[b][:, k, :], bank[:, :], ACT.Copy).then_inc(on_act.empty, 1)
                    for b in range(B):
                        bank = on_act.get(act, read)
                        hold(act, passed)
                        act.activation(s.logits[:, bass.ds((i * B + b) * G, G), :].rearrange("p t e -> p (t e)"),
                                       bank[:, 0:G * EXPERTS], ACT.Copy).then_inc(on_act.empty, 1)

                rounds(act, NG // B, body, stats, read)
                empty(NG // B - 1)

            @block.tensor
            def _(pe):
                pe.wait_ge(w_in, 16)
                xn_in, ta = Tally(xn_ready), on_act.writer()

                def body(i):
                    for b in range(B):
                        wait(pe, xn_in.add())
                        for k in range(2):
                            bank = on_act.take(pe, ta)
                            for j in range(G):
                                last = pe.transpose(bank[:, j * P:(j + 1) * P], xn[b][:, j, k * P:(k + 1) * P], s.ident[:, :])
                            on_act.filled(last, ta)
                    for b in range(B):
                        if b:
                            bank = on_act.take(pe, ta)
                        else:
                            pe.wait_ge(on_act.empty, ta.now())
                            bank = on_act.take(pe, ta, True)
                        for j in range(G):
                            o = bank[:, j * EXPERTS:(j + 1) * EXPERTS]
                            pe.matmul(o, xt[b][:, 0, j * P:(j + 1) * P], gate[:, 0, :], start=True, stop=False)
                            last = pe.matmul(o, xt[b][:, 1, j * P:(j + 1) * P], gate[:, 1, :], start=False, stop=True)
                        on_act.filled(last, ta)

                rounds(pe, NG // B, body, xn_in, ta)


def stage_router(nc, d, s, psum):
    W = NT * EXPERTS
    with Stage(nc, "ro") as m:
        ex, hot, a, b_, tot, incl = (m.sb(n, [P, NT, EXPERTS]) for n in ("ex", "hot", "a", "b", "tot", "incl"))
        hot16 = m.sb("hot16", [P, NT, EXPERTS], BF16)
        tri, ones = m.sb("tri", [P, P], BF16), m.sb("ones", [P, P], BF16)
        tri32, real = m.sb("tri32", [P, P]), m.sb("real", [P, NT])
        ones_row = m.sb("ones_row", [P, NT])
        top, total, prob = m.sb("top", [P, NT]), m.sb("total", [P, NT]), m.sb("prob", [P, NT])
        rank, base, gate_b = (m.sb(n, [P, EXPERTS]) for n in ("rank", "base", "gate_b"))
        c_in, own, shifted, exps, hot_ready, counted = (m.sem(n) for n in ("c_in", "own", "shifted", "exps", "hot_ready", "counted"))
        cuts = [(0, 512), (512, 1024), (1024, W)]
        flat = lambda t: t[:, :, :].rearrange("p t e -> p (t e)")
        with nc.Block() as block:
            @block.sync
            def _(sp):
                sp.dma_start(rank[:, :], d["expert_rank"]).then_inc(c_in, 16)
                sp.dma_start(gate_b[:, :], d["gate_b"]).then_inc(c_in, 16)
                sp.dma_start(tri32[:, :], d["tri"]).then_inc(c_in, 16)
                sp.dma_start(real[:, :], d["real"]).then_inc(c_in, 16)
                sp.dma_start(base[:, :], d["slot_base"]).then_inc(c_in, 16)
                sp.dma_start(s.entry[:, :, 0], d["node_id"], allow_slow_non_contiguous=True).then_inc(c_in, 16)

            @block.vector
            def _(dve):
                chain = Tally(own)

                def then(ins):
                    ins.then_inc(own, 1)
                    wait(dve, chain.add())

                dve.memset(ones[:, :], 1.0)
                dve.memset(ones_row[:, :], 1.0)
                dve.wait_ge(c_in, 96)
                dve.tensor_copy(tri[:, :], tri32[:, :])
                lg = s.logits
                then(dve.tensor_tensor(lg[:, :, :], lg[:, :, :], over(gate_b[:, :], NT), ALU.add))
                then(dve.tensor_reduce(top[:, :], lg[:, :, :], AX.X, ALU.max))
                dve.tensor_tensor(a[:, :, :], lg[:, :, :], each(top[:, :], EXPERTS), ALU.subtract).then_inc(shifted, 1)
                dve.wait_ge(exps, 1)
                then(dve.tensor_reduce(total[:, :], ex[:, :, :], AX.X, ALU.add))
                then(dve.tensor_reduce(top[:, :], ex[:, :, :], AX.X, ALU.max))
                then(dve.tensor_tensor(hot[:, :, :], ex[:, :, :], each(top[:, :], EXPERTS), ALU.is_ge))
                then(dve.reciprocal(total[:, :], total[:, :]))
                then(dve.tensor_tensor(s.entry[:, :, 1].bitcast(F32), top[:, :], total[:, :], ALU.mult))
                then(dve.tensor_tensor(a[:, :, :], hot[:, :, :], over(rank[:, :], NT), ALU.mult))
                then(dve.tensor_reduce(top[:, :], a[:, :, :], AX.X, ALU.max))
                then(dve.tensor_tensor(hot[:, :, :], a[:, :, :], each(top[:, :], EXPERTS), ALU.is_equal))
                then(dve.tensor_tensor(hot[:, :, :], hot[:, :, :], each(real[:, :], EXPERTS), ALU.mult))
                dve.tensor_copy(hot16[:, :, :], hot[:, :, :]).then_inc(hot_ready, 1)
                dve.wait_ge(counted, 1)
                for k, (lo, hi) in enumerate(cuts):
                    dve.tensor_copy(flat(incl)[:, lo:hi], psum[k][:, 0:hi - lo])
                    last = dve.tensor_copy(flat(tot)[:, lo:hi], psum[3 + k][:, 0:hi - lo])
                then(last)
                for e in range(EXPERTS):
                    last = dve.tensor_tensor_scan(a[:, :, e], ones_row[:, :], tot[:, :, e], 0.0, ALU.mult, ALU.add)
                then(last)
                then(dve.tensor_tensor(a[:, :, :], a[:, :, :], tot[:, :, :], ALU.subtract))
                then(dve.tensor_tensor(a[:, :, :], a[:, :, :], incl[:, :, :], ALU.add))
                then(dve.tensor_scalar(b_[:, :, :], a[:, :, :], float(CAP), float(SKIP), ALU.is_gt, ALU.mult))
                then(dve.tensor_tensor(a[:, :, :], a[:, :, :], over(base[:, :], NT), ALU.add))
                then(dve.tensor_tensor(a[:, :, :], a[:, :, :], b_[:, :, :], ALU.add))
                then(dve.tensor_scalar(a[:, :, :], a[:, :, :], -float(SKIP), None, ALU.add))
                then(dve.tensor_tensor(a[:, :, :], a[:, :, :], hot[:, :, :], ALU.mult))
                then(dve.tensor_reduce(top[:, :], a[:, :, :], AX.X, ALU.add))
                then(dve.tensor_scalar(s.slot[:, :], top[:, :], float(SKIP), None, ALU.add))

            @block.scalar
            def _(act):
                act.wait_ge(shifted, 1)
                act.activation(ex[:, :, :], a[:, :, :], ACT.Exp).then_inc(exps, 1)

            @block.tensor
            def _(pe):
                pe.wait_ge(hot_ready, 1)
                for k, (lo, hi) in enumerate(cuts):
                    pe.matmul(psum[k][:, 0:hi - lo], tri[:, :], flat(hot16)[:, lo:hi], start=True, stop=True)
                    last = pe.matmul(psum[3 + k][:, 0:hi - lo], ones[:, :], flat(hot16)[:, lo:hi], start=True, stop=True)
                last.then_inc(counted, 1)


def table_scatter(m, block, d, s, table, slots):
    K = 8
    cur = [m.sb(f"cur{b}", [P, K], I32) for b in range(2)]
    ent = [m.sb(f"ent{b}", [P, K, 2], I32) for b in range(2)]
    sent, cur_ready, passed = m.sems("sent"), m.sem("cur_ready"), m.sem("passed")

    @block.gpsimd
    def _(pool):
        ready, old = Tally(cur_ready), [Tally(sent[b], 16) for b in range(2)]

        def body(i):
            for b in range(2):
                t = (i * 2 + b) * K
                wait(pool, old[b])
                hold(pool, passed)
                pool.tensor_copy(cur[b][:, :], s.slot[:, bass.ds(t, K)])
                pool.tensor_copy(ent[b][:, :, :], s.entry[:, bass.ds(t, K), :]).then_inc(cur_ready, 1)
                wait(pool, ready.add())
                hold(pool, passed)
                for j in range(K):
                    pool.indirect_dma_start(
                        out=d[table], out_offset=bass.IndirectOffsetOnAxis(ap=cur[b][:, j:j + 1], axis=0),
                        in_=ent[b][:, j, :], in_offset=None,
                        bounds_check=slots - 1, oob_is_err=False).then_inc(sent[b], 16)
                    old[b].add()

        rounds(pool, NT // K // 2, body, ready, *old)
        for b in range(2):
            pool.wait_ge(sent[b], 16 * NT // 2)


def stage_ffn(nc, d, s, psum, moe):
    tag = "moe" if moe else "mod"
    M = 2 * XB if moe else 4
    RN = (EXPERTS * XB if moe else SB) // M
    R = XB if moe else 4
    table = d["moe_table"] if moe else d["mod_table"]
    DST = d["X"] if moe else d["out"]
    HF = FB // 2
    HC = HID // P
    LAG = R - 1
    FR = mybir.dt.float32r
    with Stage(nc, tag) as m:
        tab = [m.sb(f"tab{r}", [P, FT, 2], I32) for r in range(R)]
        rows = [m.sb(f"rows{r}", [P, FT, C]) for r in range(R)]
        xn = [m.sb(f"xn{r}", [P, FT, C]) for r in range(2 if moe else R)]
        NX = len(xn)
        RING = 4
        x_raw, x = m.sb("x_raw", [P, 2, FB]), [m.sb(f"x_{n}", [P, 2, FB], FR) for n in ("high", "low")]
        h_raw, h = m.sb("h_raw", [P, RING, FB]), [m.sb(f"h_{n}", [P, HC, FB], FR) for n in ("high", "low")]
        y = [m.sb(f"y{b}", [P, FT, C]) for b in range(2)]
        nb = 2 if moe else 1
        w1_raw, w1 = m.sb("w1_raw", [P, 2, HID]), [m.sb(f"w1_{n}", [P, 2, HID], FR) for n in ("high", "low")]
        w2_raw, w2 = m.sb("w2_raw", [P, HC, C]), [m.sb(f"w2_{n}", [P, HC, C], FR) for n in ("high", "low")]
        b1 = [m.sb(f"b1{q}", [P, HC]) for q in range(nb)]
        b2 = [m.sb(f"b2{q}", [P, C]) for q in range(nb)]
        st, mv, sd = m.sb("st", [P, FT, 6]), m.sb("mv", [P, 2, FT, 2]), m.sb("sd", [P, 2, FT])
        safe = m.sb("safe", [P, FT, C]) if moe else None
        low = m.sb("low", [P, FT, C]) if moe else None
        tab_in, rows_in, scattered = m.sems("tab_in", R), m.sems("rows_in", R), m.sems("scattered", R)
        (w_in, zeroed, stats_ready, sd_ready, xn_ready, own, y_ready, w1_high, w2_high, w1_split, w2_split, x_split, h_split) = (
            m.sem(n) for n in ("w_in", "zeroed", "stats_ready", "sd_ready", "xn_ready", "own", "y_ready",
                               "w1_high", "w2_high", "w1_split", "w2_split", "x_split", "h_split"))
        passed = m.sems("passed", 3)
        turned = m.banks("turned", 0, 2, psum)
        hidden = m.banks("hidden", 2, 4, psum)
        result = m.banks("result", 6, 2, psum)

        def last(i):
            return isinstance(i, int) and i == RN - 1

        def all_rounds(eng, body, *tallies):
            rounds(eng, RN - 1, body, *tallies)
            body(RN - 1)

        def at_start(i, k):
            return isinstance(i, int) and i == 0 and k == 0

        with nc.Block() as block:
            @block.sync
            def _(sp):
                done = Tally(w2_split)
                freed = [Tally(scattered[r], 16 * FT) for r in range(R)]

                def weights(e, q):
                    pick = (lambda a: a[bass.ds(e, 1)].rearrange("o p n -> (o p) n")) if moe else (lambda a: a)
                    for t, name in ((w1_raw[:, :, :].rearrange("p k n -> p (k n)"), "w1"),
                                    (w2_raw[:, :, :].rearrange("p k n -> p (k n)"), "w2"),
                                    (b1[q][:, :], "b1"), (b2[q][:, :], "b2")):
                        sp.dma_start(t, pick(d[f"{tag}_{name}"])).then_inc(w_in, 16)

                def body(i):
                    for k in range(M):
                        r = k % R
                        wait(sp, freed[r])
                        freed[r].add()
                        sp.dma_start(tab[r][:, :, :], rows_of(table, (i * M + k) * FB, FT)).then_inc(tab_in[r], 16)
                        if moe and k % XB == 3 and not (k > XB and last(i)):
                            wait(sp, done.add())
                            weights(i * 2 + k // XB + 1, 1 - k // XB)

                weights(0, 0)
                all_rounds(sp, body, *freed, *([done] if moe else []))

            @block.gpsimd
            def _(pool):
                for t in rows + ([] if moe else xn):
                    pool.memset(t[:, :, :], 0.0).then_inc(zeroed, 1)
                pool.wait_ge(zeroed, R if moe else 2 * R)
                here, made = [Tally(tab_in[r], 16) for r in range(R)], Tally(y_ready)

                def gather(k):
                    r = k % R
                    wait(pool, here[r].add())
                    hold(pool, passed[0])
                    for j in range(FT):
                        for t, src in ((rows[r], d["X"] if moe else d["base"]),) + (() if moe else ((xn[r], d["XN"]),)):
                            pool.indirect_dma_start(
                                out=t[:, j, :], out_offset=None, in_=src,
                                in_offset=bass.IndirectOffsetOnAxis(ap=tab[r][:, j, 0:1], axis=0),
                                bounds_check=NP - 1, oob_is_err=False).then_inc(rows_in[r], 16)

                def scatter(k):
                    r = k % R
                    wait(pool, made.add())
                    hold(pool, passed[0])
                    for j in range(FT):
                        pool.indirect_dma_start(
                            out=DST, out_offset=bass.IndirectOffsetOnAxis(ap=tab[r][:, j, 0:1], axis=0),
                            in_=rows[r][:, j, :], in_offset=None,
                            bounds_check=NP - 1, oob_is_err=False).then_inc(scattered[r], 16)

                def body(i):
                    for k in range(M):
                        gather(k)
                        if isinstance(i, int) and i == 0 and k < LAG:
                            made.skip()
                        else:
                            scatter(k - LAG)

                all_rounds(pool, body, *here, made)
                for k in range(LAG):
                    scatter(M - LAG + k)
                for r in range(R):
                    pool.wait_ge(scattered[r], 16 * FT * RN * M // R)

            @block.scalar
            def _(act):
                stats, turn, read, res = Tally(stats_ready), turned.reader(), hidden.reader(), result.reader()
                w_here, finished, used = Tally(w_in, 64), Tally(y_ready), Tally(h_split)
                fn = ACT.Relu if moe else ACT.Gelu_apprx_tanh

                def weights_high(whole, high, ready):
                    for n in range(2):
                        half = slice(n * (whole.shape[1] // 2), (n + 1) * (whole.shape[1] // 2))
                        ins = act.activation(high[:, half, :], whole[:, half, :], ACT.Copy)
                    ins.then_inc(ready, 1)

                def body(i):
                    for k in range(M):
                        q = k // XB if moe else 0
                        if at_start(i, k):
                            res.skip(FT)
                            finished.skip()
                        else:
                            wait(act, finished, 1)
                            finished.add()
                            hold(act, passed[2])
                        for j in range(FT):
                            for t in range(2 * j, min(2 * j + 2, FT)):
                                bank = turned.get(act, turn)[:, 0:C].rearrange("p (k n) -> p k n", k=2)
                                n = slice(t * P, (t + 1) * P)
                                act.activation(x_raw[:, :, n], bank, ACT.Copy)
                                act.activation(x[0][:, :, n], bank, ACT.Copy).then_inc(turned.empty, 1)
                            if not at_start(i, k):
                                result_out(k - 1, j)
                            if j == 0 and moe and not (last(i) and k == M - 1):
                                ln_deviation(act, stats, mv[:, (k + 1) % 2], sd[:, (k + 1) % 2], s.eps, sd_ready)
                            if j == 1 and moe and k % XB == 0:
                                wait(act, w_here.add())
                                hold(act, passed[2])
                                weights_high(w1_raw, w1[0], w1_high)
                        if moe and k % XB == 0:
                            weights_high(w2_raw, w2[0], w2_high)
                        for f in range(HC):
                            wait(act, used, RING - 1)
                            used.add()
                            hold(act, passed[2])
                            for half in range(2):
                                bank = hidden.get(act, read)
                                act.activation(h_raw[:, f % RING, half * HF:(half + 1) * HF], bank[:, 0:HF], fn, bias=b1[q][:, f:f + 1]).then_inc(hidden.empty, 1)

                def result_out(k, j):
                    bank = result.get(act, res)
                    act.activation(y[k % 2][:, j, :], bank[:, 0:C], ACT.Copy, scale=tab[k % R][:, j, 1:2].bitcast(F32)).then_inc(result.empty, 1)

                if moe:
                    ln_deviation(act, stats, mv[:, 0], sd[:, 0], s.eps, sd_ready)
                else:
                    wait(act, w_here.add())
                    weights_high(w1_raw, w1[0], w1_high)
                    weights_high(w2_raw, w2[0], w2_high)
                all_rounds(act, body, stats, turn, read, res, finished, used, *([w_here] if moe else []))
                wait(act, finished, 1)
                hold(act, passed[2])
                for j in range(FT):
                    result_out(M - 1, j)

            @block.vector
            def _(dve):
                chain, deviation = Tally(own), Tally(sd_ready)
                loaded = [Tally(rows_in[r], 16 * FT * (1 if moe else 2)) for r in range(R)]
                turn, read, res = turned.reader(), hidden.reader(), Tally(result.empty)
                highs = {w1_high: Tally(w1_high), w2_high: Tally(w2_high)}

                def then(ins):
                    ins.then_inc(own, 1)
                    wait(dve, chain.add())

                def split_weights(whole, w, high, ready):
                    wait(dve, highs[high].add())
                    dve.tensor_tensor(w[1][:, :, :], whole[:, :, :], w[0][:, :, :].bitcast(F32), ALU.subtract).then_inc(ready, 1)

                def statistics(k):
                    r = k % R
                    wait(dve, loaded[r].add())
                    ln_stats(dve, chain, passed[1], rows[r], st, mv[:, k % 2], FT, stats_ready)

                def normalise(k):
                    ln_apply(dve, chain, deviation, rows[k % R], mv[:, k % 2], sd[:, k % 2], xn[k % 2], FT, xn_ready)

                def bias(k, j):
                    r, q = k % R, (k % M) // XB if moe else 0
                    wait(dve, res.add())
                    yj = y[k % 2][:, j, :]
                    ins = dve.scalar_tensor_tensor(yj, b2[q][:, :], tab[r][:, j, 1:2].bitcast(F32), yj, ALU.mult, ALU.add)
                    if j == FT - 1:
                        then(ins)

                def finish(k):
                    r, z = k % R, y[k % 2]
                    if moe:
                        then(dve.tensor_scalar(low[:, :, :], z[:, :, :], 0.0, None, ALU.min))
                        yield
                        then(dve.scalar_tensor_tensor(safe[:, :, :], z[:, :, :], 0.0, low[:, :, :], ALU.max, ALU.add))
                        yield
                        dve.tensor_scalar(safe[:, :, :], safe[:, :, :], 1e4, -1e4, ALU.min, ALU.max)
                        dve.tensor_scalar(low[:, :, :].bitcast(U32), z[:, :, :], 0.0, 0.0, ALU.mult, ALU.is_equal).then_inc(own, 1)
                        wait(dve, chain.add())
                        yield
                        hold(dve, passed[1])
                        then(dve.copy_predicated(safe[:, :, :], low[:, :, :].bitcast(U32), z[:, :, :]))
                    else:
                        wait(dve, loaded[r].add())
                    yield
                    dve.tensor_tensor(rows[r][:, :, :], rows[r][:, :, :], (safe if moe else z)[:, :, :], ALU.add).then_inc(y_ready, 1)

                FINISH = 4 if moe else 0

                def body(i):
                    for k in range(M):
                        steps, last_block = iter(()), last(i) and k == M - 1
                        if at_start(i, k):
                            res.skip(FT)
                            chain.skip()
                        if at_start(i, k) or at_start(i, k - 1):
                            chain.skip(FINISH)
                            if not moe:
                                loaded[(k - 2) % R].skip()
                        else:
                            steps = finish(k - 2)
                        if moe and not last_block:
                            statistics(k + 1)
                        for j in range(FT):
                            if not at_start(i, k):
                                bias(k - 1, j)
                            if j == 1:
                                turn.add(FT)
                                dve.wait_ge(turned.empty, turn.now())
                                dve.tensor_tensor(x[1][:, :, :], x_raw[:, :, :], x[0][:, :, :].bitcast(F32), ALU.subtract).then_inc(x_split, 1)
                                if moe and k % XB == 0:
                                    split_weights(w1_raw, w1, w1_high, w1_split)
                            if j == 2 and moe and not last_block:
                                normalise(k + 1)
                            if j < 4:
                                next(steps, None)
                        for f in range(HC):
                            read.add(2)
                            dve.wait_ge(hidden.empty, read.now())
                            then(dve.tensor_copy(h[0][:, f, :], h_raw[:, f % RING, :]))
                            dve.tensor_tensor(h[1][:, f, :], h_raw[:, f % RING, :], h[0][:, f, :].bitcast(F32), ALU.subtract).then_inc(h_split, 1)
                            if f == 0:
                                next(steps, None)
                            if moe and f == 3 and k % XB == 0:
                                split_weights(w2_raw, w2, w2_high, w2_split)

                if not moe:
                    split_weights(w1_raw, w1, w1_high, w1_split)
                    split_weights(w2_raw, w2, w2_high, w2_split)
                if moe:
                    statistics(0)
                    normalise(0)
                all_rounds(dve, body, chain, deviation, *loaded, turn, read, res, *(highs.values() if moe else []))
                for _ in finish(M - 2):
                    pass
                for j in range(FT):
                    bias(M - 1, j)
                for _ in finish(M - 1):
                    pass

            @block.tensor
            def _(pe):
                tt, th, tr = turned.writer(), hidden.writer(), result.writer()
                xn_in, w1_in, w2_in, x_in, h_in = Tally(xn_ready), Tally(w1_split), Tally(w2_split), Tally(x_split), Tally(h_split)
                loaded = [Tally(rows_in[r], 16 * FT * 2) for r in range(R)]

                def product(out, a, sa, b, sb, start, stop):
                    pe.matmul(out, a[0][sa], b[0][sb], start=start, stop=False)
                    pe.matmul(out, a[0][sa], b[1][sb], start=False, stop=False)
                    return pe.matmul(out, a[1][sa], b[0][sb], start=False, stop=stop)

                every = slice(None)

                def turn(k, j):
                    bank = turned.take(pe, tt)
                    for c in range(2):
                        last = pe.transpose(bank[:, c * P:(c + 1) * P], xn[k % NX][:, j, c * P:(c + 1) * P], s.ident[:, :])
                    turned.filled(last, tt)

                def first(k):
                    wait(pe, x_in.add())
                    for f in range(HC):
                        fs = slice(f * P, (f + 1) * P)
                        for half in range(2):
                            bank = hidden.take(pe, th)
                            n = slice(half * HF, (half + 1) * HF)
                            for c in range(2):
                                last = product(bank[:, 0:HF], w1, (every, c, fs), x, (every, c, n), c == 0, c == 1)
                            hidden.filled(last, th)

                def second(k, j):
                    bank = result.take(pe, tr)
                    js = slice(j * P, (j + 1) * P)
                    for f in range(HC):
                        if j == 0:
                            wait(pe, h_in.add())
                        last = product(bank[:, 0:C], h, (every, f, js), w2, (every, f, every), f == 0, f == HC - 1)
                    result.filled(last, tr)

                def body(i):
                    for k in range(M):
                        wait(pe, xn_in.add() if moe else loaded[k % R].add())
                        if at_start(i, k):
                            tr.skip(FT)
                            h_in.skip(HC)
                        for j in range(FT):
                            for t in range(2 * j, min(2 * j + 2, FT)):
                                turn(k, t)
                            if moe and k % XB == 1 and j == 0:
                                wait(pe, w2_in.add())
                            if not at_start(i, k):
                                second(k - 1, j)
                        if moe and k % XB == 0:
                            wait(pe, w1_in.add())
                        first(k)

                if not moe:
                    wait(pe, w1_in.add())
                    wait(pe, w2_in.add())
                all_rounds(pe, body, tt, th, tr, x_in, h_in, *((xn_in, w1_in, w2_in) if moe else loaded))
                for j in range(FT):
                    second(M - 1, j)


H1 = 64


def planar(row):
    return row[:, H1:C].rearrange("p (c x) -> p x c", x=3)


def ln_apply_planar(dve, own, deviation, rows, mv, sd, out, tiles, ready):
    wait(dve, deviation.add())
    dve.reciprocal(sd[:, :], sd[:, :]).then_inc(own.sem, 1)
    wait(dve, own.add())
    for j in range(tiles):
        dve.tensor_scalar(out[:, j, 0:H1], rows[:, j, 0:H1], mv[:, j, 0:1], sd[:, j:j + 1], ALU.subtract, ALU.mult)
        last = dve.tensor_scalar(out[:, j, H1:C].rearrange("p (x c) -> p x c", x=3), planar(rows[:, j, :]),
                                 mv[:, j, 0:1], sd[:, j:j + 1], ALU.subtract, ALU.mult)
    last.then_inc(ready, 1)


def edge_mlp(m, block, d, psum):
    R_IN = 16
    PARTS = 2 * (EG // 2)
    rbf = [m.sb(f"rbf{b}", [R_IN, GR]) for b in range(2)]
    r1, r2, r3 = ([m.sb(f"r{k}{b}", [H1, GR]) for b in range(2)] for k in (1, 2, 3))
    m1, m2, m3 = m.sb("m1", [R_IN, H1]), m.sb("m2", [H1, H1]), m.sb("m3", [H1, H1])
    zeros = m.sb("zeros", [P, NP // PARTS // P, C])
    w_in, rbf_in, zeroed, filled, stored = m.sem("w_in"), m.sems("rbf_in"), m.sem("zeroed"), m.sem("filled"), m.sems("stored")
    passed = m.sem("passed_pe")
    on_act = m.banks("on_act", 0, 6, psum)

    @block.vector
    def _(dve):
        dve.memset(zeros[:, :, :], 0.0).then_inc(zeroed, 1)

    @block.sync
    def _(sp):
        for t, name in ((m1, "M1"), (m2, "M2"), (m3, "M3")):
            sp.dma_start(t[:, :], d[name]).then_inc(w_in, 16)
        sp.wait_ge(zeroed, 1)
        read, made = Tally(on_act.empty, 6), Tally(on_act.empty)

        def body(i):
            for b in range(2):
                wait(sp, read)
                sp.dma_start(rbf[b][:, :], d["rbf"][:, bass.ds((i * 2 + b) * GR, GR)]).then_inc(rbf_in[b], 16)
            read.add()
            for b in range(2):
                sp.dma_start(d["D"][bass.ds((i * 2 + b) * (NP // PARTS), NP // PARTS), :].rearrange("(p t) c -> p t c", p=P),
                             zeros[:, :, :]).then_inc(filled, 16)
            made.add(4)
            for b in range(2):
                wait(sp, made.add())
                sp.dma_start(d["R"][:, bass.ds((i * 2 + b) * GR, GR)], r3[b][:, :]).then_inc(stored[b], 16)

        rounds(sp, EG // 2, body, read, made)
        sp.wait_ge(filled, 16 * PARTS)
        for b in range(2):
            sp.wait_ge(stored[b], 16 * EG // 2)

    @block.scalar
    def _(act):
        t, old = on_act.reader(), [Tally(stored[b], 16) for b in range(2)]

        def body(i):
            for out in (r1, r2, r3):
                for b in range(2):
                    if out is r3:
                        wait(act, old[b])
                        old[b].add()
                    bank = on_act.get(act, t)
                    act.activation(out[b][:, :], bank[0:H1, :], ACT.Silu).then_inc(on_act.empty, 1)

        rounds(act, EG // 2, body, t, *old)

    @block.tensor
    def _(pe):
        pe.wait_ge(w_in, 48)
        t, here = on_act.writer(), [Tally(rbf_in[b], 16) for b in range(2)]

        def body(i):
            for w, src in ((m1, rbf), (m2, r1), (m3, r2)):
                for b in range(2):
                    if src is rbf:
                        wait(pe, here[b].add())
                    else:
                        pe.wait_ge(on_act.empty, t.now(1))
                    bank = on_act.take(pe, t, src is not rbf)
                    hold(pe, passed)
                    on_act.filled(pe.matmul(bank[0:H1, :], w[:, :], src[b][:, :], start=True, stop=True), t)

        rounds(pe, EG // 2, body, t, *here)


def stage_table(nc, d, s, psum, moe):
    with Stage(nc, "mt" if moe else "dt") as m:
        with nc.Block() as block:
            if moe:
                table_scatter(m, block, d, s, "moe_table", EXPERTS * SLOTS)
                edge_mlp(m, block, d, psum)
            else:
                table_scatter(m, block, d, s, "mod_table", SB * FB)


def stage_messages(nc, d, s, psum):
    with Stage(nc, "ms") as m:
        rows, xn, up, msg, run, dl = ([m.sb(f"{n}{b}", [P, G, C]) for b in range(2)]
                                             for n in ("rows", "xn", "up", "msg", "run", "dl"))
        aa, bb2 = (m.sb(n, [P, 2 * G, C]) for n in ("a", "bb"))
        a, bb = ([t[:, b * G:(b + 1) * G, :] for b in range(2)] for t in (aa, bb2))
        xt = [m.sb(f"xt{b}", [P, 2, GR]) for b in range(2)]
        rad = [m.sb(f"rad{b}", [H1, GR]) for b in range(2)]
        row = [m.sb(f"row{b}", [P, GR], I32) for b in range(2)]
        sh = [m.sb(f"sh{b}", [P, G, 4]) for b in range(2)]
        same = [m.sb(f"same{b}", [P, G, P]) for b in range(2)]
        carry = [m.sb(f"carry{b}", [P, G, P]) for b in range(2)]
        src_col = m.sb("src_col", [P, ET], I32)
        curg, cure = m.sb("curg", [P, 2, G], I32), m.sb("cure", [P, 2, G], I32)
        w_up, w_lin, w_b = (m.sb(n, [P, 2, P]) for n in ("w_up", "w_lin", "w_b"))
        m4 = m.sb("m4", [H1, C])
        wc = m.sb("wc", [P, 9, H1])
        t1, t2, t3 = (m.sb(n, [P, 2 * G, H1]) for n in ("t1", "t2", "t3"))
        v1, v2 = m.sb("v1", [P, 2 * G, 3, H1]), m.sb("v2", [P, G, H1])
        st, mv, sd = m.sb("st", [P, 2, G, 6]), m.sb("mv", [P, 2, G, 2]), m.sb("sd", [P, 2, G])
        w_in, row_in, rad_in, rows_in, scattered = m.sem("w_in"), m.sems("row_in"), m.sems("rad_in"), m.sems("rows_in"), m.sems("scattered")
        (own, stats_ready, sd_ready, xn_ready, msg_ready, bb_ready, start, g_ready, e_ready) = (
            m.sem(n) for n in ("own", "stats_ready", "sd_ready", "xn_ready", "msg_ready", "bb_ready", "start", "g_ready", "e_ready"))
        passed = m.sems("passed", 4)
        on_act = m.banks("on_act", 0, 4, psum)
        on_dve = m.banks("on_dve", 4, 4, psum)
        STEP, LAST = 8, EG // 2 - 1
        with nc.Block() as block:
            @block.sync
            def _(sp):
                for t, name in ((w_up[:, :, :], "w_up"), (w_lin[:, :, :], "w_lin"), (w_b[:, :, :], "w_b"), (m4[:, :], "M4"), (wc[:, :, :], "wc"), (src_col[:, :], "src_col")):
                    sp.dma_start(t, d[name]).then_inc(w_in, 16)
                made = Tally(msg_ready)

                def body(i):
                    for b in range(2):
                        g = i * 2 + b
                        wait(sp, made, 1)
                        made.add()
                        sp.dma_start(row[b][:, :], d["dst_rows"][:, bass.ds(g * GR, GR)]).then_inc(row_in[b], 16)
                        sp.dma_start(sh[b][:, :, :], rows_of(d["sh"], g * GR, G)).then_inc(row_in[b], 16)
                        sp.dma_start(rad[b][:, :], d["R"][:, bass.ds(g * GR, GR)]).then_inc(rad_in[b], 16)

                rounds(sp, EG // 2, body, made)

            @block.gpsimd
            def _(pool):
                pool.memset(run[1][:, G - 1, :], 0.0).then_inc(start, 1)
                pool.wait_ge(w_in, 96)
                gi, ei, used = Tally(g_ready), Tally(e_ready), Tally(xn_ready)
                here, old, made = [Tally(rows_in[b], 16) for b in range(2)], [Tally(scattered[b], 16) for b in range(2)], Tally(on_act.empty, STEP)

                def gather(i, b):
                    wait(pool, here[b])
                    wait(pool, used, 1)
                    used.add()
                    hold(pool, passed[0])
                    pool.tensor_copy(curg[:, b, :], src_col[:, bass.ds((i * 2 + b) * G, G)]).then_inc(g_ready, 1)
                    wait(pool, gi.add())
                    hold(pool, passed[0])
                    for j in range(G):
                        pool.indirect_dma_start(out=rows[b][:, j, :], out_offset=None, in_=d["X"],
                                                in_offset=bass.IndirectOffsetOnAxis(ap=curg[:, b, j:j + 1], axis=0),
                                                bounds_check=NP - 1, oob_is_err=False).then_inc(rows_in[b], 16)
                        here[b].add()

                def scatter(i, b, less=0):
                    wait(pool, old[b])
                    hold(pool, passed[0])
                    pool.tensor_copy(cure[:, b, :], s.end_row[:, bass.ds((i * 2 + b) * G, G)]).then_inc(e_ready, 1)
                    wait(pool, ei.add())
                    if b == 0:
                        made.add(4)
                    wait(pool, made, less)
                    hold(pool, passed[0])
                    for j in range(G):
                        pool.indirect_dma_start(out=d["D"], out_offset=bass.IndirectOffsetOnAxis(ap=cure[:, b, j:j + 1], axis=0),
                                                in_=dl[b][:, j, :], in_offset=None,
                                                bounds_check=NP - 1, oob_is_err=False).then_inc(scattered[b], 16)
                        old[b].add()

                def body(i):
                    for b in range(2):
                        gather(i, b)
                    for b in range(2):
                        if isinstance(i, int):
                            ei.skip()
                            made.skip(4 * (1 - b))
                            old[b].skip(G)
                        else:
                            scatter(i - 1, b)

                made.add()
                rounds(pool, EG // 2, body, gi, ei, used, made, *here, *old)
                for b in range(2):
                    scatter(LAST, b, 1)
                for b in range(2):
                    pool.wait_ge(scattered[b], 16 * G * EG // 2)

            @block.scalar
            def _(act):
                stats, read, old = Tally(stats_ready), on_act.reader(), [Tally(scattered[b], 16) for b in range(2)]

                def two(out, n=2):
                    for k in range(n):
                        bank = on_act.get(act, read)
                        act.activation(out[:, k * (G // n):(k + 1) * (G // n), :], bank[:, 0:G * C // n].rearrange("p (j c) -> p j c", c=C), ACT.Copy).then_inc(on_act.empty, 1)

                def turned(out):
                    for k in range(2):
                        bank = on_act.get(act, read)
                        act.activation(out[:, k, :], bank[:, :], ACT.Copy).then_inc(on_act.empty, 1)

                def deviations():
                    for b in range(2):
                        ln_deviation(act, stats, mv[:, b], sd[:, b], s.eps, sd_ready)

                def next_up():
                    for b in range(2):
                        turned(xt[b])
                    for b in range(2):
                        two(up[b])

                def body(i):
                    for b in range(2):
                        two(run[b], G)
                    if not (isinstance(i, int) and i == LAST):
                        deviations()
                    for b in range(2):
                        turned(xt[b])
                        two(a[b])
                    if not (isinstance(i, int) and i == LAST):
                        next_up()
                    for b in range(2):
                        turned(xt[b])
                        wait(act, old[b])
                        old[b].add(G)
                        two(dl[b])

                deviations()
                next_up()
                rounds(act, LAST, body, stats, read, *old)
                body(LAST)

            @block.vector
            def _(dve):
                dve.wait_ge(w_in, 96)
                chain, deviation, read = Tally(own), Tally(sd_ready), on_dve.reader()
                loaded = [Tally(rows_in[b], 16 * G) for b in range(2)]
                row_here = [Tally(row_in[b], 32) for b in range(2)]
                on_a = Tally(on_act.empty)

                def then(ins):
                    ins.then_inc(own, 1)
                    wait(dve, chain.add())

                def tt(o, x, y, op=ALU.mult):
                    then(dve.tensor_tensor(o, x, y, op))

                x3 = lambda t: t[:, :, H1:C].rearrange("p j (x c) -> p j x c", x=3)

                def messages(i, b):
                    wait(dve, row_here[b].add())
                    if isinstance(i, int) and i == 0:
                        dve.wait_ge(on_act.empty, STEP - 2 * (1 - b))
                    else:
                        wait(dve, on_a, 2 * (1 - b))
                    x0 = up[b][:, :, 0:H1]
                    s0 = sh[b][:, :, 0]
                    for k in range(2):
                        bank = on_dve.get(dve, read)
                        j2 = slice(2 * k, 2 * k + 2)
                        w = bank[:, :].rearrange("p (j f c) -> p j f c", j=2, f=4)
                        dve.tensor_tensor(t1[:, j2, :], w[:, :, 0, :], x0[:, j2, :], ALU.mult)
                        dve.tensor_tensor(t2[:, j2, :], w[:, :, 1, :], x0[:, j2, :], ALU.mult)
                        for x in range(3):
                            dve.tensor_tensor(v1[:, j2, x, :], w[:, :, 2, :], x3(up[b])[:, j2, x, :], ALU.mult)
                        dve.tensor_copy(t3[:, j2, :], w[:, :, 3, :]).then_inc(on_dve.empty, 1)
                    dve.wait_ge(on_dve.empty, read.now())
                    for x in range(3):
                        for j in range(G):
                            u, c = x3(up[b])[:, j, x, :], sh[b][:, j, 1 + x:2 + x]
                            last = (dve.tensor_scalar(v2[:, j, :], u, c, None, ALU.mult) if x == 0 else
                                    dve.scalar_tensor_tensor(v2[:, j, :], u, c, v2[:, j, :], ALU.mult, ALU.add))
                        then(last)
                    then(dve.scalar_tensor_tensor(t3[:, 0:G, :], v2[:, :, :], 3.0 ** -0.5, t3[:, 0:G, :], ALU.mult, ALU.mult))
                    for j in range(G):
                        dve.scalar_tensor_tensor(msg[b][:, j, 0:H1], t1[:, j, :], sh[b][:, j, 0:1], t3[:, j, :], ALU.mult, ALU.add)
                        last = dve.tensor_scalar(v1[:, j].rearrange("p x c -> p (x c)"), v1[:, j].rearrange("p x c -> p (x c)"), sh[b][:, j, 0:1], None, ALU.mult)
                    then(last)
                    for j in range(G):
                        for x in range(3):
                            dve.scalar_tensor_tensor(x3(msg[b])[:, j, x, :], t2[:, j, :], sh[b][:, j, 1 + x:2 + x], v1[:, j, x, :], ALU.mult, ALU.add)
                    run_masks(dve, s, (i * 2 + b) * G, same[b], carry[b], row[b]).then_inc(msg_ready, 1)

                def products():
                    wait(dve, on_a)
                    a0, a1, k = aa[:, :, 0:H1], x3(aa), lambda n: over(wc[:, n, :], 2 * G)
                    vv, p_, q_ = t1[:, :, :], t2[:, :, :], t3[:, :, :]
                    tt(v1[:, :, :, :].rearrange("p j x c -> p j (x c)"), aa[:, :, H1:C], aa[:, :, H1:C])
                    tt(vv, v1[:, :, 0, :], v1[:, :, 1, :], ALU.add)
                    tt(vv, vv, v1[:, :, 2, :], ALU.add)
                    tt(p_, a0, k(3))
                    tt(p_, p_, k(1), ALU.add)
                    tt(p_, p_, a0)
                    tt(q_, vv, k(4))
                    tt(p_, p_, q_, ALU.add)
                    tt(p_, p_, k(0), ALU.add)
                    tt(p_, p_, a0)
                    tt(q_, vv, k(2))
                    tt(bb2[:, :, 0:H1], p_, q_, ALU.add)
                    tt(p_, a0, k(7))
                    tt(p_, p_, k(6), ALU.add)
                    tt(p_, p_, a0)
                    tt(q_, vv, k(8))
                    tt(p_, p_, q_, ALU.add)
                    tt(p_, p_, k(5), ALU.add)
                    for x in range(3):
                        last = dve.tensor_tensor(x3(bb2)[:, :, x, :], a1[:, :, x, :], p_, ALU.mult)
                    last.then_inc(bb_ready, 1)

                bd, md = Tally(bb_ready), Tally(msg_ready)

                def next_rows():
                    for b in range(2):
                        wait(dve, loaded[b].add())
                        ln_stats(dve, chain, passed[1], rows[b], st[:, b], mv[:, b], G, stats_ready)
                    for b in range(2):
                        ln_apply_planar(dve, chain, deviation, rows[b], mv[:, b], sd[:, b], xn[b], G, xn_ready)

                def body(i):
                    for b in range(2):
                        messages(i, b)
                        wait(dve, md.add())
                    if not (isinstance(i, int) and i == LAST):
                        next_rows()
                    on_a.add(3 * STEP)
                    products()
                    wait(dve, bd.add())
                    on_a.add(STEP)

                next_rows()
                rounds(dve, LAST, body, chain, deviation, read, on_a, bd, md, *loaded, *row_here)
                body(LAST)

            @block.tensor
            def _(pe):
                pe.wait_ge(w_in, 96)
                pe.wait_ge(start, 1)
                ta, td = on_act.writer(), on_dve.writer()
                xn_in, rad_here, msg_in, bb_in = Tally(xn_ready), [Tally(rad_in[b], 16) for b in range(2)], Tally(msg_ready), Tally(bb_ready)

                def turn(t, all_empty=False):
                    for k in range(2):
                        bank = on_act.take(pe, ta, all_empty)
                        for j in range(G):
                            last = pe.transpose(bank[:, j * P:(j + 1) * P], t[:, j, k * P:(k + 1) * P], s.ident[:, :])
                        on_act.filled(last, ta)

                def mix(t, w, all_empty=True):
                    for j in range(G):
                        if j % 2 == 0:
                            bank = on_act.take(pe, ta, all_empty)
                        for k in range(2):
                            o = j % 2 * C + k * P
                            last = pe.matmul(bank[:, o:o + P], t[:, k, j * P:(j + 1) * P], w[:, k, :], start=True, stop=True)
                        if j % 2:
                            on_act.filled(last, ta)

                def emptied(less=0):
                    v = ta.now(less)
                    if not isinstance(v, int) or v > 0:
                        pe.wait_ge(on_act.empty, v)

                def next_up():
                    for b in range(2):
                        wait(pe, xn_in.add())
                        turn(xn[b])
                    for b in range(2):
                        emptied(2)
                        mix(xt[b], w_up)
                        wait(pe, rad_here[b].add())
                        for j in range(G):
                            if j % 2 == 0:
                                bank = on_dve.take(pe, td)
                                hold(pe, passed[2])
                            last = pe.matmul(bank[:, j % 2 * C:j % 2 * C + C], rad[b][:, j * P:(j + 1) * P], m4[:, :], start=True, stop=True)
                            if j % 2:
                                on_dve.filled(last, td)

                def body(i):
                    for b in range(2):
                        wait(pe, msg_in.add())
                        for j in range(G):
                            before = run[1 - b][:, G - 1, :] if j == 0 else run[b][:, j - 1, :]
                            bank = on_act.take(pe, ta)
                            pe.matmul(bank[:, 0:C], same[b][:, j, :], msg[b][:, j, :], start=True, stop=False)
                            emptied()
                            on_act.filled(pe.matmul(bank[:, 0:C], carry[b][:, j, :], before, start=False, stop=True), ta)
                    for b in range(2):
                        emptied()
                        turn(run[b], True)
                        emptied()
                        mix(xt[b], w_lin)
                    if not (isinstance(i, int) and i == LAST):
                        next_up()
                    wait(pe, bb_in.add())
                    for b in range(2):
                        turn(bb[b])
                        emptied()
                        mix(xt[b], w_b)

                next_up()
                rounds(pe, LAST, body, ta, td, xn_in, *rad_here, msg_in, bb_in)
                body(LAST)


def stage_node_sums(nc, d, s, psum):
    with Stage(nc, "ns") as m:
        rows, dd, xn = ([m.sb(f"{n}{b}", [P, G, C]) for b in range(2)] for n in ("rows", "dd", "xn"))
        xt = [m.sb(f"xt{b}", [P, 2, GR]) for b in range(2)]
        w_sc = m.sb("w_sc", [P, 2, P])
        st, mv, sd = m.sb("st", [P, 2, G, 6]), m.sb("mv", [P, 2, G, 2]), m.sb("sd", [P, 2, G])
        w_in, rows_in, dd_in = m.sem("w_in"), m.sems("rows_in"), m.sems("dd_in")
        own, stats_ready, sd_ready, xn_ready = (m.sem(n) for n in ("own", "stats_ready", "sd_ready", "xn_ready"))
        passed = m.sems("passed", 3)
        on_act = m.banks("on_act", 0, 8, psum)
        with nc.Block() as block:
            @block.sync
            def _(sp):
                sp.dma_start(w_sc[:, :, :], d["w_sc"]).then_inc(w_in, 16)
                used = Tally(xn_ready)

                def body(i):
                    for b in range(2):
                        g = i * 2 + b
                        wait(sp, used, 1)
                        used.add()
                        sp.dma_start(rows[b][:, :, :], rows_of(d["X"], g * GR, G)).then_inc(rows_in[b], 16)

                rounds(sp, NG // 2, body, used)

            @block.gpsimd
            def _(pool):
                summed = Tally(on_act.full, 2)

                def body(i):
                    for b in range(2):
                        g = i * 2 + b
                        wait(pool, summed, 1 - b)
                        hold(pool, passed[2])
                        pool.dma_start(dd[b][:, :, :], rows_of(d["D"], g * GR, G)).then_inc(dd_in[b], 16)
                    summed.add(4)

                rounds(pool, NG // 2, body, summed)

            @block.vector
            def _(dve):
                chain, deviation, loaded = Tally(own), Tally(sd_ready), [Tally(rows_in[b], 16) for b in range(2)]
                kept, turned = Tally(on_act.empty), Tally(on_act.full)

                def body(i):
                    for b in range(2):
                        wait(dve, loaded[b].add())
                        ln_stats(dve, chain, passed[0], rows[b], st[:, b], mv[:, b], G, stats_ready)
                    for b in range(2):
                        wait(dve, turned, 6 - 2 * b)
                        hold(dve, passed[0])
                        ln_apply_planar(dve, chain, deviation, rows[b], mv[:, b], sd[:, b], xn[b], G, xn_ready)
                    turned.add(8)
                    if isinstance(i, int):
                        kept.skip(8)
                    else:
                        o_stats(i - 2)

                def o_stats(i):
                    for b in range(2):
                        g = i * 2 + b
                        wait(dve, kept.add(6 if b == 0 else 2))
                        hold(dve, passed[0])
                        for k in range(2):
                            dve.bn_stats(s.ost[:, k, bass.ds(g, 1), :].rearrange("p a n -> p (a n)"), s.o[:, k, bass.ds(g * GR, GR)])

                rounds(dve, NG // 2, body, chain, deviation, kept, turned, *loaded, lead=2)
                for k in (2, 1):
                    o_stats(NG // 2 - k)

            @block.scalar
            def _(act):
                stats, read = Tally(stats_ready), on_act.reader()

                def body(i):
                    for b in range(2):
                        ln_deviation(act, stats, mv[:, b], sd[:, b], s.eps, sd_ready)
                    if isinstance(i, int):
                        read.skip(8)
                    else:
                        empty(i - 1)

                def empty(i):
                    for b in range(2):
                        for k in range(2):
                            bank = on_act.get(act, read)
                            act.activation(xt[b][:, k, :], bank[:, :], ACT.Copy).then_inc(on_act.empty, 1)
                    for b in range(2):
                        for k in range(2):
                            bank = on_act.get(act, read)
                            hold(act, passed[1])
                            act.activation(s.o[:, k, bass.ds((i * 2 + b) * GR, GR)], bank[:, :], ACT.Copy).then_inc(on_act.empty, 1)

                rounds(act, NG // 2, body, stats, read)
                empty(NG // 2 - 1)

            @block.tensor
            def _(pe):
                pe.wait_ge(w_in, 16)
                ta, xn_in, dd_here = on_act.writer(), Tally(xn_ready), [Tally(dd_in[b], 16) for b in range(2)]

                def body(i):
                    for b in range(2):
                        wait(pe, xn_in.add())
                        for k in range(2):
                            bank = on_act.take(pe, ta)
                            for j in range(G):
                                last = pe.transpose(bank[:, j * P:(j + 1) * P], xn[b][:, j, k * P:(k + 1) * P], s.ident[:, :])
                            on_act.filled(last, ta)
                    for b in range(2):
                        wait(pe, dd_here[b].add())
                        pe.wait_ge(on_act.empty, ta.now(2))
                        for k in range(2):
                            bank = on_act.take(pe, ta, True)
                            pe.matmul(bank[:, :], w_sc[:, k, :], xt[b][:, k, :], start=True, stop=False)
                            for j in range(G):
                                last = pe.matmul(bank[:, j * P:(j + 1) * P], dd[b][:, j, k * P:(k + 1) * P], s.ident[:, :], start=False, stop=(j == G - 1))
                            on_act.filled(last, ta)

                rounds(pe, NG // 2, body, ta, xn_in, *dd_here)


def stage_norm_factors(nc, d, s, psum):
    with Stage(nc, "nf") as m:
        mv, sq, gam, beta, sel = m.sb("mv", [P, 2, 2]), m.sb("sq", [P, 2]), m.sb("gam", [P, 2]), m.sb("beta", [P, 1]), m.sb("sel", [P, 2, P])
        val = m.sb("val", [P, 2])
        c_in, own, sq_ready, nrm, val_ready, sd = (m.sem(n) for n in ("c_in", "own", "sq_ready", "nrm", "val_ready", "sd"))
        with nc.Block() as block:
            @block.sync
            def _(sp):
                for t, name in ((gam[:, :], "gamma"), (beta[:, :], "beta"), (sel[:, :, :], "same_channel")):
                    sp.dma_start(t, d[name]).then_inc(c_in, 16)

            @block.vector
            def _(dve):
                chain = Tally(own)

                def then(ins):
                    ins.then_inc(own, 1)
                    wait(dve, chain.add())

                dve.wait_ge(c_in, 48)
                g, n = N // GR, N % GR
                for k in range(2):
                    last = dve.bn_stats(s.ost[:, k, g, :], s.o[:, k, g * GR:g * GR + n])
                then(last)
                for k in range(2):
                    last = dve.bn_aggr(mv[:, k, :], s.ost[:, k, :, :].rearrange("p g n -> p (g n)"))
                then(last)
                then(dve.tensor_tensor(sq[:, :], mv[:, :, 0], mv[:, :, 0], ALU.mult))
                dve.tensor_tensor(sq[:, :], sq[:, :], mv[:, :, 1], ALU.add).then_inc(sq_ready, 1)
                dve.wait_ge(nrm, 1)
                then(dve.tensor_scalar(val[:, 0:1], psum[0][:, 0:1], 1.0 / 3.0, None, ALU.mult))
                then(dve.tensor_scalar(val[:, 1:2], psum[0][:, 0:1], 1.0 / 3.0, None, ALU.mult))
                dve.tensor_copy(val[0:H1, 0:1], mv[0:H1, 0, 1:2]).then_inc(val_ready, 1)
                dve.wait_ge(sd, 1)
                then(dve.reciprocal(val[:, :], val[:, :]))
                then(dve.tensor_tensor(s.factor[:, :], val[:, :], gam[:, :], ALU.mult))
                then(dve.memset(s.shift[:, :], 0.0))
                then(dve.tensor_tensor(sq[0:H1, 0:1], mv[0:H1, 0, 0:1], s.factor[0:H1, 0:1], ALU.mult))
                then(dve.tensor_tensor(s.shift[0:H1, 0:1], beta[0:H1, :], sq[0:H1, 0:1], ALU.subtract))

            @block.scalar
            def _(act):
                act.wait_ge(val_ready, 1)
                act.activation(val[:, :], val[:, :], ACT.Sqrt, bias=s.eps[:, 0:1]).then_inc(sd, 1)

            @block.tensor
            def _(pe):
                pe.wait_ge(c_in, 48)
                pe.wait_ge(sq_ready, 1)
                pe.matmul(psum[0][:, 0:1], sel[:, 0, :], sq[:, 0:1], start=True, stop=False)
                pe.matmul(psum[0][:, 0:1], sel[:, 1, :], sq[:, 1:2], start=False, stop=True).then_inc(nrm, 1)


def stage_node_update(nc, d, s, psum):
    with Stage(nc, "nu") as m:
        rows = [m.sb(f"rows{b}", [P, G, C]) for b in range(2)]
        xn = [m.sb(f"xn{b}", [P, G, C]) for b in range(2)]
        base = [m.sb("base0", [P, G, C])] * 2
        nt = [m.sb(f"nt{b}", [P, 2, GR]) for b in range(2)]
        wr = m.sb("wr", [P, C])
        junk = m.sb("junk", [P, G, C])
        wt = m.sb("wt", [P, 2, G])
        st, mv, sd = m.sb("st", [P, 2, G, 6]), m.sb("mv", [P, 2, G, 2]), m.sb("sd", [P, 2, G])
        w_in, rows_in, stored = m.sem("w_in"), m.sems("rows_in"), m.sems("stored")
        base_out = m.sem("base_out")
        own, stats_ready, sd_ready, xn_ready, base_ready, nt_ready = (m.sem(n) for n in ("own", "stats_ready", "sd_ready", "xn_ready", "base_ready", "nt_ready"))
        passed = m.sems("passed", 3)
        on_dve = m.banks("on_dve", 0, 4, psum)
        with nc.Block() as block:
            @block.sync
            def _(sp):
                sp.dma_start(wr[:, :], d["wr"]).then_inc(w_in, 16)
                xr, br = Tally(xn_ready), Tally(base_ready)

                def load(g, b):
                    sp.dma_start(rows[b][:, :, :], rows_of(d["X"], g * GR, G)).then_inc(rows_in[b], 16)

                for b in range(2):
                    load(b, b)

                def body(i):
                    for b in range(2):
                        wait(sp, xr.add())
                        sp.dma_start(rows_of(d["XN"], (i * 2 + b) * GR, G), xn[b][:, :, :]).then_inc(stored[b], 16)
                        wait(sp, br.add())
                        sp.dma_start(rows_of(d["out"], (i * 2 + b) * GR, G), base[b][:, :, :]).then_inc(base_out, 16)
                        load((i * 2 + b + 2), b)

                rounds(sp, NG // 2 - 1, body, xr, br)
                for b in range(2):
                    g = NG - 2 + b
                    wait(sp, xr.add())
                    sp.dma_start(rows_of(d["XN"], g * GR, G), xn[b][:, :, :]).then_inc(stored[b], 16)
                    wait(sp, br.add())
                    sp.dma_start(rows_of(d["out"], g * GR, G), base[b][:, :, :]).then_inc(base_out, 16)
                for b in range(2):
                    sp.wait_ge(stored[b], 16 * NG // 2)
                sp.wait_ge(base_out, 16 * NG)

            @block.scalar
            def _(act):
                stats, used = Tally(stats_ready), Tally(on_dve.full, 2)

                def body(i):
                    for b in range(2):
                        wait(act, used, 1)
                        used.add()
                        hold(act, passed[0])
                        for k in range(2):
                            last = act.activation(nt[b][:, k, :], s.o[:, k, bass.ds((i * 2 + b) * GR, GR)], ACT.Identity,
                                                  bias=s.shift[:, k:k + 1], scale=s.factor[:, k:k + 1])
                        last.then_inc(nt_ready, 1)
                    for b in range(2):
                        ln_deviation(act, stats, mv[:, b], sd[:, b], s.eps, sd_ready)

                rounds(act, NG // 2, body, stats, used)

            @block.tensor
            def _(pe):
                td, made = on_dve.writer(), Tally(nt_ready)

                def body(i):
                    for b in range(2):
                        wait(pe, made.add())
                        for j in range(G):
                            if j % 2 == 0:
                                bank = on_dve.take(pe, td)
                            for k in range(2):
                                o = j % 2 * C + k * P
                                last = pe.transpose(bank[:, o:o + P], nt[b][:, k, j * P:(j + 1) * P], s.ident[:, :])
                            if j % 2:
                                on_dve.filled(last, td)

                rounds(pe, NG // 2, body, td, made)

            @block.vector
            def _(dve):
                dve.wait_ge(w_in, 16)
                chain, deviation, read = Tally(own), Tally(sd_ready), on_dve.reader()
                loaded, old = [Tally(rows_in[b], 16) for b in range(2)], [Tally(stored[b], 16) for b in range(2)]
                base_gone, base_made = Tally(base_out, 16), Tally(base_ready)

                def body(i):
                    for b in range(2):
                        wait(dve, loaded[b].add())
                        for k in range(2):
                            bank = on_dve.get(dve, read)
                            n = bank[:, :].rearrange("p (j c) -> p j c", j=2)
                            for j in range(2):
                                r = rows[b][:, 2 * k + j, :]
                                dve.tensor_tensor(r[:, 0:H1], r[:, 0:H1], n[:, j, 0:H1], ALU.add)
                                last = dve.tensor_tensor(planar(r), planar(r), n[:, j, H1:C].rearrange("p (x c) -> p x c", x=3), ALU.add)
                            last.then_inc(on_dve.empty, 1)
                        dve.wait_ge(on_dve.empty, read.now())
                        ln_stats(dve, chain, passed[1], rows[b], st[:, b], mv[:, b], G, stats_ready)
                    for b in range(2):
                        wait(dve, old[b])
                        old[b].add()
                        hold(dve, passed[1])
                        ln_apply(dve, chain, deviation, rows[b], mv[:, b], sd[:, b], xn[b], G, xn_ready)
                        wait(dve, xr.add())
                        for j in range(G):
                            last = dve.scalar_tensor_tensor(junk[:, j, :], xn[b][:, j, :], 1.0, wr[:, :], ALU.mult, ALU.mult, accum_out=wt[:, b, j:j + 1])
                        then(last)
                        dve.tensor_copy(s.weight[:, bass.ds((i * 2 + b) * G, G)], wt[:, b, :]).then_inc(own, 1)
                        wait(dve, chain.add())
                        wait(dve, base_gone)
                        base_gone.add()
                        dve.tensor_tensor(base[b][:, :, :], rows[b][:, :, :], xn[b][:, :, :], ALU.add).then_inc(base_ready, 1)

                def then(ins):
                    ins.then_inc(own, 1)
                    wait(dve, chain.add())

                xr = Tally(xn_ready)
                rounds(dve, NG // 2, body, chain, deviation, read, xr, base_gone, *loaded, *old)


def stage_select(nc, d, s, psum):
    with Stage(nc, "se") as m:
        w, v, junk, gt, eq, tot, incl, pos = (m.sb(n, [P, NT]) for n in ("w", "v", "junk", "gt", "eq", "tot", "incl", "pos"))
        h16 = m.sb("h16", [P, NT], BF16)
        real, ones_row, tri32 = m.sb("real", [P, NT]), m.sb("ones_row", [P, NT]), m.sb("tri32", [P, P])
        tri, ones = m.sb("tri", [P, P], BF16), m.sb("ones", [P, P], BF16)
        ones32 = m.sb("ones32", [P, P])
        bits = m.sb("bits", [P, 31], I32)
        best, cand, ok = m.sb("best", [P, 1], I32), m.sb("cand", [P, 1], I32), m.sb("ok", [P, 1], I32)
        br, cnt, neg, sign, want, thr, room = (m.sb(n, [P, 1]) for n in ("br", "cnt", "neg", "sign", "want", "thr", "room"))
        absent = m.sb("absent", [P, NT])
        c_in, own, cnt_ready, total_ready, h_ready, counted, passed = (m.sem(n) for n in ("c_in", "own", "cnt_ready", "total_ready", "h_ready", "counted", "passed"))
        BITS = 31
        with nc.Block() as block:
            @block.sync
            def _(sp):
                for t, name in ((real[:, :], "real"), (tri32[:, :], "tri"), (bits[:, :], "bits"), (br[:, :], "br")):
                    sp.dma_start(t, d[name]).then_inc(c_in, 16)
                sp.dma_start(s.entry[:, :, 0], d["node_id"], allow_slow_non_contiguous=True).then_inc(c_in, 16)

            @block.vector
            def _(dve):
                chain, totals, counts = Tally(own), Tally(total_ready), Tally(cnt_ready)

                def then(ins):
                    ins.then_inc(own, 1)
                    wait(dve, chain.add())

                dve.memset(ones[:, :], 1.0)
                dve.memset(ones32[:, :], 1.0)
                dve.memset(ones_row[:, :], 1.0)
                then(dve.memset(best[:, :], 0))
                dve.wait_ge(c_in, 80)
                dve.tensor_copy(tri[:, :], tri32[:, :])
                then(dve.tensor_scalar(w[:, :], s.weight[:, :], br[:, 0:1], None, ALU.add))
                then(dve.tensor_copy(s.entry[:, :, 1].bitcast(F32), w[:, :]))
                then(dve.tensor_scalar(junk[:, :], w[:, :], 0.0, None, ALU.is_ge))
                then(dve.tensor_tensor(junk[:, :], junk[:, :], real[:, :], ALU.mult))
                dve.tensor_reduce(cnt[:, :], junk[:, :], AX.X, ALU.add).then_inc(cnt_ready, 1)
                wait(dve, totals.add())
                then(dve.tensor_scalar(neg[:, :], psum[0][:, 0:1], float(KEEP), None, ALU.is_lt))
                then(dve.tensor_scalar(sign[:, :], neg[:, :], -2.0, 1.0, ALU.mult, ALU.add))
                then(dve.tensor_scalar(want[:, :], neg[:, :], float(N - KEEP + 1 - KEEP), float(KEEP), ALU.mult, ALU.add))
                then(dve.tensor_scalar(absent[:, :], real[:, :], -1.0, FAR, ALU.add, ALU.mult))
                then(dve.tensor_scalar(v[:, :], w[:, :], sign[:, 0:1], None, ALU.mult))
                then(dve.tensor_tensor(v[:, :], v[:, :], real[:, :], ALU.mult))
                then(dve.tensor_tensor(v[:, :], v[:, :], absent[:, :], ALU.add))

                def body(i):
                    then(dve.tensor_tensor(cand[:, :], best[:, :], bits[:, bass.ds(i, 1)], ALU.bitwise_or))
                    dve.tensor_scalar(junk[:, :], v[:, :], cand[:, 0:1].bitcast(F32), None, ALU.is_ge, ALU.add, accum_out=cnt[:, :]).then_inc(cnt_ready, 1)
                    wait(dve, totals.add())
                    dve.tensor_scalar(ok[:, :], psum[0][:, 0:1], want[:, 0:1], None, ALU.is_ge).then_inc(own, 1)
                    wait(dve, chain.add())
                    hold(dve, passed)
                    then(dve.copy_predicated(best[:, :], ok[:, :], cand[:, :]))

                rounds(dve, BITS, body, chain, totals)
                then(dve.tensor_scalar(thr[:, :], best[:, :].bitcast(F32), sign[:, 0:1], None, ALU.mult))
                then(dve.tensor_scalar(gt[:, :], w[:, :], thr[:, 0:1], None, ALU.is_gt))
                then(dve.tensor_tensor(gt[:, :], gt[:, :], real[:, :], ALU.mult))
                dve.tensor_reduce(cnt[:, :], gt[:, :], AX.X, ALU.add).then_inc(cnt_ready, 1)
                then(dve.tensor_scalar(eq[:, :], w[:, :], thr[:, 0:1], None, ALU.is_equal))
                then(dve.tensor_tensor(eq[:, :], eq[:, :], real[:, :], ALU.mult))
                wait(dve, totals.add())
                then(dve.tensor_scalar(room[:, :], psum[0][:, 0:1], -1.0, float(KEEP), ALU.mult, ALU.add))

                def order(hot, n):
                    dve.tensor_copy(h16[:, :], hot[:, :]).then_inc(h_ready, 1)
                    dve.wait_ge(counted, n)
                    dve.tensor_copy(incl[:, :], psum[1][:, 0:NT])
                    then(dve.tensor_copy(tot[:, :], psum[2][:, 0:NT]))
                    then(dve.tensor_tensor_scan(pos[:, :], ones_row[:, :], tot[:, :], 0.0, ALU.mult, ALU.add))
                    then(dve.tensor_tensor(pos[:, :], pos[:, :], tot[:, :], ALU.subtract))
                    then(dve.tensor_tensor(pos[:, :], pos[:, :], incl[:, :], ALU.add))

                order(eq, 1)
                then(dve.tensor_scalar(pos[:, :], pos[:, :], room[:, 0:1], None, ALU.is_le))
                then(dve.tensor_tensor(eq[:, :], eq[:, :], pos[:, :], ALU.mult))
                then(dve.tensor_tensor(gt[:, :], gt[:, :], eq[:, :], ALU.add))
                order(gt, 2)
                then(dve.tensor_scalar(pos[:, :], pos[:, :], -1.0 - SKIP, None, ALU.add))
                then(dve.tensor_tensor(pos[:, :], pos[:, :], gt[:, :], ALU.mult))
                then(dve.tensor_scalar(s.slot[:, :], pos[:, :], float(SKIP), None, ALU.add))

            @block.tensor
            def _(pe):
                counts = Tally(cnt_ready)

                def total(i):
                    wait(pe, counts.add())
                    pe.matmul(psum[0][:, 0:1], ones32[:, :], cnt[:, :], start=True, stop=True).then_inc(total_ready, 1)

                total(0)
                rounds(pe, BITS, total, counts)
                total(0)
                for n in range(2):
                    pe.wait_ge(h_ready, n + 1)
                    pe.matmul(psum[1][:, 0:NT], tri[:, :], h16[:, :], start=True, stop=True)
                    pe.matmul(psum[2][:, 0:NT], ones[:, :], h16[:, :], start=True, stop=True).then_inc(counted, 1)


def stages(nc, d, s, psum):
    with nc.sbuf_tensor("scores", [HEADS, EP], F32) as s.scores:
        stage_edge_scores(nc, d, s, psum)
        stage_edge_softmax(nc, d, s, psum)
        stage_edge_sum(nc, d, s, psum)
    with nc.sbuf_tensor("slot", [P, NT], I32) as s.slot, nc.sbuf_tensor("entry", [P, NT, 2], I32) as s.entry:
        with nc.sbuf_tensor("logits", [P, NT, EXPERTS], F32) as s.logits:
            stage_router_logits(nc, d, s, psum)
            stage_router(nc, d, s, psum)
        stage_table(nc, d, s, psum, True)
    stage_ffn(nc, d, s, psum, True)
    stage_messages(nc, d, s, psum)
    with ExitStack() as kept:
        sb = lambda name, shape, dt=F32: kept.enter_context(nc.sbuf_tensor(name, shape, dt))
        s.weight, s.slot, s.entry = sb("weight", [P, NT]), sb("slot2", [P, NT], I32), sb("entry2", [P, NT, 2], I32)
        with nc.sbuf_tensor("o", [P, 2, NP], F32) as s.o, nc.sbuf_tensor("ost", [P, 2, NG, 6], F32) as s.ost, \
                nc.sbuf_tensor("factor", [P, 2], F32) as s.factor, nc.sbuf_tensor("shift", [P, 2], F32) as s.shift:
            stage_node_sums(nc, d, s, psum)
            stage_norm_factors(nc, d, s, psum)
            stage_node_update(nc, d, s, psum)
        stage_select(nc, d, s, psum)
        stage_table(nc, d, s, psum, False)
    d["base"] = d["out"]
    stage_ffn(nc, d, s, psum, False)


def _layout_rest(np, v, a, f, pad, col, halves):
    spread = lambda z: np.broadcast_to(f(z).reshape(1, -1), (P, z.size))
    a["gate_w"] = halves(v["L0_ffn_gate_w"])
    a["gate_b"] = spread(v["L0_ffn_gate_b"])
    a["expert_rank"] = np.broadcast_to(np.arange(EXPERTS, 0, -1, dtype=np.float32), (P, EXPERTS))
    a["slot_base"] = np.broadcast_to(np.arange(EXPERTS, dtype=np.float32) * SLOTS - 1, (P, EXPERTS))
    a["node_id"] = np.arange(NP, dtype=np.int32).reshape(NT, P).T
    a["real"] = (a["node_id"] < N).astype(np.float32)
    a["tri"] = np.triu(np.ones((P, P), np.float32))
    k = HID // P
    a["moe_w1"] = f(v["L0_ffn_w1"]).reshape(EXPERTS, 2, P, HID).transpose(0, 2, 1, 3).reshape(EXPERTS, P, -1)
    a["moe_w2"] = f(v["L0_ffn_w2"]).reshape(EXPERTS, k, P, C).transpose(0, 2, 1, 3).reshape(EXPERTS, P, -1)
    a["moe_b1"] = f(v["L0_ffn_b1"]).reshape(EXPERTS, k, P).transpose(0, 2, 1)
    a["moe_b2"] = np.broadcast_to(f(v["L0_ffn_b2"])[:, None], (EXPERTS, P, C))
    def blocks(w0, w1):
        z = np.zeros((P, 2, P), np.float32)
        w0, w1 = f(w0), f(w1)
        z[:H1, 0, :H1], z[H1:, 0, H1:], z[:H1, 1, :H1], z[H1:, 1, H1:] = w0, w1, w1, w1
        return z
    for name, w in (("w_up", "W_up"), ("w_lin", "W_lin"), ("w_sc", "Wsc"), ("w_b", "WB")):
        a[name] = blocks(v[f"L1_gnn_{w}0"], v[f"L1_gnn_{w}1"])
    for n in ("M1", "M2", "M3", "M4"):
        a[n] = f(v[f"L1_gnn_{n}"])
    a["wc"] = np.broadcast_to(np.concatenate([f(v["L1_gnn_Wc0"]).T, f(v["L1_gnn_Wc1"]).T])[None], (P, 9, H1))
    a["rbf"] = pad(f(v["edge_attr_16"]), EP).T
    a["sh"] = pad(f(v["edge_attr_4"]), EP)
    g0, g1 = f(v["L1_gnn_gamma0"]), f(v["L1_gnn_gamma1"])
    a["gamma"] = np.stack([np.concatenate([g0, g1]), np.concatenate([g1, g1])], 1)
    a["beta"] = np.concatenate([f(v["L1_gnn_beta0"]), np.zeros(H1, np.float32)])[:, None]
    p, q = np.arange(P)[:, None], np.arange(P)[None]
    same = (p % H1 == q % H1)
    a["same_channel"] = np.stack([same & (p >= H1), same], 1).astype(np.float32)
    a["wr"] = spread(v["L1_ffn_wr"])
    a["bits"] = np.broadcast_to((1 << np.arange(30, -1, -1)).astype(np.int32), (P, 31))
    a["br"] = np.broadcast_to(f(v["L1_ffn_br"]).reshape(1, 1), (P, 1))
    a["mod_w1"] = halves(v["L1_ffn_w1"]).reshape(P, -1)
    a["mod_w2"] = f(v["L1_ffn_w2"]).reshape(k, P, C).transpose(1, 0, 2).reshape(P, -1)
    a["mod_b1"] = f(v["L1_ffn_b1"]).reshape(k, P).T
    a["mod_b2"] = spread(v["L1_ffn_b2"])


class Kept:
    pass


def build(nc, d):
    s = Kept()
    with ExitStack() as ctx:
        def sb(name, shape, dt=F32):
            return ctx.enter_context(nc.sbuf_tensor(name, shape, dt))

        psum = [ctx.enter_context(nc.psum_tensor(f"bank{k}", [P, 512], F32)) for k in range(8)]
        s.ident = sb("ident", [P, P])
        s.eps = sb("eps", [P, 1])
        s.last_row = sb("last_row", [P, 1])
        s.dst_col = sb("dst_col", [P, 1 + ET])
        s.dst_row_id = sb("dst_row_id", [P, ET], I32)
        s.end_row = sb("end_row", [P, ET], I32)
        set_up = ctx.enter_context(nc.semaphore("set_up"))
        with nc.Block() as block:
            @block.sync
            def _(sp):
                sp.dma_start(s.last_row[:, :], d["last_row"]).then_inc(set_up, 16)
                sp.wait_ge(set_up, 16)

            @block.vector
            def _(dve):
                dve.memset(s.eps[:, :], EPS)
        stages(nc, d, s, psum)


def _layout(np, v):
    f = lambda a: np.ascontiguousarray(np.asarray(a))
    pad = lambda a, n, c=0: np.concatenate([f(a), np.full((n - len(a),) + a.shape[1:], c, a.dtype)])
    a = {}
    a["x"] = pad(f(v["x"]), NP)
    src = pad(f(v["src"]).astype(np.int32), EP, NP - 1)
    dst = pad(f(v["dst"]).astype(np.int32), EP, NP - 1)
    col = lambda z: z.reshape(-1, P).T
    both = np.stack([src.reshape(EG, G, P), dst.reshape(EG, G, P)], 1)
    a["edge_idx"] = both.reshape(EG, 2 * G, P).transpose(2, 0, 1)
    a["src_col"] = col(src)
    a["dst_col"] = np.concatenate([np.full((P, 1), -1, np.int32), col(dst)], 1)
    a["dst_next"] = col(np.concatenate([dst[1:], np.full(1, -1, np.int32)]))
    a["dst_row"] = dst[None]
    a["ident"] = np.eye(P, dtype=np.float32)
    a["last_row"] = (np.arange(P) == P - 1).astype(np.float32)[:, None]
    halves = lambda w: f(w).reshape(2, P, -1).transpose(1, 0, 2)
    a["gat_w"] = halves(f(v["L0_gnn_W"]).transpose(1, 0, 2).reshape(C, C))
    a["gat_a"] = np.broadcast_to(np.stack([f(v["L0_gnn_a_src"]).reshape(C), f(v["L0_gnn_a_dst"]).reshape(C)])[None], (P, 2, C))
    _layout_rest(np, v, a, f, pad, col, halves)
    return {k: np.ascontiguousarray(z) for k, z in a.items()}


SCRATCH = {"X": (NP, C), "XN": (NP, C), "H": (EP, C), "D": (NP, C), "R": (H1, EP)}
TABLES = {"moe_table": (EXPERTS * SLOTS, 2), "mod_table": (SB * FB, 2)}


def kernel(**inputs):
    import numpy as np
    import concourse.bacc as bacc
    from concourse import mybir as mb
    from concourse.bass_utils import run_bass_kernel_spmd

    nc = bacc.Bacc("TRN2", target_bir_lowering=False, num_devices=1)
    arrays = _layout(np, inputs)
    d = {k: nc.dram_tensor(f"in_{k}", z.shape, mb.dt.from_np(z.dtype), kind="ExternalInput").ap()
         for k, z in arrays.items()}
    for k, shape in SCRATCH.items():
        d[k] = nc.dram_tensor(f"scratch_{k}", shape, F32, kind="Internal").ap()
    for k, shape in TABLES.items():
        d[k] = nc.dram_tensor(f"scratch_{k}", shape, I32, kind="Internal").ap()
    d["out"] = nc.dram_tensor("out", (NP, C), F32, kind="ExternalOutput").ap()
    d["dst_rows"] = d["dst_row"].to_broadcast([P, EP])
    build(nc, d)
    r = run_bass_kernel_spmd(nc, [{f"in_{k}": z for k, z in arrays.items()}], core_ids=[0])
    return r.results[0]["out"][:N]
```
